# Optimizing a Trainium2 kernel written in Bass

```python
import numpy as np
import jax
import jax.numpy as jnp

def _softmax(x, axis=-1):
    return jax.nn.softmax(x, axis=axis)

def _gelu(x):
    return jax.nn.gelu(x, approximate=True)

def _silu(x):
    return jax.nn.silu(x)

def _sigmoid(x):
    return jax.nn.sigmoid(x)

def _layernorm(x, axis=-1, eps=1e-05):
    m = jnp.mean(x, axis=axis, keepdims=True)
    v = jnp.var(x, axis=axis, keepdims=True)
    return (x - m) / jnp.sqrt(v + eps)

def _scatter_add(tgt, idx, src, axis=0):
    return tgt.at[idx].add(src)

def _segment_sum(src, seg, n):
    return jax.ops.segment_sum(src, seg, n)
kernel_name = 'mk_decoder_preln_d2_seqx_r8_91b9d9'

def setup_inputs(seed: int=0):
    np.random.seed(seed)
    _w = jnp.asarray

    def _rec_inputs():
        import jax
        import jax.numpy as jnp
        _rk = jax.random.key(seed)
        x = -0.000125 + 0.9999 * jax.random.normal(jax.random.fold_in(_rk, 1), (8, 256, 128), jnp.float32)
        _lenS = 256 - jax.random.randint(jax.random.fold_in(_rk, 7), (8,), 0, max(1, 256 // 4) + 1, jnp.int32)
        _lenS2 = 512 - jax.random.randint(jax.random.fold_in(_rk, 8), (8,), 0, max(1, 512 // 4) + 1, jnp.int32)
        _ctx_1024P = jax.random.normal(jax.random.fold_in(_rk, 11), (8, 16, 128), jnp.float32)
        _ctx_1024c = jax.random.dirichlet(jax.random.fold_in(_rk, 511), 0.3 * jnp.ones((16,), jnp.float32), (8, 512))
        _ctx_1024t = jnp.einsum('bsk,bkd->bsd', _ctx_1024c, _ctx_1024P)
        _ctx_1024t = _ctx_1024t * jax.lax.rsqrt(jnp.mean(jnp.square(_ctx_1024t)) + 1e-12) * 0.953939
        ctx_1024 = 4.13588e-05 + 0.999923 * (_ctx_1024t + 0.3 * jax.random.normal(jax.random.fold_in(_rk, 611), (8, 512, 128), jnp.float32))
        return (x, ctx_1024)
    x, ctx_1024 = _rec_inputs()

    def _L0_attn_setup():
        import jax, jax.numpy as jnp
        import numpy as np
        B, S, D_IN = (2, 256, 128)
        H, D_HEAD = (16, 64)
        key = jax.random.key(seed)
        k1, k2, k3 = jax.random.split(key, 3)
        x = jax.random.normal(k1, (B, S, D_IN), dtype=jnp.float32)
        kernel = jax.random.normal(k2, (3, H, D_IN, D_HEAD), dtype=jnp.float32) * np.float32(np.sqrt(2.0 / D_IN))
        WO = jax.random.normal(k3, (1, H * D_HEAD, D_IN), dtype=jnp.float32) * np.float32(np.sqrt(2.0 / (H * D_HEAD)))
        return {'x': x, 'kernel': kernel, 'WO': WO}
    _L0_attn_all = _L0_attn_setup()
    _L0_attn_in = {k: v for k, v in _L0_attn_all.items() if k in ('kernel', 'WO')}
    del _L0_attn_all

    def _L0_xattn_setup():
        import jax, jax.numpy as jnp
        import numpy as np
        key = jax.random.key(seed)
        k1, k2 = jax.random.split(key)
        hidden_states = jax.random.normal(k1, (8, 512, 128), dtype=jnp.float32)
        visual_hidden_state = jax.random.normal(k2, (8, 128, 128), dtype=jnp.float32)
        return {'hidden_states': hidden_states, 'visual_hidden_state': visual_hidden_state}
    _L0_xattn_all = _L0_xattn_setup()
    _L0_xattn_in = {k: v for k, v in _L0_xattn_all.items() if k in ()}
    del _L0_xattn_all

    def _L0_ffn_setup():
        import jax, jax.numpy as jnp
        import numpy as np
        CHUNK = 128
        NUM_BITS = 6
        key = jax.random.key(seed)
        k1, k2, k3 = jax.random.split(key, 3)
        B, L, D, E = (4, 512, 128, 64)
        x = jax.random.normal(k1, (B, L, D), dtype=jnp.float32)
        expert_weights = jax.random.normal(k2, (E, D, D), dtype=jnp.float32) * 0.02
        hyperplanes = jax.random.normal(k3, (D, NUM_BITS), dtype=jnp.float32)
        return {'x': x, 'expert_weights': expert_weights, 'hyperplanes': hyperplanes}
    _L0_ffn_all = _L0_ffn_setup()
    _L0_ffn_in = {k: v for k, v in _L0_ffn_all.items() if k in ('expert_weights', 'hyperplanes')}
    del _L0_ffn_all

    def _L1_attn_setup():
        import jax, jax.numpy as jnp
        import numpy as np
        B, S, D_IN, D_H = (8, 512, 128, 128)

        def _uniform(k, shape, bound):
            return jax.random.uniform(k, shape, jnp.float32, -bound, bound)

        def log_g(v):
            return jnp.where(v >= 0, jnp.log(jnp.where(v >= 0, v + 0.5, 1.0)), -jax.nn.softplus(-v))
        key = jax.random.key(seed)
        ks = jax.random.split(key, 5)
        stdv = 1.0 / np.sqrt(D_IN)
        x = jax.random.normal(ks[0], (B, S, D_IN), jnp.float32)
        Wz = _uniform(ks[1], (D_H, D_IN), stdv)
        bz = _uniform(ks[2], (D_H,), stdv)
        Wh = _uniform(ks[3], (D_H, D_IN), stdv)
        bh = _uniform(ks[4], (D_H,), stdv)
        return {'x': x, 'Wz': Wz, 'bz': bz, 'Wh': Wh, 'bh': bh}
    _L1_attn_all = _L1_attn_setup()
    _L1_attn_in = {k: v for k, v in _L1_attn_all.items() if k in ('Wz', 'bz', 'Wh', 'bh')}
    del _L1_attn_all

    def _L1_xattn_setup():
        import jax, jax.numpy as jnp
        import numpy as np
        D_K = 64
        N_HEADS = 16
        D_MODEL = 128
        BATCH = 4
        SEQ = 256
        key = jax.random.key(seed)
        ks = jax.random.split(key, 11)
        s = 0.02
        inp = {'q': jax.random.normal(ks[0], (BATCH, SEQ, D_MODEL), jnp.float32), 'k': jax.random.normal(ks[1], (BATCH, SEQ, D_MODEL), jnp.float32), 'v': jax.random.normal(ks[2], (BATCH, SEQ, D_MODEL), jnp.float32), 'Wq': jax.random.normal(ks[3], (D_MODEL, N_HEADS * D_K), jnp.float32) * s, 'bq': jax.random.normal(ks[4], (N_HEADS * D_K,), jnp.float32) * s, 'Wk': jax.random.normal(ks[5], (D_MODEL, N_HEADS * D_K), jnp.float32) * s, 'bk': jax.random.normal(ks[6], (N_HEADS * D_K,), jnp.float32) * s, 'Wv': jax.random.normal(ks[7], (D_MODEL, N_HEADS * D_K), jnp.float32) * s, 'bv': jax.random.normal(ks[8], (N_HEADS * D_K,), jnp.float32) * s, 'Wo': jax.random.normal(ks[9], (N_HEADS * D_K, D_MODEL), jnp.float32) * s, 'bo': jax.random.normal(ks[10], (D_MODEL,), jnp.float32) * s}
        return inp
    _L1_xattn_all = _L1_xattn_setup()
    _L1_xattn_in = {k: v for k, v in _L1_xattn_all.items() if k in ('Wq', 'bq', 'Wk', 'bk', 'Wv', 'bv', 'Wo', 'bo')}
    del _L1_xattn_all

    def _L1_ffn_setup():
        import jax, jax.numpy as jnp
        import numpy as np
        B, S, D_MODEL, D_HIDDEN = (4, 256, 128, 512)

        def act_quant(x):
            scale = 127.0 / jnp.clip(jnp.max(jnp.abs(x), axis=-1, keepdims=True), 1e-05)
            return jnp.clip(jnp.round(x * scale), -128, 127) / scale

        def weight_quant(w):
            scale = 1.0 / jnp.clip(jnp.mean(jnp.abs(w)), 1e-05)
            return jnp.clip(jnp.round(w * scale), -1, 1) / scale

        def bit_linear(x, w):
            xq = x + jax.lax.stop_gradient(act_quant(x) - x)
            wq = w + jax.lax.stop_gradient(weight_quant(w) - w)
            return jnp.einsum('bsd,hd->bsh', xq, wq)

        def depthwise_conv1d(x_bcl, w, b):
            y = jax.lax.conv_general_dilated(x_bcl, w, window_strides=(1,), padding=[(1, 1)], dimension_numbers=('NCH', 'OIH', 'NCH'), feature_group_count=x_bcl.shape[1])
            return y + b[None, :, None]
        key = jax.random.key(seed)
        ks = jax.random.split(key, 5)
        lim1 = 1.0 / np.sqrt(D_MODEL)
        lim2 = 1.0 / np.sqrt(D_HIDDEN)
        limc = 1.0 / np.sqrt(3.0)
        return {'x': jax.random.normal(ks[0], (B, S, D_MODEL), dtype=jnp.float32), 'w1': jax.random.uniform(ks[1], (D_HIDDEN, D_MODEL), jnp.float32, -lim1, lim1), 'conv_w': jax.random.uniform(ks[2], (D_HIDDEN, 1, 3), jnp.float32, -limc, limc), 'conv_b': jax.random.uniform(ks[3], (D_HIDDEN,), jnp.float32, -limc, limc), 'w2': jax.random.uniform(ks[4], (D_MODEL, D_HIDDEN), jnp.float32, -lim2, lim2)}
    _L1_ffn_all = _L1_ffn_setup()
    _L1_ffn_in = {k: v for k, v in _L1_ffn_all.items() if k in ('w1', 'conv_w', 'conv_b', 'w2')}
    del _L1_ffn_all
    return {'x': x, 'ctx_1024': ctx_1024, 'L0_attn_kernel': _L0_attn_in['kernel'], 'L0_attn_WO': _L0_attn_in['WO'], 'L0_ffn_expert_weights': _L0_ffn_in['expert_weights'], 'L0_ffn_hyperplanes': _L0_ffn_in['hyperplanes'], 'L1_attn_Wz': _L1_attn_in['Wz'], 'L1_attn_bz': _L1_attn_in['bz'], 'L1_attn_Wh': _L1_attn_in['Wh'], 'L1_attn_bh': _L1_attn_in['bh'], 'L1_xattn_Wq': _L1_xattn_in['Wq'], 'L1_xattn_bq': _L1_xattn_in['bq'], 'L1_xattn_Wk': _L1_xattn_in['Wk'], 'L1_xattn_bk': _L1_xattn_in['bk'], 'L1_xattn_Wv': _L1_xattn_in['Wv'], 'L1_xattn_bv': _L1_xattn_in['bv'], 'L1_xattn_Wo': _L1_xattn_in['Wo'], 'L1_xattn_bo': _L1_xattn_in['bo'], 'L1_ffn_w1': _L1_ffn_in['w1'], 'L1_ffn_conv_w': _L1_ffn_in['conv_w'], 'L1_ffn_conv_b': _L1_ffn_in['conv_b'], 'L1_ffn_w2': _L1_ffn_in['w2']}

def reference(x, ctx_1024, L0_attn_kernel, L0_attn_WO, L0_ffn_expert_weights, L0_ffn_hyperplanes, L1_attn_Wz, L1_attn_bz, L1_attn_Wh, L1_attn_bh, L1_xattn_Wq, L1_xattn_bq, L1_xattn_Wk, L1_xattn_bk, L1_xattn_Wv, L1_xattn_bv, L1_xattn_Wo, L1_xattn_bo, L1_ffn_w1, L1_ffn_conv_w, L1_ffn_conv_b, L1_ffn_w2):
    import jax
    import jax.numpy as jnp

    def _L0_attn_ref(x, kernel, WO):
        import jax, jax.numpy as jnp
        import numpy as np
        B, S, D_IN = (2, 256, 128)
        H, D_HEAD = (16, 64)
        b, s, _ = x.shape
        h, d = (kernel.shape[1], kernel.shape[3])
        q = jnp.einsum('bsm,hmd->bhsd', x, kernel[0])
        k = jnp.einsum('bsm,hmd->bhsd', x, kernel[1])
        v = jnp.einsum('bsm,hmd->bhsd', x, kernel[2])
        scale = jnp.float32(1.0 / (d * d * h))
        scores = jnp.einsum('bhsd,bhtd->bhst', q, k) * scale
        attn = jax.nn.softmax(scores, axis=-1)
        out = jnp.einsum('bhst,bhtd->bhsd', attn, v)
        out = jnp.transpose(out, (0, 2, 3, 1)).reshape(b, s, d * h)
        out = jnp.einsum('bsf,fm->bsm', out, WO[0])
        return out

    def _L0_xattn_ref(hidden_states, visual_hidden_state):
        import jax, jax.numpy as jnp
        import numpy as np
        fusion_scores = jnp.einsum('bsd,bvd->bsv', hidden_states, visual_hidden_state)
        fusion_probs = jax.nn.softmax(fusion_scores, axis=-1)
        fusion_output = jnp.einsum('bsv,bvd->bsd', fusion_probs, visual_hidden_state)
        return fusion_output

    def _L0_ffn_ref(x, expert_weights, hyperplanes):
        import jax, jax.numpy as jnp
        import numpy as np
        CHUNK = 128
        NUM_BITS = 6
        B, L, D = x.shape
        C = L // CHUNK
        xr = x.reshape(B, C, CHUNK, D)
        chunk_emb = xr.mean(axis=2)
        proj = chunk_emb @ hyperplanes
        bits = (proj > 0).astype(jnp.int32)
        powers = (2 ** jnp.arange(NUM_BITS)).astype(jnp.int32)
        e1 = jnp.sum(bits * powers, axis=-1)
        weakest = jnp.argmin(jnp.abs(proj), axis=-1)
        flip = (2 ** weakest).astype(jnp.int32)
        e2 = jnp.bitwise_xor(e1, flip)
        out = jnp.zeros_like(xr)
        for idx in (e1, e2):
            w = expert_weights[idx]
            out = out + jnp.einsum('bcld,bcde->bcle', xr, w)
        out = out * 0.5
        return out.reshape(B, L, D)

    def _L1_attn_ref(x, Wz, bz, Wh, bh):
        import jax, jax.numpy as jnp
        import numpy as np
        B, S, D_IN, D_H = (8, 512, 128, 128)

        def _uniform(k, shape, bound):
            return jax.random.uniform(k, shape, jnp.float32, -bound, bound)

        def log_g(v):
            return jnp.where(v >= 0, jnp.log(jnp.where(v >= 0, v + 0.5, 1.0)), -jax.nn.softplus(-v))
        k = jnp.einsum('bsd,hd->bsh', x, Wz) + bz
        log_z = -jax.nn.softplus(-k)
        log_coeffs = -jax.nn.softplus(k)
        pre = jnp.einsum('bsd,hd->bsh', x, Wh) + bh
        log_tilde_h = log_g(pre)
        log_h0 = jnp.full((x.shape[0], 1, Wh.shape[0]), jnp.log(0.5), x.dtype)
        log_b = jnp.concatenate([log_h0, log_z + log_tilde_h], axis=1)
        a_star = jnp.pad(jnp.cumsum(log_coeffs, axis=1), ((0, 0), (1, 0), (0, 0)))
        log_x = a_star + jax.lax.cumlogsumexp(log_b - a_star, axis=1)
        h = jnp.exp(log_x)
        return h[:, 1:]

    def _L1_xattn_ref(q, k, v, Wq, bq, Wk, bk, Wv, bv, Wo, bo):
        import jax, jax.numpy as jnp
        import numpy as np
        D_K = 64
        N_HEADS = 16
        D_MODEL = 128
        BATCH = 4
        SEQ = 256
        N, Tq, _ = q.shape
        Tk = k.shape[1]
        qh = (q @ Wq + bq).reshape(N, Tq, N_HEADS, D_K).transpose(0, 2, 1, 3)
        kh = (k @ Wk + bk).reshape(N, Tk, N_HEADS, D_K).transpose(0, 2, 1, 3)
        vh = (v @ Wv + bv).reshape(N, Tk, N_HEADS, D_K).transpose(0, 2, 1, 3)
        scores = jnp.einsum('nhqd,nhkd->nhqk', qh, kh) / jnp.sqrt(jnp.asarray(D_K, qh.dtype))
        causal = jnp.tril(jnp.ones((Tq, Tk), bool))
        scores = jnp.where(causal[None, None], scores, -jnp.inf)
        attn = jax.nn.softmax(scores, axis=-1)
        A = jnp.einsum('nhqk,nhkd->nhqd', attn, vh)
        A = A.transpose(0, 2, 1, 3).reshape(N, Tq, N_HEADS * D_K)
        return A @ Wo + bo

    def _L1_ffn_ref(x, w1, conv_w, conv_b, w2):
        import jax, jax.numpy as jnp
        import numpy as np
        B, S, D_MODEL, D_HIDDEN = (4, 256, 128, 512)

        def act_quant(x):
            scale = 127.0 / jnp.clip(jnp.max(jnp.abs(x), axis=-1, keepdims=True), 1e-05)
            return jnp.clip(jnp.round(x * scale), -128, 127) / scale

        def weight_quant(w):
            scale = 1.0 / jnp.clip(jnp.mean(jnp.abs(w)), 1e-05)
            return jnp.clip(jnp.round(w * scale), -1, 1) / scale

        def bit_linear(x, w):
            xq = x + jax.lax.stop_gradient(act_quant(x) - x)
            wq = w + jax.lax.stop_gradient(weight_quant(w) - w)
            return jnp.einsum('bsd,hd->bsh', xq, wq)

        def depthwise_conv1d(x_bcl, w, b):
            y = jax.lax.conv_general_dilated(x_bcl, w, window_strides=(1,), padding=[(1, 1)], dimension_numbers=('NCH', 'OIH', 'NCH'), feature_group_count=x_bcl.shape[1])
            return y + b[None, :, None]
        h = bit_linear(x, w1)
        h = depthwise_conv1d(h.transpose(0, 2, 1), conv_w, conv_b)
        h = h.transpose(0, 2, 1)
        h = jax.nn.silu(h)
        return bit_linear(h, w2)
    x = x + _L0_attn_ref(_layernorm(x, axis=-1), L0_attn_kernel, L0_attn_WO)
    x = x + _L0_xattn_ref(_layernorm(x, axis=-1), ctx_1024)
    x = x + _L0_ffn_ref(_layernorm(x, axis=-1), L0_ffn_expert_weights, L0_ffn_hyperplanes)
    x = x + _L1_attn_ref(_layernorm(x, axis=-1), L1_attn_Wz, L1_attn_bz, L1_attn_Wh, L1_attn_bh)
    x = x + _L1_xattn_ref(_layernorm(x, axis=-1), ctx_1024, ctx_1024, L1_xattn_Wq, L1_xattn_bq, L1_xattn_Wk, L1_xattn_bk, L1_xattn_Wv, L1_xattn_bv, L1_xattn_Wo, L1_xattn_bo)
    x = x + _L1_ffn_ref(_layernorm(x, axis=-1), L1_ffn_w1, L1_ffn_conv_w, L1_ffn_conv_b, L1_ffn_w2)
    return x

_drawn_inputs = setup_inputs


def setup_inputs(seed=0):
    import zlib

    import numpy as np

    out = dict(_drawn_inputs(seed))
    spreads = {}
    factors = {'L1_attn_bz': 22.162,
     'L1_attn_bh': 3.046,
     'L1_xattn_Wq': 8.0,
     'L1_xattn_bq': 64.0,
     'L1_xattn_Wk': 8.0,
     'L1_xattn_bk': 64.0,
     'L1_xattn_bv': 8.0,
     'L1_xattn_bo': 4.613}
    for name, (base, spread) in spreads.items():
        noise = np.random.default_rng([zlib.crc32(name.encode()), seed]).standard_normal(out[name].shape)
        drawn = base * np.exp(spread * noise) if base else spread * noise
        out[name] = jnp.asarray(drawn.astype(out[name].dtype))
    for name, factor in factors.items():
        out[name] = (out[name] * factor).astype(out[name].dtype)
    return out
```

```python
from contextlib import ExitStack

import concourse.bass as bass
from concourse import mybir

P = 128
B, T, D = 8, 256, 128
NT = T // P
CTX = 512
NC = CTX // P
H, DH = 16, 64
HD = H * DH
PAIRS = H // 2
E = 64
BITS = 6
HID = 512
NH = HID // P
SCALE0 = 1.0 / (DH * DH * H)
SCALE1 = 1.0 / 8.0
EPS = 1e-5
ROUND = 12582912.0
MASKED = -1e36
GUESS = float(0x5F3759DF)
SLOTS = H + 4

F32 = mybir.dt.float32
F32R = mybir.dt.float32r
BF16 = mybir.dt.bfloat16
I32 = mybir.dt.int32
ALU = mybir.AluOpType
ACT = mybir.ActivationFunctionType
AX = mybir.AxisListType

ATTN_STEPS = (16, 17)
CHAIN_STEPS = 72
FFN_STEPS = 39


def build(nc, x, ctx_d, w0, wo0, experts, planes, wz, bz, wh, bh, wq1, bq1, wk1, bk1, wv1, bv1,
          wo1, bo1, w1, conv_w, conv_b, w2, out):
    with ExitStack() as st:
        def sb(name, shape, dt=F32):
            return st.enter_context(nc.sbuf_tensor(name, shape, dt))

        def pb(name):
            return st.enter_context(nc.psum_tensor(name, [P, 512], F32))

        def sem(name):
            return st.enter_context(nc.semaphore(name))

        ident = sb("ident", [P, P])
        identb = sb("identb", [P, P], BF16)
        mask = sb("mask", [P, P], BF16)
        ones = sb("ones", [P, P])
        onesr = sb("onesr", [P, P], F32R)
        powers = sb("powers", [1, NT, BITS])
        powers_up = sb("powers_up", [1, NT, BITS])
        stage = sb("stage", [P, 3, HD])
        whi = [sb(f"whi{l}", [P, 3, HD], F32R) for l in range(2)]
        wlo = [sb(f"wlo{l}", [P, 3, HD], F32R) for l in range(2)]
        wo = [sb(f"wo{l}", [P, PAIRS, D]) for l in range(2)]
        expert = sb("expert", [P, E * D])
        plane = sb("plane", [P, BITS])
        wzh = sb("wzh", [P, 2, D])
        wzh_t = sb("wzh_t", [P, 2, D])
        bzh = sb("bzh", [P, 2])
        bzh_half = sb("bzh_half", [P, 2])
        bqkv = sb("bqkv", [P, 3, PAIRS])
        bq_scaled = sb("bq_scaled", [P, PAIRS])
        bo_all = sb("bo_all", [P, D])
        w12 = sb("w12", [P, 2, HID])
        convw = sb("convw", [P, NH, 3])
        convb_r = sb("convb_r", [P, HID], F32R)
        w1_hi = sb("w1_hi", [P, 3, HID], F32R)
        w1_lo = sb("w1_lo", [P, 3, HID], F32R)
        w2t = sb("w2t", [P, NH, D], BF16)
        wsum = sb("wsum", [P, 2])
        wmean = sb("wmean", [P, 2])
        wscale = sb("wscale", [P, 2])
        winv = sb("winv", [P, 2])
        x_in = sb("x_in", [P, NT, D])
        x_a = sb("x_a", [P, NT, D])
        x_c = sb("x_c", [P, NT, D])
        x_f = sb("x_f", [P, NT, D])
        y_out = sb("y_out", [P, NT, D])
        stats = sb("stats", [P, NT, 6])
        mv = sb("mv", [P, NT, 2])
        rstd = sb("rstd", [P, NT])
        var = sb("var", [P, NT])
        newton = sb("newton", [P, NT])
        beat = sb("beat", [P, 1])
        xn = sb("xn", [P, NT, D])
        xt_hi = sb("xt_hi", [P, T], F32R)
        xt_lo = sb("xt_lo", [P, T], F32R)
        ct_hi = sb("ct_hi", [P, T], F32R)
        ct_lo = sb("ct_lo", [P, T], F32R)
        q_hi = sb("q_hi", [P, 2, T], F32R)
        q_lo = sb("q_lo", [P, 2, T], F32R)
        k_hi = sb("k_hi", [P, 2, 2, T], F32R)
        k_lo = sb("k_lo", [P, 2, 2, T], F32R)
        v_sb = [sb(f"v_sb{l}", [P, NT, HD]) for l in range(2)]
        probs = sb("probs", [P, 4, NT, T])
        negmax = sb("negmax", [P, 4, NT])
        rsum = sb("rsum", [P, 4, NT])
        rinv = sb("rinv", [P, 4, NT])
        probs_t = sb("probs_t", [P, 4, NT, T])
        heads_t = sb("heads_t", [P, 2, T])
        ctx = sb("ctx", [P, NC, D])
        ctx_t = sb("ctx_t", [P, CTX])
        cn = sb("cn", [P, NT, D])
        cn_t = sb("cn_t", [P, T])
        cprobs = sb("cprobs", [P, CTX])
        cprobs_t = sb("cprobs_t", [P, NC, P])
        cneg = sb("cneg", [P, NT])
        csum = sb("csum", [P, NT])
        cinv = sb("cinv", [P, NT])
        emb = sb("emb", [P, NT])
        hsh = sb("hsh", [1, 6, NT, BITS])
        hsv = sb("hsv", [1, 6, NT])
        chosen = sb("chosen", [1, 2, NT])
        index = sb("index", [1, 2, NT], I32)
        tz = sb("tz", [P, T])
        th = sb("th", [P, T])
        keep = sb("keep", [P, T])
        cand = sb("cand", [P, T])
        pos_part = sb("pos_part", [P, T])
        hid = sb("hid", [P, T])
        fn = sb("fn", [P, NT, D])
        fmax = sb("fmax", [P, NT])
        fscale = sb("fscale", [P, NT])
        finv = sb("finv", [P, NT])
        f_hi = sb("f_hi", [P, T + 2], F32R)
        f_lo = sb("f_lo", [P, T + 2], F32R)
        ftanh = stage[:, 0, 0:HID]
        fy = sb("fy", [P, HID])
        convb = fy
        gmax = sb("gmax", [P, NT])
        gscale = sb("gscale", [P, NT])
        ginv = sb("ginv", [P, NT])
        fq = sb("fq", [P, NT, HID], BF16)
        fq_t = stage[:, 1, 0:HID].bitcast(BF16).rearrange("p (c q) -> p c q", q=P)
        filt = probs[:, :, :, :].rearrange("p a b c -> p (a b c)")[:, 0:3 * HID].rearrange(
            "p (j c d) -> p j c d", j=3, c=NH)
        tern2 = fq[:, 0, :]

        s_ps = [pb("s_ps0"), pb("s_ps1")]
        t_ps = [pb("t_ps0"), pb("t_ps1")]
        qk_ps = pb("qk_ps")
        o_ps = pb("o_ps")
        out_ps = pb("out_ps")
        m_ps = pb("m_ps")
        m_bf = m_ps[:, :].bitcast(BF16)

        load_x = sem("load_x")
        load_ctx = sem("load_ctx")
        load_w0 = sem("load_w0")
        load_wo0 = sem("load_wo0")
        load_w1 = sem("load_w1")
        load_wo1 = sem("load_wo1")
        load_experts = sem("load_experts")
        load_small = sem("load_small")
        consts_ready = sem("consts_ready")
        w_hi_ready = sem("w_hi_ready")
        w_lo_ready = sem("w_lo_ready")
        prep_step = sem("prep_step")
        prep_psum = sem("prep_psum")
        prep_hi = sem("prep_hi")
        prep_in = sem("prep_in")
        prep_read = sem("prep_read")
        xn_ready = sem("xn_ready")
        xt_psum = sem("xt_psum")
        xt_hi_ready = sem("xt_hi_ready")
        xt_ready = sem("xt_ready")
        v_psum = sem("v_psum")
        v_even = sem("v_even")
        v_odd = sem("v_odd")
        qk_psum = sem("qk_psum")
        qk_hi = sem("qk_hi")
        qk_ready = sem("qk_ready")
        scores_ready = sem("scores_ready")
        max_ready = sem("max_ready")
        exp_done = sem("exp_done")
        rinv_ready = sem("rinv_ready")
        probs_ready = sem("probs_ready")
        pt_psum = sem("pt_psum")
        pt_even = sem("pt_even")
        pt_odd = sem("pt_odd")
        o_psum = sem("o_psum")
        o_ready = sem("o_ready")
        out_done = sem("out_done")
        resid_done = sem("resid_done")
        attn_step = [sem("attn_step0"), sem("attn_step1")]
        chain_step = sem("chain_step")
        ffn_step = sem("ffn_step")
        chain_psum = sem("chain_psum")
        chain_act = sem("chain_act")
        chain_dve = sem("chain_dve")
        chain_in = sem("chain_in")
        ctx_split = sem("ctx_split")
        ffn_in = sem("ffn_in")
        ffn_psum = sem("ffn_psum")
        ffn_act = sem("ffn_act")
        ffn_dve = sem("ffn_dve")
        m_free = sem("m_free")
        y_ready = sem("y_ready")
        stored = sem("stored")

        def wait(eng, s, value):
            if not isinstance(value, int) or value > 0:
                eng.wait_ge(s, value)

        def f32(ap):
            return ap.bitcast(F32)

        def rows(h):
            return slice(DH * (h % 2), DH * (h % 2) + DH)

        def layer_norm_steps(dve, link, src, dst):
            for t in range(NT):
                link(dve.bn_stats(stats[:, t, :], src[:, t, :]), wait=t == NT - 1)
            dve.memset(beat[:, 0:1], 0.0)
            for t in range(NT):
                link(dve.bn_aggr(mv[:, t, :], stats[:, t, :]), wait=t == NT - 1)
            link(dve.tensor_scalar(var[:, :], mv[:, :, 1], EPS, None, ALU.add))
            link(dve.tensor_scalar(rstd[:, :].bitcast(I32), var[:, :].bitcast(I32), 1, None,
                                   ALU.logical_shift_right))
            link(dve.tensor_scalar(rstd[:, :].bitcast(I32), rstd[:, :].bitcast(I32), -1.0, GUESS,
                                   ALU.mult, ALU.add))
            for _ in range(3):
                link(dve.tensor_tensor(newton[:, :], rstd[:, :], rstd[:, :], ALU.mult))
                link(dve.scalar_tensor_tensor(out=newton[:, :], in0=newton[:, :], scalar=-0.5, in1=var[:, :],
                                              op0=ALU.mult, op1=ALU.mult))
                link(dve.scalar_tensor_tensor(out=rstd[:, :], in0=newton[:, :], scalar=1.5, in1=rstd[:, :],
                                              op0=ALU.add, op1=ALU.mult))
            for t in range(NT):
                ins = dve.tensor_scalar(dst[:, t, :], src[:, t, :], mv[:, t, 0:1], rstd[:, t:t + 1],
                                        ALU.subtract, ALU.mult)
            return ins

        class Steps:

            def __init__(self, eng, s, base):
                self.eng, self.s, self.base, self.n = eng, s, base, 0

            def __call__(self, ins, wait=True):
                self.n += 1
                ins.then_inc(self.s, 1)
                if wait:
                    self.eng.wait_ge(self.s, self.base + self.n)

            def end(self, total):
                assert self.n == total, (self.n, total)

        block = st.enter_context(nc.Block())

        @block.sync
        def _(sp):
            def load_batch_x(b):
                sp.dma_start(x_in[:, :, :], x[b, :, :].rearrange("(t p) d -> p t d", p=P))\
                    .then_inc(load_x, 16)

            def load_batch_ctx(b):
                sp.dma_start(ctx[:, :, :], ctx_d[b, :, :].rearrange("(t p) d -> p t d", p=P))\
                    .then_inc(load_ctx, 16)

            def store(b):
                sp.wait_ge(y_ready, 1 * (b + 1))
                sp.dma_start(out[b, :, :].rearrange("(t p) d -> p t d", p=P), y_out[:, :, :])\
                    .then_inc(stored, 16)

            load_batch_x(0)
            for j in range(3):
                sp.dma_start(stage[:, j, :].rearrange("p (h d) -> p h d", h=H),
                             w0[j, :, :, :].rearrange("h m d -> m h d")).then_inc(load_w0, 16)
            load_batch_ctx(0)
            sp.dma_start(wo[1][:, :, :], wo1.rearrange("(c p) m -> p c m", p=P)).then_inc(load_wo1, 16)
            sp.dma_start(expert[:, :].rearrange("p (e n) -> p e n", e=E),
                         experts.rearrange("e d n -> d e n")).then_inc(load_experts, 16)
            sp.wait_ge(w_lo_ready, 3)
            for j, w in enumerate((wq1, wk1, wv1)):
                sp.dma_start(stage[:, j, :], w).then_inc(load_w1, 16)
            sp.wait_ge(resid_done, 1)
            load_batch_x(1)
            sp.wait_ge(chain_dve, 2)
            load_batch_ctx(1)
            with sp.Fori(2, B) as i:
                sp.wait_ge(resid_done, 2 * i - 2)
                load_batch_x(i)
                sp.wait_ge(chain_dve, 7 * (i - 1) + 2)
                load_batch_ctx(i)
                store(i - 2)
            store(B - 2)
            store(B - 1)
            sp.wait_ge(stored, 16 * B)

        @block.gpsimd
        def _(pool):
            pool.memset(ident[:, :], 0.0).then_inc(consts_ready, 1)
            pool.memset(mask[:, :], 0.0).then_inc(consts_ready, 1)
            pool.memset(identb[:, :], 0.0).then_inc(consts_ready, 1)
            pool.wait_ge(consts_ready, 3)
            pool.affine_select(out=ident[:, :], in_=ident[:, :], compare_op=ALU.not_equal, fill=1.0,
                               base=0, pattern=[[-1, P]], channel_multiplier=1).then_inc(consts_ready, 1)
            pool.affine_select(out=identb[:, :], in_=identb[:, :], compare_op=ALU.not_equal, fill=1.0,
                               base=0, pattern=[[-1, P]], channel_multiplier=1).then_inc(consts_ready, 1)
            pool.affine_select(out=mask[:, :], in_=mask[:, :], compare_op=ALU.is_ge, fill=MASKED,
                               base=0, pattern=[[-1, P]], channel_multiplier=1).then_inc(consts_ready, 1)
            for k in (k_hi, k_lo):
                pool.memset(f32(k[:, :, :, :]), 0.0).then_inc(consts_ready, 1)
            pool.memset(ones[:, :], 1.0).then_inc(consts_ready, 1)
            pool.memset(f32(onesr[:, :]), 1.0).then_inc(consts_ready, 1)
            pool.memset(f32(convb_r[:, :]), 0.0).then_inc(consts_ready, 1)
            for f in (f_hi, f_lo):
                pool.memset(f32(f[:, 0:1]), 0.0).then_inc(consts_ready, 1)
                pool.memset(f32(f[:, T + 1:T + 2]), 0.0).then_inc(consts_ready, 1)
            for j in range(BITS):
                pool.memset(powers[:, :, j], float(2 ** j)).then_inc(consts_ready, 1)
                pool.memset(powers_up[:, :, j], float(2 ** j + E)).then_inc(consts_ready, 1)

            def normalise(layer, pos, split=None):
                for h in range(H):
                    if h == 4 and split is not None:
                        split_context(split)
                    b4 = h % 4
                    pool.wait_ge(rinv_ready, 16 * pos + h + 1)
                    if layer == 0:
                        last = pool.tensor_tensor(
                            probs[:, b4, :, :], probs[:, b4, :, :],
                            rinv[:, b4, :].rearrange("p (t o) -> p t o", o=1).to_broadcast([P, NT, T]),
                            ALU.mult)
                    else:
                        for t in range(NT):
                            n = P * (t + 1)
                            last = pool.tensor_tensor(
                                probs[:, b4, t, 0:n], probs[:, b4, t, 0:n],
                                rinv[:, b4, t:t + 1].to_broadcast([P, n]), ALU.mult)
                    last.then_inc(probs_ready, 1)

            def split_context(b):
                pool.wait_ge(chain_act, 9 * b + 1)
                pool.tensor_tensor(ct_hi[:, :], ctx_t[:, 0:T], ones[:, 0:1].to_broadcast([P, T]), ALU.mult)\
                    .then_inc(ctx_split, 1)
                pool.wait_ge(ctx_split, 2 * b + 1)
                pool.tensor_tensor(ct_lo[:, :], ctx_t[:, 0:T], f32(ct_hi[:, :]), ALU.subtract)\
                    .then_inc(ctx_split, 1)

            normalise(0, 0)
            normalise(0, 1, 0)
            normalise(1, 2)
            with pool.Fori(2, B) as i:
                normalise(0, 2 * i - 1, i - 1)
                normalise(1, 2 * i)
            split_context(B - 1)
            normalise(1, 2 * B - 1)

        @block.scalar
        def _(act):
            act.dma_start(wo[0][0:DH, :, :],
                          wo0[0, :, :].rearrange("(d c h) m -> h d c m", c=PAIRS, h=2)[0, :, :, :])\
                .then_inc(load_wo0, 16)
            act.dma_start(wo[0][DH:P, :, :],
                          wo0[0, :, :].rearrange("(d c h) m -> h d c m", c=PAIRS, h=2)[1, :, :, :])\
                .then_inc(load_wo0, 16)
            for dst, src in (
                    (w12[:, 0, :].rearrange("p (c d) -> p c d", c=NH), w1.rearrange("(c p) d -> p c d", p=P)),
                    (w12[:, 1, :], w2),
                    (plane[:, :], planes),
                    (wzh[:, 0, :], wz),
                    (wzh[:, 1, :], wh),
                    (bzh[:, 0:1], bz.rearrange("(p o) -> p o", o=1)),
                    (bzh[:, 1:2], bh.rearrange("(p o) -> p o", o=1)),
                    (bqkv[:, 0, :], bq1.rearrange("(c p) -> p c", p=P)),
                    (bqkv[:, 1, :], bk1.rearrange("(c p) -> p c", p=P)),
                    (bqkv[:, 2, :], bv1.rearrange("(c p) -> p c", p=P)),
                    (bo_all[:, :], bo1.rearrange("(o m) -> o m", o=1).to_broadcast([P, D])),
                    (convw[:, :, :], conv_w.rearrange("(c p) o j -> p c (o j)", p=P)),
                    (convb[0:1, :], conv_b.rearrange("(o m) -> o m", o=1)),
                    (convb[32:33, :], conv_b.rearrange("(o m) -> o m", o=1))):
                act.dma_start(dst, src, allow_slow_non_contiguous=True).then_inc(load_small, 16)

            def split_weights(layer):
                act.wait_ge((load_w0, load_w1)[layer], 48)
                for j in range(3):
                    act.activation(whi[layer][:, j, :], stage[:, j, :], ACT.Copy,
                                   scale=(SCALE0, SCALE1)[layer] if j == 0 else 1.0)\
                        .then_inc(w_hi_ready, 1)

            def pair_hi(layer, pos, p):
                act.wait_ge(qk_psum, 8 * pos + p + 1)
                wait(act, scores_ready, 16 * pos + 2 * (p - 1))
                wait(act, qk_ready, 8 * pos + p - 1)
                j = p % 2
                if layer == 0:
                    act.activation(q_hi[:, j, :], qk_ps[:, 0:T], ACT.Copy)
                else:
                    act.activation(q_hi[:, j, :], qk_ps[:, 0:T], ACT.Identity, bias=bq_scaled[:, p:p + 1])
                for h in range(2):
                    if layer == 0:
                        last = act.activation(k_hi[rows(h), j, h, :], qk_ps[rows(h), T:2 * T], ACT.Copy)
                    else:
                        last = act.activation(k_hi[rows(h), j, h, :], qk_ps[rows(h), T:2 * T],
                                              ACT.Identity, bias=bqkv[rows(h), 1, p:p + 1])
                last.then_inc(qk_hi, 1)

            def attention(layer, pos, beside=None, b=None):
                act.wait_ge(xt_psum, pos + 1)
                wait(act, qk_psum, 8 * pos)
                act.activation(xt_hi[:, :], qk_ps[:, 0:T], ACT.Copy).then_inc(xt_hi_ready, 1)
                for g in (1, 3):
                    act.wait_ge(v_psum, 4 * pos + g + 1)
                    act.activation(v_sb[layer][:, g // 2, 512:1024], s_ps[1][:, :], ACT.Copy)\
                        .then_inc(v_odd, 1)
                pair_hi(layer, pos, 0)
                for s in range(SLOTS):
                    if s % 2 == 0 and s // 2 + 1 < PAIRS:
                        pair_hi(layer, pos, s // 2 + 1)
                    if s < H:
                        act.wait_ge(max_ready, 16 * pos + s + 1)
                        wait(act, pt_psum, 16 * pos + s - 3)
                        for t in range(NT):
                            n = T if layer == 0 else P * (t + 1)
                            last = act.activation(probs[:, s % 4, t, 0:n], s_ps[s % 2][:, t * T:t * T + n],
                                                  ACT.Exp, bias=negmax[:, s % 4, t:t + 1],
                                                  accum_out=rsum[:, s % 4, t:t + 1])
                        last.then_inc(exp_done, 1)
                    h = s - 2
                    if 0 <= h < H and h % 2 == 1:
                        act.wait_ge(pt_psum, 16 * pos + h + 1)
                        wait(act, o_psum, 8 * pos + h // 2 - 1)
                        if layer == 0:
                            act.activation(probs_t[:, h % 4, :, :], t_ps[1][:, :].rearrange(
                                "p (c q) -> p c q", c=NT), ACT.Copy).then_inc(pt_odd, 1)
                        else:
                            act.activation(probs_t[:, h % 4, 0, :], t_ps[1][:, 0:T], ACT.Copy)
                            act.activation(probs_t[:, h % 4, 1, P:T], t_ps[1][:, T + P:2 * T], ACT.Copy)\
                                .then_inc(pt_odd, 1)
                    if s % 2 == 0 and 0 <= s - 4:
                        p = (s - 4) // 2
                        act.wait_ge(o_psum, 8 * pos + p + 1)
                        wait(act, out_done, 8 * pos + p - 1)
                        if layer == 0:
                            act.activation(heads_t[:, p % 2, :], o_ps[:, 0:T], ACT.Copy).then_inc(o_ready, 1)
                        else:
                            act.activation(heads_t[:, p % 2, :], o_ps[:, 0:T], ACT.Identity,
                                           bias=bqkv[:, 2, p:p + 1]).then_inc(o_ready, 1)
                    if beside == "chain" and 0 <= s - 2 < 14:
                        chain(b, s - 2)
                    if beside == "ffn" and s % 3 == 1 and s // 3 < 5:
                        ffn(b, s // 3)

            def chain(b, k):
                def here():
                    act.wait_ge(chain_psum, 14 * b + k + 1)

                if k == 0:
                    here()
                    wait(act, ctx_split, 2 * b)
                    act.activation(ctx_t[:, :], m_ps[:, :], ACT.Copy).then_inc(chain_act, 1)
                elif k in (1, 11):
                    here()
                    act.activation(cn_t[:, :], m_ps[:, 0:T], ACT.Copy).then_inc(chain_act, 1)
                elif k in (2, 5):
                    t = (k - 2) // 3
                    act.wait_ge(chain_in, 6 * b + 2 + t)
                    act.activation(cprobs[:, :], m_ps[:, :], ACT.Exp, bias=cneg[:, t:t + 1],
                                   accum_out=csum[:, t:t + 1]).then_inc(chain_act, 1)
                elif k in (3, 6):
                    here()
                    act.activation(cprobs_t[:, :, :], m_ps[:, :].rearrange("p (c q) -> p c q", c=NC),
                                   ACT.Copy).then_inc(chain_act, 1)
                elif k == 12:
                    here()
                    act.activation(tz[:, :], m_ps[:, 0:T], ACT.Tanh, bias=bzh_half[:, 0:1], scale=0.5)\
                        .then_inc(chain_act, 1)
                    act.activation(th[:, :], m_ps[:, T:2 * T], ACT.Tanh, bias=bzh_half[:, 1:2], scale=0.5)\
                        .then_inc(chain_act, 1)

            def ffn(b, k):
                if k == 4:
                    return
                act.wait_ge(ffn_psum, 5 * b + k + 1)
                if k == 0:
                    act.activation(f_hi[:, 1:T + 1], m_ps[:, 0:T], ACT.Copy).then_inc(ffn_act, 1)
                elif k in (1, 2):
                    act.activation(ftanh, m_ps[:, :], ACT.Tanh, scale=0.5).then_inc(ffn_act, 1)
                elif k == 3:
                    act.activation(fq_t, m_bf.rearrange("p (c q) -> p c q", q=P), ACT.Copy)\
                        .then_inc(ffn_act, 1)

            split_weights(0)
            attention(0, 0)
            split_weights(1)
            for j in range(3):
                act.wait_ge(prep_psum, 3 + j)
                act.activation(w1_hi[:, j, :], m_ps[:, :], ACT.Copy).then_inc(prep_hi, 1)
            act.wait_ge(prep_read, 8)
            attention(0, 1, "chain", 0)
            attention(1, 2)
            with act.Fori(2, B) as i:
                attention(0, 2 * i - 1, "chain", i - 1)
                attention(1, 2 * i, "ffn", i - 2)
            for k in range(14):
                chain(B - 1, k)
            attention(1, 2 * B - 1, "ffn", B - 2)
            for k in range(5):
                ffn(B - 1, k)

        @block.tensor
        def _(pe):
            def product3(dst, l_hi, l_lo, r_hi, r_lo, start=True, stop=True):
                pe.matmul(dst, l_hi, r_hi, start=start, stop=False)
                pe.matmul(dst, l_hi, r_lo, start=False, stop=False)
                return pe.matmul(dst, l_lo, r_hi, start=False, stop=stop)

            def project_pair(layer, pos, p):
                if p > 0:
                    pe.wait_ge(qk_ready, 8 * pos + p)
                cols = slice(P * p, P * p + P)
                c_hi, c_lo = (xt_hi, xt_lo) if layer == 0 else (ct_hi, ct_lo)
                product3(qk_ps[:, 0:T], whi[layer][:, 0, cols], wlo[layer][:, 0, cols], xt_hi[:, :], xt_lo[:, :])
                product3(qk_ps[:, T:2 * T], whi[layer][:, 1, cols], wlo[layer][:, 1, cols],
                         c_hi[:, :], c_lo[:, :]).then_inc(qk_psum, 1)

            def scores(layer, pos, h):
                j = (h // 2) % 2
                pe.wait_ge(qk_ready, 8 * pos + h // 2 + 1)
                if h < 2:
                    pe.wait_ge((v_even, v_odd)[h], 2 * pos + 2)
                else:
                    pe.wait_ge(exp_done, 16 * pos + h - 1)
                for t in range(NT):
                    q = slice(P * t, P * t + P)
                    dst = s_ps[h % 2][:, T * t:T * t + T]
                    last = product3(dst, q_hi[:, j, q], q_lo[:, j, q], k_hi[:, j, h % 2, :],
                                    k_lo[:, j, h % 2, :], stop=layer == 0)
                    if layer == 1:
                        last = pe.matmul(s_ps[h % 2][:, T * t + P * t:T * t + P * t + P], identb[:, :],
                                         mask[:, :], start=False, stop=True)
                last.then_inc(scores_ready, 1)

            def transposes(layer, pos, h):
                pe.wait_ge(probs_ready, 16 * pos + h + 1)
                wait(pe, (pt_even, pt_odd)[h % 2], 8 * pos + h // 2)
                for c in range(NT):
                    for t in range(NT):
                        if layer == 1 and t < c:
                            continue
                        last = pe.transpose(t_ps[h % 2][:, T * c + P * t:T * c + P * t + P],
                                            probs[:, h % 4, t, P * c:P * c + P], ident[:, :])
                last.then_inc(pt_psum, 1)

            def values(layer, pos, p):
                pe.wait_ge(pt_even, 8 * pos + p + 1)
                pe.wait_ge(pt_odd, 8 * pos + p + 1)
                wait(pe, o_ready, 8 * pos + p)
                for c in range(NT):
                    q0 = P * c if layer == 1 else 0
                    for h in (2 * p, 2 * p + 1):
                        last = pe.matmul(o_ps[rows(h), q0:T], v_sb[layer][:, c, DH * h:DH * h + DH],
                                         probs_t[:, h % 4, c, q0:T], start=(c == 0), stop=(c == NT - 1),
                                         skip_group_check=True)
                last.then_inc(o_psum, 1)

            def output(layer, pos, p):
                pe.wait_ge(o_ready, 8 * pos + p + 1)
                if p == 0:
                    wait(pe, resid_done, pos)
                for t in range(NT):
                    last = pe.matmul(out_ps[:, D * t:D * t + D], heads_t[:, p % 2, P * t:P * t + P],
                                     wo[layer][:, p, :], start=(p == 0 and t == 0),
                                     stop=(p == PAIRS - 1 and t == NT - 1), skip_group_check=True)
                last.then_inc(out_done, 1)

            def attention(layer, b, pos, beside=None, bb=None):
                pe.wait_ge(xn_ready, pos + 1)
                wait(pe, qk_ready, 8 * pos)
                for t in range(NT):
                    last = pe.transpose(qk_ps[:, P * t:P * t + P], xn[:, t, :], ident[:, :])
                last.then_inc(xt_psum, 1)
                pe.wait_ge(xt_ready, pos + 1)
                wait(pe, exp_done, 16 * pos)
                c_hi, c_lo = (xt_hi, xt_lo) if layer == 0 else (ct_hi, ct_lo)
                if layer == 1:
                    pe.wait_ge(ctx_split, 2 * (b + 1))
                for g in range(4):
                    if g >= 2:
                        pe.wait_ge((v_even, v_odd)[g % 2], 2 * pos + 1)
                    tile, cols = slice(P * (g // 2), P * (g // 2) + P), slice(512 * (g % 2), 512 * (g % 2) + 512)
                    product3(s_ps[g % 2][:, :], c_hi[:, tile], c_lo[:, tile], whi[layer][:, 2, cols],
                             wlo[layer][:, 2, cols]).then_inc(v_psum, 1)
                project_pair(layer, pos, 0)
                for s in range(SLOTS):
                    if s % 2 == 0 and s // 2 + 1 < PAIRS:
                        project_pair(layer, pos, s // 2 + 1)
                    if s < H:
                        scores(layer, pos, s)
                    if 0 <= s - 2 < H:
                        transposes(layer, pos, s - 2)
                    if s % 2 == 0 and s >= 4:
                        values(layer, pos, (s - 4) // 2)
                    if s % 2 == 1 and s >= 5:
                        output(layer, pos, (s - 5) // 2)
                    if beside == "chain" and 0 <= s - 2 < 14:
                        chain(bb, s - 2)
                    if beside == "ffn" and s % 3 == 1 and s // 3 < 5:
                        ffn(bb, s // 3)

            def chain(b, k):
                if k == 0:
                    pe.wait_ge(m_free, 1 if isinstance(b, int) and b == 0 else b)
                    pe.wait_ge(load_ctx, 16 * (b + 1))
                    for c in range(NC):
                        last = pe.transpose(m_ps[:, P * c:P * c + P], ctx[:, c, :], ident[:, :])
                elif k in (1, 8, 11):
                    pe.wait_ge(chain_in, 6 * b + {1: 1, 8: 4, 11: 6}[k])
                    if k == 1:
                        pe.wait_ge(chain_act, 9 * b + 1)
                    for t in range(NT):
                        last = pe.transpose(m_ps[:, P * t:P * t + P], cn[:, t, :], ident[:, :])
                elif k in (2, 5):
                    t = (k - 2) // 3
                    if k == 2:
                        pe.wait_ge(chain_act, 9 * b + 2)
                    else:
                        pe.wait_ge(chain_dve, 7 * b + 1)
                    last = pe.matmul(m_ps[:, :], cn_t[:, P * t:P * t + P], ctx_t[:, :], start=True, stop=True)
                elif k in (3, 6):
                    pe.wait_ge(chain_act, 9 * b + k - (k == 6))
                    for c in range(NC):
                        last = pe.transpose(m_ps[:, P * c:P * c + P], cprobs[:, P * c:P * c + P], ident[:, :])
                elif k in (4, 7):
                    pe.wait_ge(chain_act, 9 * b + k - (k == 7))
                    for c in range(NC):
                        last = pe.matmul(m_ps[:, 0:D], cprobs_t[:, c, :], ctx[:, c, :], start=(c == 0),
                                         stop=(c == NC - 1))
                elif k == 9:
                    pe.wait_ge(chain_dve, 7 * b + 3)
                    for t in range(NT):
                        last = pe.matmul(m_ps[0:1, BITS * t:BITS * t + BITS], emb[:, t:t + 1], plane[:, :],
                                         start=(t == 0), stop=(t == NT - 1), skip_group_check=True)
                elif k == 10:
                    pe.wait_ge(chain_in, 6 * b + 5)
                    pe.matmul(m_ps[:, 0:1], identb[:, :], identb[:, 0:1], start=True, stop=True)
                    if isinstance(b, int) and b == 0:
                        pe.wait_ge(load_experts, 16)
                    for t in range(NT):
                        for e in range(2):
                            i = pe.value_load(index[0:1, e, t:t + 1], min_val=0, max_val=E - 1)
                            last = pe.matmul(m_ps[:, D * t:D * t + D], cn_t[:, P * t:P * t + P],
                                             expert[:, bass.ds(i * D, D)], start=(t == 0 and e == 0),
                                             stop=(t == NT - 1 and e == 1), skip_group_check=True)
                elif k == 12:
                    pe.wait_ge(chain_act, 9 * b + 7)
                    for j in range(2):
                        last = pe.matmul(m_ps[:, T * j:T * j + T], wzh_t[:, j, :], cn_t[:, :],
                                         start=True, stop=True)
                elif k == 13:
                    pe.wait_ge(chain_dve, 7 * b + 6)
                    for t in range(NT):
                        last = pe.transpose(m_ps[:, P * t:P * t + P], hid[:, P * t:P * t + P], ident[:, :])
                last.then_inc(chain_psum, 1)

            def ffn(b, k):
                if k == 0:
                    pe.wait_ge(ffn_in, 3 * b + 1)
                    for t in range(NT):
                        last = pe.transpose(m_ps[:, P * t:P * t + P], fn[:, t, :], ident[:, :])
                elif k in (1, 2):
                    t = k - 1
                    pe.wait_ge(ffn_dve, 3 * b + k)
                    pe.matmul(m_ps[:, :], onesr[:, :], convb_r[:, :], start=True, stop=False)
                    for j in range(3):
                        q = slice(P * t + j, P * t + j + P)
                        last = product3(m_ps[:, :], f_hi[:, q], f_lo[:, q], w1_hi[:, j, :], w1_lo[:, j, :],
                                        start=False, stop=(j == 2))
                elif k == 3:
                    pe.wait_ge(ffn_in, 3 * b + 3)
                    for t in range(NT):
                        for c in range(NH):
                            n = NH * t + c
                            last = pe.transpose(m_bf[:, P * n:P * n + P], fq[:, t, P * c:P * c + P],
                                                identb[:, :])
                elif k == 4:
                    pe.wait_ge(ffn_act, 4 * b + 4)
                    for t in range(NT):
                        for c in range(NH):
                            last = pe.matmul(m_ps[:, D * t:D * t + D], fq_t[:, NH * t + c, :], w2t[:, c, :],
                                             start=(t == 0 and c == 0), stop=(t == NT - 1 and c == NH - 1),
                                             skip_group_check=True)
                last.then_inc(ffn_psum, 1)

            def prepare():
                pe.wait_ge(load_small, 16 * 14)
                for j in range(2):
                    last = pe.transpose(m_ps[:, P * j:P * j + P], wzh[:, j, :], ident[:, :])
                last.then_inc(prep_psum, 1)
                pe.wait_ge(prep_in, 1)
                pe.wait_ge(prep_read, 1)
                pe.matmul(m_ps[:, 0:2], ones[:, :], wsum[:, :], start=True, stop=True).then_inc(prep_psum, 1)
                for j in range(3):
                    pe.wait_ge(prep_in, 2)
                    pe.wait_ge(prep_read, 2 + j)
                    for c in range(NH):
                        last = pe.transpose(m_ps[:, P * c:P * c + P], filt[:, j, c, :], ident[:, :])
                    last.then_inc(prep_psum, 1)
                pe.wait_ge(prep_read, 5)
                for c in range(NH):
                    last = pe.transpose(m_bf[:, P * c:P * c + P], tern2[:, P * c:P * c + P], identb[:, :])
                last.then_inc(prep_psum, 1)

            pe.wait_ge(consts_ready, 27)
            pe.wait_ge(w_lo_ready, 3)
            pe.wait_ge(load_wo0, 32)
            attention(0, 0, 0)
            prepare()
            attention(0, 1, 1, "chain", 0)
            pe.wait_ge(w_lo_ready, 6)
            pe.wait_ge(load_wo1, 16)
            attention(1, 0, 2)
            with pe.Fori(2, B) as i:
                attention(0, i, 2 * i - 1, "chain", i - 1)
                attention(1, i - 1, 2 * i, "ffn", i - 2)
            for k in range(14):
                chain(B - 1, k)
            attention(1, B - 1, 2 * B - 1, "ffn", B - 2)
            for k in range(5):
                ffn(B - 1, k)

        @block.vector
        def _(dve):
            def split_weights(layer):
                for j in range(3):
                    dve.wait_ge(w_hi_ready, 3 * layer + j + 1)
                    dve.scalar_tensor_tensor(
                        out=wlo[layer][:, j, :], in0=stage[:, j, :],
                        scalar=(SCALE0, SCALE1)[layer] if j == 0 else 1.0,
                        in1=f32(whi[layer][:, j, :]), op0=ALU.mult, op1=ALU.subtract).then_inc(w_lo_ready, 1)

            def pair_lo(layer, pos, p):
                dve.wait_ge(qk_hi, 8 * pos + p + 1)
                j = p % 2
                if layer == 0:
                    dve.tensor_tensor(q_lo[:, j, :], qk_ps[:, 0:T], f32(q_hi[:, j, :]), ALU.subtract)
                else:
                    dve.scalar_tensor_tensor(out=q_lo[:, j, :], in0=qk_ps[:, 0:T], scalar=bq_scaled[:, p:p + 1],
                                             in1=f32(q_hi[:, j, :]), op0=ALU.add, op1=ALU.subtract)
                for h in range(2):
                    r = rows(h)
                    if layer == 0:
                        last = dve.tensor_tensor(k_lo[r, j, h, :], qk_ps[r, T:2 * T], f32(k_hi[r, j, h, :]),
                                                 ALU.subtract)
                    else:
                        last = dve.scalar_tensor_tensor(
                            out=k_lo[r, j, h, :], in0=qk_ps[r, T:2 * T], scalar=bqkv[r, 1, p:p + 1],
                            in1=f32(k_hi[r, j, h, :]), op0=ALU.add, op1=ALU.subtract)
                last.then_inc(qk_ready, 1)

            def inverse(pos, h):
                dve.wait_ge(exp_done, 16 * pos + h + 1)
                wait(dve, probs_ready, 16 * pos + h - 3)
                dve.reciprocal(rinv[:, h % 4, :], rsum[:, h % 4, :]).then_inc(rinv_ready, 1)

            def attention(layer, b, pos, beside=None, bb=None):
                link = Steps(dve, attn_step[layer], ATTN_STEPS[layer] * b)
                src = x_in if layer == 0 else x_c
                if layer == 0:
                    dve.wait_ge(load_x, 16 * (b + 1))
                wait(dve, xt_psum, pos)
                layer_norm_steps(dve, link, src, xn).then_inc(xn_ready, 1)
                dve.wait_ge(xt_hi_ready, pos + 1)
                dve.tensor_tensor(xt_lo[:, :], qk_ps[:, 0:T], f32(xt_hi[:, :]), ALU.subtract)\
                    .then_inc(xt_ready, 1)
                for g in (0, 2):
                    dve.wait_ge(v_psum, 4 * pos + g + 1)
                    dve.tensor_copy(v_sb[layer][:, g // 2, 0:512], s_ps[0][:, :]).then_inc(v_even, 1)
                pair_lo(layer, pos, 0)
                for s in range(SLOTS):
                    if s % 2 == 0 and s // 2 + 1 < PAIRS:
                        pair_lo(layer, pos, s // 2 + 1)
                    if s < H:
                        dve.wait_ge(scores_ready, 16 * pos + s + 1)
                        wait(dve, exp_done, 16 * pos + s - 3)
                        if layer == 0:
                            dve.tensor_reduce(negmax[:, s % 4, :], s_ps[s % 2][:, :].rearrange(
                                "p (t k) -> p t k", t=NT), AX.X, ALU.max, negate=True).then_inc(max_ready, 1)
                        else:
                            dve.tensor_reduce(negmax[:, s % 4, 0:1], s_ps[s % 2][:, 0:P], AX.X, ALU.max,
                                              negate=True)
                            dve.tensor_reduce(negmax[:, s % 4, 1:2], s_ps[s % 2][:, T:2 * T], AX.X, ALU.max,
                                              negate=True).then_inc(max_ready, 1)
                    if 0 <= s - 1 < H:
                        inverse(pos, s - 1)
                    h = s - 2
                    if 0 <= h < H and h % 2 == 0:
                        dve.wait_ge(pt_psum, 16 * pos + h + 1)
                        wait(dve, o_psum, 8 * pos + h // 2 - 1)
                        if layer == 0:
                            dve.tensor_copy(probs_t[:, h % 4, :, :], t_ps[0][:, :].rearrange(
                                "p (c q) -> p c q", c=NT)).then_inc(pt_even, 1)
                        else:
                            dve.tensor_copy(probs_t[:, h % 4, 0, :], t_ps[0][:, 0:T])
                            dve.tensor_copy(probs_t[:, h % 4, 1, P:T], t_ps[0][:, T + P:2 * T])\
                                .then_inc(pt_even, 1)
                    if beside == "chain" and 0 <= s - 2 < 14:
                        chain(bb, s - 2)
                    if beside == "ffn" and s % 3 == 1 and s // 3 < 5:
                        ffn(bb, s // 3)
                dve.wait_ge(out_done, 8 * (pos + 1))
                o = out_ps[:, 0:NT * D].rearrange("p (t d) -> p t d", t=NT)
                if layer == 0:
                    dve.tensor_tensor(x_a[:, :, :], o, x_in[:, :, :], ALU.add).then_inc(resid_done, 1)
                else:
                    link(dve.tensor_tensor(x_f[:, :, :], x_c[:, :, :], bo_all[:, :].rearrange(
                        "p (o d) -> p o d", o=1).to_broadcast([P, NT, D]), ALU.add))
                    dve.tensor_tensor(x_f[:, :, :], o, x_f[:, :, :], ALU.add).then_inc(resid_done, 1)
                dve.wait_ge(resid_done, pos + 1)
                if beside == "ffn":
                    dve.wait_ge(stored, 16 * (bb + 1))
                link.end(ATTN_STEPS[layer])

            chain_link = [None]

            def chain(b, k):
                if k == 0:
                    chain_link[0] = Steps(dve, chain_step, CHAIN_STEPS * b)
                    link = chain_link[0]
                    layer_norm_steps(dve, link, x_a, cn).then_inc(chain_in, 1)
                    return
                link = chain_link[0]

                def here():
                    dve.wait_ge(chain_psum, 14 * b + k + 1)

                if k in (2, 5):
                    t = (k - 2) // 3
                    here()
                    dve.tensor_reduce(cneg[:, t:t + 1], m_ps[:, :], AX.X, ALU.max, negate=True)\
                        .then_inc(chain_in, 1)
                elif k in (4, 7):
                    t = (k - 4) // 3
                    here()
                    link(dve.reciprocal(cinv[:, t:t + 1], csum[:, t:t + 1]))
                    dve.scalar_tensor_tensor(out=x_c[:, t, :], in0=m_ps[:, 0:D], scalar=cinv[:, t:t + 1],
                                             in1=x_a[:, t, :], op0=ALU.mult, op1=ALU.add)\
                        .then_inc(chain_dve, 1)
                    if k == 7:
                        dve.wait_ge(chain_dve, 7 * b + 2)
                        layer_norm_steps(dve, link, x_c, cn).then_inc(chain_in, 1)
                elif k == 8:
                    here()
                    link(dve.tensor_copy(cn_t[:, :], m_ps[:, 0:T]))
                    link(dve.tensor_reduce(emb[:, :], cn_t[:, :].rearrange("p (t q) -> p t q", t=NT), AX.X,
                                           ALU.add))
                    dve.tensor_scalar(emb[:, :], emb[:, :], 1.0 / P, None, ALU.mult).then_inc(chain_dve, 1)
                elif k == 9:
                    here()
                    proj, size, bits, weak, cands, tmp = (hsh[:, j, :, :] for j in range(6))
                    code, least, flip, bit, sign, _ = (hsv[:, j, :] for j in range(6))

                    def spread(v):
                        return v.rearrange("p (t o) -> p t o", o=1).to_broadcast([1, NT, BITS])

                    dve.tensor_copy(proj, m_ps[0:1, 0:NT * BITS].rearrange("p (t j) -> p t j", t=NT))\
                        .then_inc(chain_dve, 1)
                    dve.wait_ge(chain_dve, 7 * b + 4)
                    link(dve.tensor_scalar(bits, proj, 0.0, None, ALU.is_gt))
                    link(dve.tensor_tensor(tmp, bits, powers[:, :, :], ALU.mult))
                    link(dve.tensor_reduce(code, tmp, AX.X, ALU.add))
                    link(dve.scalar_tensor_tensor(out=size, in0=proj, scalar=-1.0, in1=proj, op0=ALU.mult,
                                                  op1=ALU.max))
                    link(dve.tensor_reduce(least, size, AX.X, ALU.min))
                    link(dve.tensor_tensor(weak, size, spread(least), ALU.is_equal))
                    link(dve.scalar_tensor_tensor(out=cands, in0=weak, scalar=-float(E), in1=powers_up[:, :, :],
                                                  op0=ALU.mult, op1=ALU.add))
                    link(dve.tensor_reduce(flip, cands, AX.X, ALU.min))
                    link(dve.tensor_tensor(weak, cands, spread(flip), ALU.is_equal))
                    link(dve.tensor_tensor(tmp, weak, bits, ALU.mult))
                    link(dve.tensor_reduce(bit, tmp, AX.X, ALU.add))
                    link(dve.tensor_scalar(sign, bit, -2.0, 1.0, ALU.mult, ALU.add))
                    link(dve.tensor_copy(chosen[:, 0, :], code))
                    link(dve.tensor_tensor(sign, sign, flip, ALU.mult))
                    link(dve.tensor_tensor(chosen[:, 1, :], sign, code, ALU.add))
                    dve.tensor_copy(index[:, :, :], chosen[:, :, :]).then_inc(chain_in, 1)
                elif k == 10:
                    here()
                    dve.scalar_tensor_tensor(out=x_c[:, :, :], in0=m_ps[:, 0:NT * D].rearrange(
                        "p (t d) -> p t d", t=NT), scalar=0.5, in1=x_c[:, :, :], op0=ALU.mult, op1=ALU.add)\
                        .then_inc(chain_dve, 1)
                    dve.wait_ge(chain_dve, 7 * b + 5)
                    layer_norm_steps(dve, link, x_c, cn).then_inc(chain_in, 1)
                elif k == 12:
                    dve.wait_ge(chain_act, 9 * b + 9)
                    link(dve.tensor_scalar(pos_part[:, :], m_ps[:, T:2 * T], bzh[:, 1:2], 0.0, ALU.add, ALU.max))
                    link(dve.tensor_scalar(cand[:, :], th[:, :], 0.5, 0.0, ALU.mult, ALU.min))
                    link(dve.scalar_tensor_tensor(out=cand[:, :], in0=cand[:, :], scalar=0.5, in1=pos_part[:, :],
                                                  op0=ALU.add, op1=ALU.add))
                    link(dve.scalar_tensor_tensor(out=cand[:, :], in0=tz[:, :], scalar=1.0, in1=cand[:, :],
                                                  op0=ALU.add, op1=ALU.mult))
                    link(dve.tensor_scalar(keep[:, :], tz[:, :], -0.5, 0.5, ALU.mult, ALU.add))
                    dve.tensor_tensor_scan(hid[:, :], keep[:, :], cand[:, :], 1.0, ALU.mult, ALU.add)\
                        .then_inc(chain_dve, 1)
                elif k == 13:
                    here()
                    dve.scalar_tensor_tensor(out=x_c[:, :, :], in0=m_ps[:, 0:NT * D].rearrange(
                        "p (t d) -> p t d", t=NT), scalar=0.5, in1=x_c[:, :, :], op0=ALU.mult, op1=ALU.add)\
                        .then_inc(chain_dve, 1)
                    dve.wait_ge(chain_dve, 7 * (b + 1))
                    link.end(CHAIN_STEPS)

            ffn_link = [None]

            def ffn(b, k):
                if k == 0:
                    link = ffn_link[0] = Steps(dve, ffn_step, FFN_STEPS * b)
                    link(layer_norm_steps(dve, link, x_f, fn))
                    link(dve.tensor_reduce(fmax[:, :], fn[:, :, :], AX.X, ALU.max, apply_absolute_value=True))
                    link(dve.tensor_scalar(fmax[:, :], fmax[:, :], 1e-5, None, ALU.max))
                    link(dve.reciprocal(fscale[:, :], fmax[:, :]))
                    link(dve.tensor_scalar(fscale[:, :], fscale[:, :], 127.0, None, ALU.mult))
                    link(dve.reciprocal(finv[:, :], fscale[:, :]))
                    for t in range(NT):
                        link(dve.tensor_scalar(fn[:, t, :], fn[:, t, :], fscale[:, t:t + 1], ROUND, ALU.mult,
                                               ALU.add))
                    for t in range(NT):
                        ins = dve.tensor_scalar(fn[:, t, :], fn[:, t, :], ROUND, finv[:, t:t + 1],
                                                ALU.subtract, ALU.mult)
                    ins.then_inc(ffn_in, 1)
                    dve.wait_ge(ffn_act, 4 * b + 1)
                    dve.tensor_tensor(f_lo[:, 1:T + 1], m_ps[:, 0:T], f32(f_hi[:, 1:T + 1]), ALU.subtract)\
                        .then_inc(ffn_dve, 1)
                    return
                link = ffn_link[0]
                if k in (1, 2):
                    t = k - 1
                    dve.wait_ge(ffn_act, 4 * b + k + 1)
                    dve.wait_ge(ffn_in, 3 * b + k)
                    dve.scalar_tensor_tensor(out=fy[:, :], in0=ftanh, scalar=1.0, in1=m_ps[:, :],
                                             op0=ALU.add, op1=ALU.mult).then_inc(ffn_dve, 1)
                    dve.wait_ge(ffn_dve, 3 * b + k + 1)
                    link(dve.tensor_reduce(gmax[:, t:t + 1], fy[:, :], AX.X, ALU.max, apply_absolute_value=True))
                    link(dve.tensor_scalar(gmax[:, t:t + 1], gmax[:, t:t + 1], 0.5, 1e-5, ALU.mult, ALU.max))
                    link(dve.reciprocal(gscale[:, t:t + 1], gmax[:, t:t + 1]))
                    link(dve.tensor_scalar(gscale[:, t:t + 1], gscale[:, t:t + 1], 127.0, None, ALU.mult))
                    link(dve.reciprocal(ginv[:, t:t + 1], gscale[:, t:t + 1]))
                    link(dve.tensor_scalar(gscale[:, t:t + 1], gscale[:, t:t + 1], 0.5, None, ALU.mult))
                    link(dve.tensor_scalar(fy[:, :], fy[:, :], gscale[:, t:t + 1], ROUND, ALU.mult, ALU.add))
                    dve.tensor_scalar(fq[:, t, :], fy[:, :], ROUND, None, ALU.subtract).then_inc(ffn_in, 1)
                elif k == 4:
                    link(dve.tensor_scalar(ginv[:, :], ginv[:, :], winv[:, 1:2], None, ALU.mult))
                    dve.wait_ge(ffn_psum, 5 * (b + 1))
                    for t in range(NT):
                        last = dve.scalar_tensor_tensor(
                            out=y_out[:, t, :], in0=m_ps[:, D * t:D * t + D], scalar=ginv[:, t:t + 1],
                            in1=x_f[:, t, :], op0=ALU.mult, op1=ALU.add)
                    last.then_inc(y_ready, 1)
                    dve.wait_ge(y_ready, b + 1)
                    dve.memset(beat[:, 0:1], 0.0).then_inc(m_free, 1)
                    link.end(FFN_STEPS)

            def prepare():
                link = Steps(dve, prep_step, 0)
                dve.wait_ge(load_small, 16 * 14)
                for j in range(2):
                    link(dve.tensor_reduce(wsum[:, j:j + 1], w12[:, j, :], AX.X, ALU.add,
                                           apply_absolute_value=True))
                dve.engine_nop().then_inc(prep_in, 1)
                dve.wait_ge(prep_psum, 1)
                dve.tensor_copy(wzh_t[:, :, :], m_ps[:, 0:2 * P].rearrange("p (j h) -> p j h", j=2))\
                    .then_inc(prep_read, 1)
                dve.wait_ge(prep_psum, 2)
                dve.tensor_scalar(wmean[:, :], m_ps[:, 0:2], 1.0 / (HID * D), 1e-5, ALU.mult, ALU.max)\
                    .then_inc(prep_read, 1)
                dve.wait_ge(prep_read, 2)
                link(dve.reciprocal(wscale[:, :], wmean[:, :]))
                link(dve.reciprocal(winv[:, :], wscale[:, :]))
                for j in range(2):
                    w = w12[:, j, :]
                    link(dve.tensor_scalar(w, w, wscale[:, j:j + 1], ROUND, ALU.mult, ALU.add))
                    link(dve.tensor_scalar(w, w, ROUND, 1.0, ALU.subtract, ALU.min))
                link(dve.tensor_scalar(w12[:, 0, :], w12[:, 0, :], -1.0, winv[:, 0:1], ALU.max, ALU.mult))
                link(dve.tensor_scalar(tern2, w12[:, 1, :], -1.0, None, ALU.max))
                for j in range(3):
                    for c in range(NH):
                        link(dve.tensor_scalar(filt[:, j, c, :], w12[:, 0, P * c:P * c + P],
                                               convw[:, c, j:j + 1], None, ALU.mult))
                dve.engine_nop().then_inc(prep_in, 1)
                for j in range(3):
                    dve.wait_ge(prep_hi, j + 1)
                    dve.tensor_tensor(w1_lo[:, j, :], m_ps[:, :], f32(w1_hi[:, j, :]), ALU.subtract)\
                        .then_inc(prep_read, 1)
                dve.wait_ge(prep_psum, 6)
                dve.tensor_copy(w2t[:, :, :], m_bf[:, 0:HID].rearrange("p (c m) -> p c m", c=NH))\
                    .then_inc(prep_read, 1)
                link(dve.tensor_copy(convb_r[0:1, :], convb[0:1, :]))
                link(dve.tensor_copy(convb_r[32:33, :], convb[32:33, :]))
                link(dve.tensor_tensor(convb_r[32:33, :], convb[32:33, :], f32(convb_r[32:33, :]), ALU.subtract))
                dve.tensor_scalar(bq_scaled[:, :], bqkv[:, 0, :], SCALE1, None, ALU.mult).then_inc(prep_read, 1)
                dve.tensor_scalar(bzh_half[:, :], bzh[:, :], 0.5, None, ALU.mult).then_inc(prep_read, 1)
                dve.wait_ge(prep_read, 8)
                dve.engine_nop().then_inc(m_free, 1)

            dve.wait_ge(consts_ready, 27)
            split_weights(0)
            attention(0, 0, 0)
            split_weights(1)
            prepare()
            attention(0, 1, 1, "chain", 0)
            attention(1, 0, 2)
            with dve.Fori(2, B) as i:
                attention(0, i, 2 * i - 1, "chain", i - 1)
                attention(1, i - 1, 2 * i, "ffn", i - 2)
            for k in range(14):
                chain(B - 1, k)
            attention(1, B - 1, 2 * B - 1, "ffn", B - 2)
            for k in range(5):
                ffn(B - 1, k)


_INS = ['x', 'ctx_1024', 'L0_attn_kernel', 'L0_attn_WO', 'L0_ffn_expert_weights', 'L0_ffn_hyperplanes',
        'L1_attn_Wz', 'L1_attn_bz', 'L1_attn_Wh', 'L1_attn_bh', 'L1_xattn_Wq', 'L1_xattn_bq', 'L1_xattn_Wk',
        'L1_xattn_bk', 'L1_xattn_Wv', 'L1_xattn_bv', 'L1_xattn_Wo', 'L1_xattn_bo', 'L1_ffn_w1',
        'L1_ffn_conv_w', 'L1_ffn_conv_b', 'L1_ffn_w2']
_OUTS = [((8, 256, 128), 'float32')]


def kernel(**inputs):
    import numpy as _np
    import concourse.bacc as _bacc
    from concourse import mybir as _mybir
    from concourse.bass_utils import run_bass_kernel_spmd as _run

    nc = _bacc.Bacc("TRN2", target_bir_lowering=False, num_devices=1)
    arrays, args = {}, []
    for name in _INS:
        a = _np.ascontiguousarray(inputs[name])
        arrays[f"in_{name}_dram"] = a
        args.append(nc.dram_tensor(f"in_{name}_dram", a.shape, _mybir.dt.from_np(a.dtype), kind="ExternalInput").ap())
    for i, (shape, dtype) in enumerate(_OUTS):
        dt = _mybir.dt.from_np(_np.dtype(dtype))
        args.append(nc.dram_tensor(f"out_{i}_dram", shape, dt, kind="ExternalOutput").ap())
    build(nc, *args)
    r = _run(nc, [arrays], core_ids=[0])
    return r.results[0]["out_0_dram"]
```

```python
from contextlib import ExitStack

import concourse.bass as bass
from concourse import mybir

P = 128
B, T, D = 8, 256, 128
NT = T // P
CTX = 512
NC = CTX // P
H, DH = 16, 64
HD = H * DH
PAIRS = H // 2
E = 64
BITS = 6
HID = 512
NH = HID // P
SCALE0 = 1.0 / (DH * DH * H)
SCALE1 = 1.0 / 8.0
EPS = 1e-5
ROUND = 12582912.0
MASKED = -1e36

CHAIN_AT = {3: (0,), 4: ("stats0",), 5: ("apply0", 1), 6: (2,), 7: (3,), 8: (4,), 9: (5,), 10: (6,),
            11: (7, "stats1"), 12: ("apply1", 8), 13: (9,)}
CHAIN_END_AT = {0: (10, "stats2"), 1: ("apply2", 11), 2: (12,), 4: (13,)}
FFN_AT = {4: ("stats",), 5: ("apply",), 7: (0,), 9: (1,), 11: (2,), 13: (3,), 15: (4,)}
CHAIN_END = (10, "stats2", "apply2", 11, 12, 13)
FFN_ALL = ("stats", "apply", 0, 1, 2, 3, 4)
PREP_AT = {4: (0,), 5: (1,), 7: (2,), 9: (3,), 11: (4,), 13: (5,), 14: (6,)}
CHAIN_PARTS = {9: 5, 12: 3}
CHAIN_DVE_AT = {
    (4, "end"): (("stats0", 0),), (5, "mid"): (("apply0", 0),), (6, "end"): ((2, 0),),
    (8, "end"): ((4, 0),), (9, "end"): ((5, 0),), (11, "end"): ((7, 0), ("stats1", 0)),
    (12, "mid"): (("apply1", 0),), (12, "end"): ((8, 0),), (13, "end"): ((9, 0),),
    (14, "mid"): ((9, 1),), (14, "end"): ((9, 2),), (15, "mid"): ((9, 3),), (15, "end"): ((9, 4),)}
CHAIN_END_DVE_AT = {
    (0, "end"): ((10, 0), ("stats2", 0)), (1, "mid"): (("apply2", 0),), (2, "end"): ((12, 0),),
    (3, "mid"): ((12, 1),), (3, "end"): ((12, 2),), (4, "end"): ((13, 0),)}
FFN_PARTS = {"apply": 4, 1: 3, 2: 3, 4: 2}
FFN_DVE_AT = {
    (4, "end"): (("stats", 0),), (5, "mid"): (("apply", 0),), (5, "end"): (("apply", 1),),
    (6, "mid"): (("apply", 2),), (6, "end"): (("apply", 3),), (7, "end"): ((0, 0),),
    (9, "end"): ((1, 0),), (10, "mid"): ((1, 1),), (10, "end"): ((1, 2),),
    (11, "end"): ((2, 0),), (12, "mid"): ((2, 1),), (12, "end"): ((2, 2),),
    (14, "mid"): ((4, 0),), (15, "end"): ((4, 1),)}

F32 = mybir.dt.float32
F32R = mybir.dt.float32r
BF16 = mybir.dt.bfloat16
I32 = mybir.dt.int32
ALU = mybir.AluOpType
ACT = mybir.ActivationFunctionType
AX = mybir.AxisListType

LN_STEPS = 3
CHAIN_STEPS = 23
FFN_STEPS = 20


def build(nc, x, ctx_d, w0, wo0, experts, planes, wz, bz, wh, bh, wq1, bq1, wk1, bk1, wv1, bv1,
          wo1, bo1, w1, conv_w, conv_b, w2, out):
    with ExitStack() as st:
        def sb(name, shape, dt=F32):
            return st.enter_context(nc.sbuf_tensor(name, shape, dt))

        def pb(name):
            return st.enter_context(nc.psum_tensor(name, [P, 512], F32))

        def sem(name):
            return st.enter_context(nc.semaphore(name))

        ident = sb("ident", [P, P])
        identb = sb("identb", [P, P], BF16)
        mask = sb("mask", [P, P], BF16)
        ones = sb("ones", [P, P])
        onesr = sb("onesr", [P, P], F32R)
        powers = sb("powers", [1, NT, BITS])
        powers_up = sb("powers_up", [1, NT, BITS])
        stage = sb("stage", [P, 3, HD])
        whi = [sb(f"whi{l}", [P, 3, HD], F32R) for l in range(2)]
        wlo = [sb(f"wlo{l}", [P, 3, HD], F32R) for l in range(2)]
        wo = [sb(f"wo{l}", [P, PAIRS, D]) for l in range(2)]
        expert = sb("expert", [P, E * D])
        plane = sb("plane", [P, BITS])
        wzh = sb("wzh", [P, 2, D])
        wzh_t = sb("wzh_t", [P, 2, D])
        bzh = sb("bzh", [P, 2])
        bzh_half = sb("bzh_half", [P, 2])
        bqkv = sb("bqkv", [P, 3, PAIRS])
        bq_scaled = sb("bq_scaled", [P, PAIRS])
        bo_all = sb("bo_all", [P, D])
        w12 = sb("w12", [P, 2, HID])
        convw = sb("convw", [P, NH, 3])
        convb_r = sb("convb_r", [P, HID], F32R)
        w1_hi = sb("w1_hi", [P, 3, HID], F32R)
        w1_lo = sb("w1_lo", [P, 3, HID], F32R)
        w2t = sb("w2t", [P, NH, D], BF16)
        wsum = sb("wsum", [P, 2])
        wmean = sb("wmean", [P, 2])
        wscale = sb("wscale", [P, 2])
        winv = sb("winv", [P, 2])
        x_in = sb("x_in", [P, NT, D])
        x_a = sb("x_a", [P, NT, D])
        x_c = sb("x_c", [P, NT, D])
        x_f = sb("x_f", [P, NT, D])
        y_out = sb("y_out", [P, NT, D])
        stats = sb("stats", [P, 3, NT, 6])
        mv = sb("mv", [P, 3, NT, 2])
        rstd = sb("rstd", [P, 3, NT])
        eps_pow = sb("eps_pow", [P, 2, NT])
        beat = sb("beat", [P, 1])
        xn = sb("xn", [P, NT, D])
        xt_hi = [sb(f"xt_hi{j}", [P, T], F32R) for j in range(2)]
        xt_lo = [sb(f"xt_lo{j}", [P, T], F32R) for j in range(2)]
        ct_hi = sb("ct_hi", [P, T], F32R)
        ct_lo = sb("ct_lo", [P, T], F32R)
        q_hi = sb("q_hi", [P, 2, T], F32R)
        q_lo = sb("q_lo", [P, 2, T], F32R)
        k_hi = sb("k_hi", [P, 2, 2, T], F32R)
        k_lo = sb("k_lo", [P, 2, 2, T], F32R)
        v_sb = [sb(f"v_sb{j}", [P, NT, HD]) for j in range(2)]
        probs = sb("probs", [P, 4, NT, T])
        negmax = sb("negmax", [P, 4, NT])
        rsum = sb("rsum", [P, 4, NT])
        rinv = sb("rinv", [P, 4, NT])
        probs_t = sb("probs_t", [P, 4, NT, T])
        heads_t = sb("heads_t", [P, 2, T])
        ctx = sb("ctx", [P, NC, D])
        ctx_t = sb("ctx_t", [P, CTX])
        cn = sb("cn", [P, NT, D])
        cn_t = sb("cn_t", [P, T])
        cprobs = sb("cprobs", [P, CTX])
        cprobs_t = sb("cprobs_t", [P, NC, P])
        cneg = sb("cneg", [P, NT])
        csum = sb("csum", [P, NT])
        cinv = sb("cinv", [P, NT])
        emb = sb("emb", [P, NT])
        hsh = sb("hsh", [1, 8, NT, BITS])
        hsv = sb("hsv", [1, 4, NT])
        chosen = sb("chosen", [1, 2, NT])
        index = sb("index", [1, 2, NT], I32)
        tz = sb("tz", [P, T])
        th = sb("th", [P, T])
        keep = sb("keep", [P, T])
        cand = sb("cand", [P, T])
        pos_part = sb("pos_part", [P, T])
        hid = sb("hid", [P, T])
        fn = sb("fn", [P, NT, D])
        fmax = sb("fmax", [P, NT])
        fscale = sb("fscale", [P, NT])
        finv = sb("finv", [P, NT])
        f_hi = sb("f_hi", [P, T + 2], F32R)
        f_lo = sb("f_lo", [P, T + 2], F32R)
        ftanh = stage[:, 0, 0:HID]
        fy = sb("fy", [P, HID])
        convb = fy
        gmax = sb("gmax", [P, NT])
        gscale = sb("gscale", [P, NT])
        ginv = sb("ginv", [P, NT])
        fq = sb("fq", [P, NT, HID], BF16)
        fq_t = stage[:, 1, 0:HID].bitcast(BF16).rearrange("p (c q) -> p c q", q=P)
        filt = expert[:, 0:3 * HID].rearrange("p (j c d) -> p j c d", j=3, c=NH)
        tern2 = fq[:, 0, :]

        s_ps = [pb("s_ps0"), pb("s_ps1")]
        t_ps = pb("t_ps")
        qk_ps = pb("qk_ps")
        v_ps = pb("v_ps")
        o_ps = pb("o_ps")
        out_ps = pb("out_ps")
        m_ps = pb("m_ps")
        m_bf = m_ps[:, :].bitcast(BF16)

        load_x = sem("load_x")
        load_ctx = sem("load_ctx")
        load_w0 = sem("load_w0")
        load_wo0 = sem("load_wo0")
        load_w1 = sem("load_w1")
        load_wo1 = sem("load_wo1")
        load_experts = sem("load_experts")
        load_small = sem("load_small")
        consts_ready = sem("consts_ready")
        w_hi_ready = sem("w_hi_ready")
        w_lo_ready = sem("w_lo_ready")
        prep_step = sem("prep_step")
        prep_psum = sem("prep_psum")
        prep_hi = sem("prep_hi")
        prep_in = sem("prep_in")
        prep_read = sem("prep_read")
        xn_ready = sem("xn_ready")
        xt_psum = sem("xt_psum")
        xt_hi_ready = sem("xt_hi_ready")
        xt_ready = sem("xt_ready")
        v_psum = sem("v_psum")
        v_even = sem("v_even")
        v_odd = sem("v_odd")
        qk_psum = sem("qk_psum")
        qk_hi = sem("qk_hi")
        qk_ready = sem("qk_ready")
        scores_ready = sem("scores_ready")
        max_ready = sem("max_ready")
        exp_done = sem("exp_done")
        rinv_ready = sem("rinv_ready")
        probs_ready = sem("probs_ready")
        pt_psum = sem("pt_psum")
        pt_even = sem("pt_even")
        pt_odd = sem("pt_odd")
        o_psum = sem("o_psum")
        o_ready = sem("o_ready")
        out_done = sem("out_done")
        resid_done = sem("resid_done")
        carry_done = sem("carry_done")
        ln_step = [sem(f"ln_step{j}") for j in range(3)]
        ln_stats = [sem(f"ln_stats{j}") for j in range(3)]
        ln_rstd = [sem(f"ln_rstd{j}") for j in range(3)]
        chain_step = sem("chain_step")
        ffn_step = sem("ffn_step")
        chain_psum = sem("chain_psum")
        chain_act = sem("chain_act")
        chain_dve = sem("chain_dve")
        chain_in = sem("chain_in")
        ctx_split = sem("ctx_split")
        ffn_in = sem("ffn_in")
        ffn_psum = sem("ffn_psum")
        ffn_act = sem("ffn_act")
        ffn_dve = sem("ffn_dve")
        m_free = sem("m_free")
        y_ready = sem("y_ready")
        stored = sem("stored")

        def wait(eng, s, value):
            if not isinstance(value, int) or value > 0:
                eng.wait_ge(s, value)

        def f32(ap):
            return ap.bitcast(F32)

        def rows(h):
            return slice(DH * (h % 2), DH * (h % 2) + DH)

        LN_PHASE, LN_CHAIN, LN_FFN = range(3)

        def norm_stats(dve, j, n, src):
            link = Steps(dve, ln_step[j], LN_STEPS * n)
            for t in range(NT):
                link(dve.bn_stats(stats[:, j, t, :], src[:, t, :]), wait=t == NT - 1)
            dve.memset(beat[:, 0:1], 0.0)
            link(dve.bn_aggr(mv[:, j, 0, :], stats[:, j, 0, :]), wait=False)
            dve.bn_aggr(mv[:, j, 1, :], stats[:, j, 1, :]).then_inc(ln_stats[j], 1)
            link.end(LN_STEPS)

        def norm_scale(pool, j, n):
            pool.wait_ge(ln_stats[j], n + 1)
            pool.tensor_tensor(rstd[:, j, :], mv[:, j, :, 1], eps_pow[:, 0, :], ALU.add)\
                .then_inc(ln_rstd[j], 1)
            pool.wait_ge(ln_rstd[j], 2 * n + 1)
            pool.tensor_tensor(rstd[:, j, :], rstd[:, j, :], eps_pow[:, 1, :], ALU.pow)\
                .then_inc(ln_rstd[j], 1)

        def norm_apply(dve, j, n, src, dst):
            dve.wait_ge(ln_rstd[j], 2 * n + 2)
            for t in range(NT):
                ins = dve.tensor_scalar(dst[:, t, :], src[:, t, :], mv[:, j, t, 0:1], rstd[:, j, t:t + 1],
                                        ALU.subtract, ALU.mult)
            return ins

        class Steps:

            def __init__(self, eng, s, base):
                self.eng, self.s, self.base, self.n = eng, s, base, 0

            def __call__(self, ins, wait=True):
                self.n += 1
                ins.then_inc(self.s, 1)
                if wait:
                    self.eng.wait_ge(self.s, self.base + self.n)

            def end(self, total):
                assert self.n == total, (self.n, total)

        def phase_a(b):
            return (0, b, 0, 0) if isinstance(b, int) and b == 0 else (0, b, 2 * b - 1, 1)

        def phase_b(b):
            return (1, b, 2 * B - 1, 1) if isinstance(b, int) and b == B - 1 else (1, b, 2 * b + 2, 0)

        def program(eng, phase, chain, ffn, prepare, bridge):
            bridge(phase_a(0))
            phase(phase_a(0), None, phase_a(1), prep=True)
            phase(phase_a(1), phase_a(0), None, chain_of=0)
            for k in CHAIN_END:
                chain(0, k)
            bridge(phase_b(0))
            phase(phase_b(0), phase_a(1), phase_a(2), chain_of=1)
            with eng.Fori(2, B - 1) as i:
                phase(phase_a(i), phase_b(i - 2), phase_b(i - 1), end_of=i - 1, ffn_of=i - 2)
                phase(phase_b(i - 1), phase_a(i), phase_a(i + 1), chain_of=i)
            phase(phase_a(B - 1), phase_b(B - 3), phase_b(B - 2), end_of=B - 2, ffn_of=B - 3)
            phase(phase_b(B - 2), phase_a(B - 1), None, chain_of=B - 1)
            for k in CHAIN_END:
                chain(B - 1, k)
            bridge(phase_b(B - 1))
            phase(phase_b(B - 1), phase_b(B - 2), None, ffn_of=B - 2)
            phase(None, phase_b(B - 1), None)
            for k in FFN_ALL:
                ffn(B - 1, k)

        def beside(s, when, chain, ffn, prepare, prep, chain_of, end_of, ffn_of):
            for steps, at, b in ((prepare, PREP_AT, 0 if prep else None), (chain, CHAIN_END_AT, end_of),
                                 (chain, CHAIN_AT, chain_of), (ffn, FFN_AT, ffn_of)):
                for k in at.get(s, ()) if b is not None else ():
                    if (not str(k).startswith("apply")) == when:
                        steps(b, k)

        block = st.enter_context(nc.Block())

        @block.sync
        def _(sp):
            def load_batch_x(b, dst=x_in):
                sp.dma_start(dst[:, :, :], x[b, :, :].rearrange("(t p) d -> p t d", p=P))\
                    .then_inc(load_x, 16)

            def load_batch_ctx(b):
                sp.dma_start(ctx[:, :, :], ctx_d[b, :, :].rearrange("(t p) d -> p t d", p=P))\
                    .then_inc(load_ctx, 16)

            def store(b):
                sp.wait_ge(y_ready, 1 * (b + 1))
                sp.dma_start(out[b, :, :].rearrange("(t p) d -> p t d", p=P), y_out[:, :, :])\
                    .then_inc(stored, 16)

            load_batch_x(0)
            for j in range(3):
                sp.dma_start(stage[:, j, :].rearrange("p (h d) -> p h d", h=H),
                             w0[j, :, :, :].rearrange("h m d -> m h d")).then_inc(load_w0, 16)
            load_batch_x(1, y_out)
            load_batch_ctx(0)
            sp.dma_start(wo[1][:, :, :], wo1.rearrange("(c p) m -> p c m", p=P)).then_inc(load_wo1, 16)
            sp.wait_ge(w_lo_ready, 3)
            for j, w in enumerate((wq1, wk1, wv1)):
                sp.dma_start(stage[:, j, :], w).then_inc(load_w1, 16)
            sp.wait_ge(prep_read, 5)
            sp.dma_start(expert[:, :].rearrange("p (e n) -> p e n", e=E),
                         experts.rearrange("e d n -> d e n")).then_inc(load_experts, 16)
            sp.wait_ge(resid_done, 1)
            load_batch_x(2)
            sp.wait_ge(chain_dve, 2)
            load_batch_ctx(1)
            sp.wait_ge(chain_dve, 9)
            load_batch_ctx(2)
            with sp.Fori(2, B - 1) as i:
                store(i - 2)
                sp.wait_ge(resid_done, 2 * i)
                load_batch_x(i + 1)
                sp.wait_ge(chain_dve, 7 * i + 2)
                load_batch_ctx(i + 1)
            for b in range(B - 3, B):
                store(b)
            sp.wait_ge(stored, 16 * B)

        @block.gpsimd
        def _(pool):
            pool.memset(ident[:, :], 0.0).then_inc(consts_ready, 1)
            pool.memset(mask[:, :], 0.0).then_inc(consts_ready, 1)
            pool.memset(identb[:, :], 0.0).then_inc(consts_ready, 1)
            pool.wait_ge(consts_ready, 3)
            pool.affine_select(out=ident[:, :], in_=ident[:, :], compare_op=ALU.not_equal, fill=1.0,
                               base=0, pattern=[[-1, P]], channel_multiplier=1).then_inc(consts_ready, 1)
            pool.affine_select(out=identb[:, :], in_=identb[:, :], compare_op=ALU.not_equal, fill=1.0,
                               base=0, pattern=[[-1, P]], channel_multiplier=1).then_inc(consts_ready, 1)
            pool.affine_select(out=mask[:, :], in_=mask[:, :], compare_op=ALU.is_ge, fill=MASKED,
                               base=0, pattern=[[-1, P]], channel_multiplier=1).then_inc(consts_ready, 1)
            for k in (k_hi, k_lo):
                pool.memset(f32(k[:, :, :, :]), 0.0).then_inc(consts_ready, 1)
            pool.memset(ones[:, :], 1.0).then_inc(consts_ready, 1)
            pool.memset(f32(onesr[:, :]), 1.0).then_inc(consts_ready, 1)
            pool.memset(f32(convb_r[:, :]), 0.0).then_inc(consts_ready, 1)
            for f in (f_hi, f_lo):
                pool.memset(f32(f[:, 0:1]), 0.0).then_inc(consts_ready, 1)
                pool.memset(f32(f[:, T + 1:T + 2]), 0.0).then_inc(consts_ready, 1)
            for j in range(BITS):
                pool.memset(powers[:, :, j], float(2 ** j)).then_inc(consts_ready, 1)
                pool.memset(powers_up[:, :, j], float(2 ** j + E)).then_inc(consts_ready, 1)

            for t in range(2):
                pool.memset(eps_pow[:, t, :], (EPS, -0.5)[t]).then_inc(consts_ready, 1)
            pool.wait_ge(consts_ready, 29)

            def normalise(layer, pos, h):
                b4 = h % 4
                pool.wait_ge(rinv_ready, 16 * pos + h + 1)
                if layer == 0:
                    last = pool.tensor_tensor(
                        probs[:, b4, :, :], probs[:, b4, :, :],
                        rinv[:, b4, :].rearrange("p (t o) -> p t o", o=1).to_broadcast([P, NT, T]),
                        ALU.mult)
                else:
                    for t in range(NT):
                        n = P * (t + 1)
                        last = pool.tensor_tensor(
                            probs[:, b4, t, 0:n], probs[:, b4, t, 0:n],
                            rinv[:, b4, t:t + 1].to_broadcast([P, n]), ALU.mult)
                last.then_inc(probs_ready, 1)

            def split_context(b, pos):
                pool.wait_ge(chain_act, 9 * b + 1)
                pool.wait_ge(qk_psum, 8 * pos + 8)
                pool.tensor_tensor(ct_hi[:, :], ctx_t[:, 0:T], ones[:, 0:1].to_broadcast([P, T]), ALU.mult)\
                    .then_inc(ctx_split, 1)
                pool.wait_ge(ctx_split, 2 * b + 1)
                pool.tensor_tensor(ct_lo[:, :], ctx_t[:, 0:T], f32(ct_hi[:, :]), ALU.subtract)\
                    .then_inc(ctx_split, 1)

            def chain(b, k):
                if str(k).startswith("stats"):
                    norm_scale(pool, LN_CHAIN, 3 * b + int(k[-1]))

            def ffn(b, k):
                if k == "stats":
                    norm_scale(pool, LN_FFN, b)

            def prepare(b, k):
                pass

            def bridge(nxt):
                norm_scale(pool, LN_PHASE, nxt[2])

            def phase(cur, prev, nxt, prep=False, chain_of=None, end_of=None, ffn_of=None):
                for s in range(H if cur else 4):
                    beside(s, 0, chain, ffn, prepare, prep, chain_of, end_of, ffn_of)
                    if cur:
                        normalise(cur[0], cur[2], s)
                    if nxt and s == 5:
                        norm_scale(pool, LN_PHASE, nxt[2])
                    beside(s, 1, chain, ffn, prepare, prep, chain_of, end_of, ffn_of)
                    if chain_of is not None and s == 14:
                        split_context(chain_of, cur[2])

            program(pool, phase, chain, ffn, prepare, bridge)

        @block.scalar
        def _(act):
            act.dma_start(wo[0][0:DH, :, :],
                          wo0[0, :, :].rearrange("(d c h) m -> h d c m", c=PAIRS, h=2)[0, :, :, :])\
                .then_inc(load_wo0, 16)
            act.dma_start(wo[0][DH:P, :, :],
                          wo0[0, :, :].rearrange("(d c h) m -> h d c m", c=PAIRS, h=2)[1, :, :, :])\
                .then_inc(load_wo0, 16)
            for dst, src in (
                    (w12[:, 0, :].rearrange("p (c d) -> p c d", c=NH), w1.rearrange("(c p) d -> p c d", p=P)),
                    (w12[:, 1, :], w2),
                    (plane[:, :], planes),
                    (wzh[:, 0, :], wz),
                    (wzh[:, 1, :], wh),
                    (bzh[:, 0:1], bz.rearrange("(p o) -> p o", o=1)),
                    (bzh[:, 1:2], bh.rearrange("(p o) -> p o", o=1)),
                    (bqkv[:, 0, :], bq1.rearrange("(c p) -> p c", p=P)),
                    (bqkv[:, 1, :], bk1.rearrange("(c p) -> p c", p=P)),
                    (bqkv[:, 2, :], bv1.rearrange("(c p) -> p c", p=P)),
                    (bo_all[:, :], bo1.rearrange("(o m) -> o m", o=1).to_broadcast([P, D])),
                    (convw[:, :, :], conv_w.rearrange("(c p) o j -> p c (o j)", p=P)),
                    (convb[0:1, :], conv_b.rearrange("(o m) -> o m", o=1)),
                    (convb[32:33, :], conv_b.rearrange("(o m) -> o m", o=1))):
                act.dma_start(dst, src, allow_slow_non_contiguous=True).then_inc(load_small, 16)

            def split_weights(layer, j):
                act.wait_ge((load_w0, load_w1)[layer], 48)
                act.activation(whi[layer][:, j, :], stage[:, j, :], ACT.Copy,
                               scale=(SCALE0, SCALE1)[layer] if j == 0 else 1.0).then_inc(w_hi_ready, 1)

            def pair_hi(layer, pos, p):
                act.wait_ge(qk_psum, 8 * pos + p + 1)
                wait(act, scores_ready, 16 * pos + 2 * (p - 1))
                wait(act, qk_ready, 8 * pos + p - 1)
                j = p % 2
                if layer == 0:
                    act.activation(q_hi[:, j, :], qk_ps[:, 0:T], ACT.Copy)
                else:
                    act.activation(q_hi[:, j, :], qk_ps[:, 0:T], ACT.Identity, bias=bq_scaled[:, p:p + 1])
                for h in range(2):
                    if layer == 0:
                        last = act.activation(k_hi[rows(h), j, h, :], qk_ps[rows(h), T:2 * T], ACT.Copy)
                    else:
                        last = act.activation(k_hi[rows(h), j, h, :], qk_ps[rows(h), T:2 * T],
                                              ACT.Identity, bias=bqkv[rows(h), 1, p:p + 1])
                last.then_inc(qk_hi, 1)

            def input_hi(nxt):
                _, _, pos, j = nxt
                act.wait_ge(xt_psum, pos + 1)
                act.activation(xt_hi[j][:, :], v_ps[:, 0:T], ACT.Copy).then_inc(xt_hi_ready, 1)

            def values_out(nxt, g):
                _, _, pos, j = nxt
                act.wait_ge(v_psum, 4 * pos + g + 1)
                act.activation(v_sb[j][:, g // 2, 512:1024], v_ps[:, :], ACT.Copy).then_inc(v_odd, 1)

            def exponentials(layer, pos, h):
                act.wait_ge(max_ready, 16 * pos + h + 1)
                wait(act, pt_psum, 16 * pos + h - 3)
                for t in range(NT):
                    n = T if layer == 0 else P * (t + 1)
                    last = act.activation(probs[:, h % 4, t, 0:n], s_ps[h % 2][:, t * T:t * T + n],
                                          ACT.Exp, bias=negmax[:, h % 4, t:t + 1],
                                          accum_out=rsum[:, h % 4, t:t + 1])
                last.then_inc(exp_done, 1)

            def probs_t_out(layer, pos, h):
                act.wait_ge(pt_psum, 16 * pos + h + 1)
                wait(act, o_psum, 8 * pos + h // 2 - 1)
                if layer == 0:
                    act.activation(probs_t[:, h % 4, :, :], t_ps[:, :].rearrange(
                        "p (c q) -> p c q", c=NT), ACT.Copy).then_inc(pt_odd, 1)
                else:
                    act.activation(probs_t[:, h % 4, 0, :], t_ps[:, 0:T], ACT.Copy)
                    act.activation(probs_t[:, h % 4, 1, P:T], t_ps[:, T + P:2 * T], ACT.Copy)\
                        .then_inc(pt_odd, 1)

            def heads_out(layer, pos, p):
                act.wait_ge(o_psum, 8 * pos + p + 1)
                wait(act, out_done, 8 * pos + p - 1)
                if layer == 0:
                    act.activation(heads_t[:, p % 2, :], o_ps[:, 0:T], ACT.Copy).then_inc(o_ready, 1)
                else:
                    act.activation(heads_t[:, p % 2, :], o_ps[:, 0:T], ACT.Identity,
                                   bias=bqkv[:, 2, p:p + 1]).then_inc(o_ready, 1)

            def bridge(nxt):
                input_hi(nxt)
                values_out(nxt, 1)
                values_out(nxt, 3)
                pair_hi(nxt[0], nxt[2], 0)

            def phase(cur, prev, nxt, prep=False, chain_of=None, end_of=None, ffn_of=None):
                for s in range(H if cur else 4):
                    beside(s, 0, chain, ffn, prepare, prep, chain_of, end_of, ffn_of)
                    if s % 2 == 0 and cur and s // 2 + 1 < PAIRS:
                        pair_hi(cur[0], cur[2], s // 2 + 1)
                    if s == 14 and nxt:
                        pair_hi(nxt[0], nxt[2], 0)
                    if cur:
                        exponentials(cur[0], cur[2], s)
                    if nxt and s == 7:
                        input_hi(nxt)
                    if nxt and s in (11, 15):
                        values_out(nxt, 1 if s == 11 else 3)
                    at, h = (cur, s - 2) if s >= 2 else (prev, H + s - 2)
                    if at and h % 2 == 1:
                        probs_t_out(at[0], at[2], h)
                    at, p = (cur, s // 2 - 2) if s >= 4 else (prev, PAIRS + s // 2 - 2)
                    if at and s % 2 == 0:
                        heads_out(at[0], at[2], p)
                    beside(s, 1, chain, ffn, prepare, prep, chain_of, end_of, ffn_of)

            def chain(b, k):
                def here():
                    act.wait_ge(chain_psum, 14 * b + k + 1)

                if k == 0:
                    here()
                    wait(act, ctx_split, 2 * b)
                    act.activation(ctx_t[:, :], m_ps[:, :], ACT.Copy).then_inc(chain_act, 1)
                elif k in (1, 11):
                    here()
                    act.activation(cn_t[:, :], m_ps[:, 0:T], ACT.Copy).then_inc(chain_act, 1)
                elif k in (2, 5):
                    t = (k - 2) // 3
                    act.wait_ge(chain_in, 6 * b + 2 + t)
                    act.activation(cprobs[:, :], m_ps[:, :], ACT.Exp, bias=cneg[:, t:t + 1],
                                   accum_out=csum[:, t:t + 1]).then_inc(chain_act, 1)
                elif k in (3, 6):
                    here()
                    act.activation(cprobs_t[:, :, :], m_ps[:, :].rearrange("p (c q) -> p c q", c=NC),
                                   ACT.Copy).then_inc(chain_act, 1)
                elif k == 12:
                    here()
                    act.activation(tz[:, :], m_ps[:, 0:T], ACT.Tanh, bias=bzh_half[:, 0:1], scale=0.5)\
                        .then_inc(chain_act, 1)
                    act.activation(th[:, :], m_ps[:, T:2 * T], ACT.Tanh, bias=bzh_half[:, 1:2], scale=0.5)\
                        .then_inc(chain_act, 1)

            def ffn(b, k):
                if k not in (0, 1, 2, 3):
                    return
                act.wait_ge(ffn_psum, 5 * b + k + 1)
                if k == 0:
                    act.activation(f_hi[:, 1:T + 1], m_ps[:, 0:T], ACT.Copy).then_inc(ffn_act, 1)
                elif k in (1, 2):
                    act.activation(ftanh, m_ps[:, :], ACT.Tanh, scale=0.5).then_inc(ffn_act, 1)
                elif k == 3:
                    act.activation(fq_t, m_bf.rearrange("p (c q) -> p c q", q=P), ACT.Copy)\
                        .then_inc(ffn_act, 1)

            def prepare(b, k):
                if 2 <= k <= 4:
                    act.wait_ge(prep_psum, 1 + k)
                    act.activation(w1_hi[:, k - 2, :], m_ps[:, :], ACT.Copy).then_inc(prep_hi, 1)
                    split_weights(1, k - 2)
                if k == 6:
                    act.wait_ge(prep_read, 8)

            for j in range(3):
                split_weights(0, j)
            program(act, phase, chain, ffn, prepare, bridge)

        @block.tensor
        def _(pe):
            def product3(dst, l_hi, l_lo, r_hi, r_lo, start=True, stop=True):
                pe.matmul(dst, l_hi, r_hi, start=start, stop=False)
                pe.matmul(dst, l_hi, r_lo, start=False, stop=False)
                return pe.matmul(dst, l_lo, r_hi, start=False, stop=stop)

            def project_pair(at, p):
                layer, _, pos, j = at
                cols = slice(P * p, P * p + P)
                c_hi, c_lo = (xt_hi[j], xt_lo[j]) if layer == 0 else (ct_hi, ct_lo)
                product3(qk_ps[:, 0:T], whi[layer][:, 0, cols], wlo[layer][:, 0, cols],
                         xt_hi[j][:, :], xt_lo[j][:, :])
                product3(qk_ps[:, T:2 * T], whi[layer][:, 1, cols], wlo[layer][:, 1, cols],
                         c_hi[:, :], c_lo[:, :]).then_inc(qk_psum, 1)

            def transpose_input(nxt):
                pe.wait_ge(xn_ready, nxt[2] + 1)
                for t in range(NT):
                    last = pe.transpose(v_ps[:, P * t:P * t + P], xn[:, t, :], ident[:, :])
                last.then_inc(xt_psum, 1)

            def project_values(nxt, g):
                layer, _, _, j = nxt
                c_hi, c_lo = (xt_hi[j], xt_lo[j]) if layer == 0 else (ct_hi, ct_lo)
                tile, cols = slice(P * (g // 2), P * (g // 2) + P), slice(512 * (g % 2), 512 * (g % 2) + 512)
                product3(v_ps[:, :], c_hi[:, tile], c_lo[:, tile], whi[layer][:, 2, cols],
                         wlo[layer][:, 2, cols]).then_inc(v_psum, 1)

            def scores(layer, pos, h):
                j = (h // 2) % 2
                pe.wait_ge(qk_ready, 8 * pos + h // 2 + 1)
                wait(pe, exp_done, 16 * pos + h - 1)
                for t in range(NT):
                    q = slice(P * t, P * t + P)
                    dst = s_ps[h % 2][:, T * t:T * t + T]
                    last = product3(dst, q_hi[:, j, q], q_lo[:, j, q], k_hi[:, j, h % 2, :],
                                    k_lo[:, j, h % 2, :], stop=layer == 0)
                    if layer == 1:
                        last = pe.matmul(s_ps[h % 2][:, T * t + P * t:T * t + P * t + P], identb[:, :],
                                         mask[:, :], start=False, stop=True)
                last.then_inc(scores_ready, 1)

            def transposes(layer, pos, h):
                pe.wait_ge(probs_ready, 16 * pos + h + 1)
                wait(pe, (pt_odd, pt_even)[h % 2], 8 * pos + (h + 1) // 2)
                for c in range(NT):
                    for t in range(NT):
                        if layer == 1 and t < c:
                            continue
                        last = pe.transpose(t_ps[:, T * c + P * t:T * c + P * t + P],
                                            probs[:, h % 4, t, P * c:P * c + P], ident[:, :])
                last.then_inc(pt_psum, 1)

            def values(layer, pos, j, p):
                if p == 0:
                    pe.wait_ge(v_odd, 2 * pos + 2)
                    pe.wait_ge(v_even, 2 * pos + 2)
                pe.wait_ge(pt_even, 8 * pos + p + 1)
                pe.wait_ge(pt_odd, 8 * pos + p + 1)
                wait(pe, o_ready, 8 * pos + p)
                for c in range(NT):
                    q0 = P * c if layer == 1 else 0
                    for h in (2 * p, 2 * p + 1):
                        last = pe.matmul(o_ps[rows(h), q0:T], v_sb[j][:, c, DH * h:DH * h + DH],
                                         probs_t[:, h % 4, c, q0:T], start=(c == 0), stop=(c == NT - 1),
                                         skip_group_check=True)
                last.then_inc(o_psum, 1)

            def output(layer, pos, p):
                pe.wait_ge(o_ready, 8 * pos + p + 1)
                if p == 0:
                    wait(pe, resid_done, pos)
                for t in range(NT):
                    last = pe.matmul(out_ps[:, D * t:D * t + D], heads_t[:, p % 2, P * t:P * t + P],
                                     wo[layer][:, p, :], start=(p == 0 and t == 0),
                                     stop=(p == PAIRS - 1 and t == NT - 1), skip_group_check=True)
                last.then_inc(out_done, 1)

            def bridge(nxt):
                _, b, pos, _ = nxt
                if pos == 0:
                    pe.wait_ge(consts_ready, 29)
                    pe.wait_ge(w_lo_ready, 3)
                transpose_input(nxt)
                pe.wait_ge(xt_ready, pos + 1)
                if nxt[0] == 1:
                    pe.wait_ge(ctx_split, 2 * (b + 1))
                    pe.wait_ge(w_lo_ready, 6)
                for g in range(4):
                    if g > 0:
                        pe.wait_ge((v_even, v_odd)[(g - 1) % 2], 2 * pos + (g + 1) // 2)
                    project_values(nxt, g)
                wait(pe, qk_ready, 8 * pos)
                project_pair(nxt, 0)

            def phase(cur, prev, nxt, prep=False, chain_of=None, end_of=None, ffn_of=None):
                for s in range(H if cur else 4):
                    beside(s, 0, chain, ffn, prepare, prep, chain_of, end_of, ffn_of)
                    if s % 2 == 0 and cur and s // 2 + 1 < PAIRS:
                        p, pos = s // 2 + 1, cur[2]
                        pe.wait_ge(qk_ready, 8 * pos + p)
                        project_pair(cur, p)
                    if s == 14 and nxt:
                        pe.wait_ge(qk_ready, 8 * nxt[2])
                        project_pair(nxt, 0)
                    if cur:
                        scores(cur[0], cur[2], s)
                    if nxt and s == 7:
                        transpose_input(nxt)
                    if nxt and s in (9, 11, 13, 15):
                        g = (s - 9) // 2
                        if g == 0:
                            pe.wait_ge(xt_ready, nxt[2] + 1)
                        else:
                            pe.wait_ge((v_even, v_odd)[(g - 1) % 2], 2 * nxt[2] + (g + 1) // 2)
                        if nxt[0] == 1 and g == 0:
                            pe.wait_ge(ctx_split, 2 * (nxt[1] + 1))
                        project_values(nxt, g)
                    if s % 2 == 0:
                        at, p = (cur, s // 2 - 2) if s >= 4 else (prev, PAIRS + s // 2 - 2)
                        if at:
                            values(at[0], at[2], at[3], p)
                    else:
                        at, p = (cur, s // 2 - 2) if s >= 5 else (prev, PAIRS + s // 2 - 2)
                        if at:
                            output(at[0], at[2], p)
                    at, h = (cur, s - 2) if s >= 2 else (prev, H + s - 2)
                    if at:
                        transposes(at[0], at[2], h)
                    beside(s, 1, chain, ffn, prepare, prep, chain_of, end_of, ffn_of)

            def chain(b, k):
                if not isinstance(k, int):
                    return
                if k == 0:
                    pe.wait_ge(m_free, max(1, b) if isinstance(b, int) else b)
                    pe.wait_ge(load_ctx, 16 * (b + 1))
                    for c in range(NC):
                        last = pe.transpose(m_ps[:, P * c:P * c + P], ctx[:, c, :], ident[:, :])
                elif k in (1, 8, 11):
                    pe.wait_ge(chain_in, 6 * b + {1: 1, 8: 4, 11: 6}[k])
                    if k == 1:
                        pe.wait_ge(chain_act, 9 * b + 1)
                    for t in range(NT):
                        last = pe.transpose(m_ps[:, P * t:P * t + P], cn[:, t, :], ident[:, :])
                elif k in (2, 5):
                    t = (k - 2) // 3
                    if k == 2:
                        pe.wait_ge(chain_act, 9 * b + 2)
                    else:
                        pe.wait_ge(chain_dve, 7 * b + 1)
                    last = pe.matmul(m_ps[:, :], cn_t[:, P * t:P * t + P], ctx_t[:, :], start=True, stop=True)
                elif k in (3, 6):
                    pe.wait_ge(chain_act, 9 * b + k - (k == 6))
                    for c in range(NC):
                        last = pe.transpose(m_ps[:, P * c:P * c + P], cprobs[:, P * c:P * c + P], ident[:, :])
                elif k in (4, 7):
                    pe.wait_ge(chain_act, 9 * b + k - (k == 7))
                    for c in range(NC):
                        last = pe.matmul(m_ps[:, 0:D], cprobs_t[:, c, :], ctx[:, c, :], start=(c == 0),
                                         stop=(c == NC - 1))
                elif k == 9:
                    pe.wait_ge(chain_dve, 7 * b + 3)
                    for t in range(NT):
                        last = pe.matmul(m_ps[0:1, BITS * t:BITS * t + BITS], emb[:, t:t + 1], plane[:, :],
                                         start=(t == 0), stop=(t == NT - 1), skip_group_check=True)
                elif k == 10:
                    pe.wait_ge(chain_in, 6 * b + 5)
                    pe.matmul(m_ps[:, 0:1], identb[:, :], identb[:, 0:1], start=True, stop=True)
                    if isinstance(b, int) and b == 0:
                        pe.wait_ge(load_experts, 16)
                    picked = [[pe.value_load(index[0:1, e, t:t + 1], min_val=0, max_val=E - 1)
                               for e in range(2)] for t in range(NT)]
                    for t in range(NT):
                        for e in range(2):
                            last = pe.matmul(m_ps[:, D * t:D * t + D], cn_t[:, P * t:P * t + P],
                                             expert[:, bass.ds(picked[t][e] * D, D)], start=(t == 0 and e == 0),
                                             stop=(t == NT - 1 and e == 1), skip_group_check=True)
                elif k == 12:
                    pe.wait_ge(chain_act, 9 * b + 7)
                    for j in range(2):
                        last = pe.matmul(m_ps[:, T * j:T * j + T], wzh_t[:, j, :], cn_t[:, :],
                                         start=True, stop=True)
                elif k == 13:
                    pe.wait_ge(chain_dve, 7 * b + 6)
                    for t in range(NT):
                        last = pe.transpose(m_ps[:, P * t:P * t + P], hid[:, P * t:P * t + P], ident[:, :])
                last.then_inc(chain_psum, 1)

            def ffn(b, k):
                if not isinstance(k, int):
                    return
                if k == 0:
                    pe.wait_ge(ffn_in, 3 * b + 1)
                    for t in range(NT):
                        last = pe.transpose(m_ps[:, P * t:P * t + P], fn[:, t, :], ident[:, :])
                elif k in (1, 2):
                    t = k - 1
                    pe.wait_ge(ffn_dve, 3 * b + k)
                    pe.matmul(m_ps[:, :], onesr[:, :], convb_r[:, :], start=True, stop=False)
                    for j in range(3):
                        q = slice(P * t + j, P * t + j + P)
                        last = product3(m_ps[:, :], f_hi[:, q], f_lo[:, q], w1_hi[:, j, :], w1_lo[:, j, :],
                                        start=False, stop=(j == 2))
                elif k == 3:
                    pe.wait_ge(ffn_in, 3 * b + 3)
                    for t in range(NT):
                        for c in range(NH):
                            n = NH * t + c
                            last = pe.transpose(m_bf[:, P * n:P * n + P], fq[:, t, P * c:P * c + P],
                                                identb[:, :])
                elif k == 4:
                    pe.wait_ge(ffn_act, 4 * b + 4)
                    for t in range(NT):
                        for c in range(NH):
                            last = pe.matmul(m_ps[:, D * t:D * t + D], fq_t[:, NH * t + c, :], w2t[:, c, :],
                                             start=(t == 0 and c == 0), stop=(t == NT - 1 and c == NH - 1),
                                             skip_group_check=True)
                last.then_inc(ffn_psum, 1)

            def prepare(b, k):
                if k == 0:
                    pe.wait_ge(load_small, 16 * 14)
                    for j in range(2):
                        last = pe.transpose(m_ps[:, P * j:P * j + P], wzh[:, j, :], ident[:, :])
                    last.then_inc(prep_psum, 1)
                elif k == 1:
                    pe.wait_ge(prep_in, 1)
                    pe.wait_ge(prep_read, 1)
                    pe.matmul(m_ps[:, 0:2], ones[:, :], wsum[:, :], start=True, stop=True)\
                        .then_inc(prep_psum, 1)
                elif k <= 4:
                    pe.wait_ge(prep_in, k)
                    pe.wait_ge(prep_read, k)
                    for c in range(NH):
                        last = pe.transpose(m_ps[:, P * c:P * c + P], filt[:, k - 2, c, :], ident[:, :])
                    last.then_inc(prep_psum, 1)
                elif k == 5:
                    pe.wait_ge(prep_in, 5)
                    pe.wait_ge(prep_read, 5)
                    for c in range(NH):
                        last = pe.transpose(m_bf[:, P * c:P * c + P], tern2[:, P * c:P * c + P], identb[:, :])
                    last.then_inc(prep_psum, 1)
                elif k == 6:
                    pe.wait_ge(load_wo0, 32)
                    pe.wait_ge(load_wo1, 16)

            pe.wait_ge(load_wo0, 32)
            program(pe, phase, chain, ffn, prepare, bridge)

        @block.vector
        def _(dve):
            def split_weights(layer, j):
                dve.wait_ge(w_hi_ready, 3 * layer + j + 1)
                dve.scalar_tensor_tensor(
                    out=wlo[layer][:, j, :], in0=stage[:, j, :],
                    scalar=(SCALE0, SCALE1)[layer] if j == 0 else 1.0,
                    in1=f32(whi[layer][:, j, :]), op0=ALU.mult, op1=ALU.subtract).then_inc(w_lo_ready, 1)

            def pair_lo(layer, pos, p):
                dve.wait_ge(qk_hi, 8 * pos + p + 1)
                j = p % 2
                if layer == 0:
                    dve.tensor_tensor(q_lo[:, j, :], qk_ps[:, 0:T], f32(q_hi[:, j, :]), ALU.subtract)
                else:
                    dve.scalar_tensor_tensor(out=q_lo[:, j, :], in0=qk_ps[:, 0:T], scalar=bq_scaled[:, p:p + 1],
                                             in1=f32(q_hi[:, j, :]), op0=ALU.add, op1=ALU.subtract)
                for h in range(2):
                    r = rows(h)
                    if layer == 0:
                        last = dve.tensor_tensor(k_lo[r, j, h, :], qk_ps[r, T:2 * T], f32(k_hi[r, j, h, :]),
                                                 ALU.subtract)
                    else:
                        last = dve.scalar_tensor_tensor(
                            out=k_lo[r, j, h, :], in0=qk_ps[r, T:2 * T], scalar=bqkv[r, 1, p:p + 1],
                            in1=f32(k_hi[r, j, h, :]), op0=ALU.add, op1=ALU.subtract)
                last.then_inc(qk_ready, 1)

            def inverse(pos, h):
                dve.wait_ge(exp_done, 16 * pos + h + 1)
                wait(dve, probs_ready, 16 * pos + h - 3)
                dve.reciprocal(rinv[:, h % 4, :], rsum[:, h % 4, :]).then_inc(rinv_ready, 1)

            def source(at):
                layer, b, _, _ = at
                return x_c if layer == 1 else y_out if isinstance(b, int) and b == 1 else x_in

            def input_stats(nxt):
                layer, b, pos, _ = nxt
                if layer == 0:
                    dve.wait_ge(load_x, 16 * (b + 1))
                norm_stats(dve, LN_PHASE, pos, source(nxt))

            def input_apply(nxt):
                wait(dve, xt_psum, nxt[2])
                norm_apply(dve, LN_PHASE, nxt[2], source(nxt), xn).then_inc(xn_ready, 1)

            def input_lo(nxt):
                _, _, pos, j = nxt
                dve.wait_ge(xt_hi_ready, pos + 1)
                dve.tensor_tensor(xt_lo[j][:, :], v_ps[:, 0:T], f32(xt_hi[j][:, :]), ALU.subtract)\
                    .then_inc(xt_ready, 1)

            def values_out(nxt, g):
                _, _, pos, j = nxt
                dve.wait_ge(v_psum, 4 * pos + g + 1)
                dve.tensor_copy(v_sb[j][:, g // 2, 0:512], v_ps[:, :]).then_inc(v_even, 1)

            def maxima(layer, pos, h):
                dve.wait_ge(scores_ready, 16 * pos + h + 1)
                wait(dve, exp_done, 16 * pos + h - 3)
                if layer == 0:
                    dve.tensor_reduce(negmax[:, h % 4, :], s_ps[h % 2][:, :].rearrange(
                        "p (t k) -> p t k", t=NT), AX.X, ALU.max, negate=True).then_inc(max_ready, 1)
                else:
                    dve.tensor_reduce(negmax[:, h % 4, 0:1], s_ps[h % 2][:, 0:P], AX.X, ALU.max,
                                      negate=True)
                    dve.tensor_reduce(negmax[:, h % 4, 1:2], s_ps[h % 2][:, T:2 * T], AX.X, ALU.max,
                                      negate=True).then_inc(max_ready, 1)

            def probs_t_out(layer, pos, h):
                dve.wait_ge(pt_psum, 16 * pos + h + 1)
                wait(dve, o_psum, 8 * pos + h // 2 - 1)
                if layer == 0:
                    dve.tensor_copy(probs_t[:, h % 4, :, :], t_ps[:, :].rearrange(
                        "p (c q) -> p c q", c=NT)).then_inc(pt_even, 1)
                else:
                    dve.tensor_copy(probs_t[:, h % 4, 0, :], t_ps[:, 0:T])
                    dve.tensor_copy(probs_t[:, h % 4, 1, P:T], t_ps[:, T + P:2 * T])\
                        .then_inc(pt_even, 1)

            def last_phase(at):
                return isinstance(at[1], int) and at[1] == B - 1

            def carry(b):
                dve.tensor_tensor(x_f[:, :, :], x_c[:, :, :], bo_all[:, :].rearrange(
                    "p (o d) -> p o d", o=1).to_broadcast([P, NT, D]), ALU.add).then_inc(carry_done, 1)

            def residual(at):
                layer, b, pos, _ = at
                dve.wait_ge(out_done, 8 * (pos + 1))
                o = out_ps[:, 0:NT * D].rearrange("p (t d) -> p t d", t=NT)
                if layer == 0:
                    dve.tensor_tensor(x_a[:, :, :], o, source(at)[:, :, :], ALU.add).then_inc(resid_done, 1)
                else:
                    dve.wait_ge(carry_done, b + 1)
                    dve.tensor_tensor(x_f[:, :, :], o, x_f[:, :, :], ALU.add).then_inc(resid_done, 1)
                dve.wait_ge(resid_done, pos + 1)

            def bridge(nxt):
                input_stats(nxt)
                input_apply(nxt)
                input_lo(nxt)
                values_out(nxt, 0)
                values_out(nxt, 2)
                pair_lo(nxt[0], nxt[2], 0)

            def beside_dve(s, place, prep, chain_of, end_of, ffn_of):
                for steps, at, b in ((chain, CHAIN_END_DVE_AT, end_of), (chain, CHAIN_DVE_AT, chain_of),
                                     (ffn, FFN_DVE_AT, ffn_of)):
                    for k, part in at.get((s, place), ()) if b is not None else ():
                        steps(b, k, part)
                if prep and place == "end":
                    for k in PREP_AT.get(s, ()):
                        prepare(0, k)

            def phase(cur, prev, nxt, prep=False, chain_of=None, end_of=None, ffn_of=None):
                sides = (prep, chain_of, end_of, ffn_of)
                for s in range(H if cur else 4):
                    if s == 4 and prev:
                        residual(prev)
                    if cur:
                        maxima(cur[0], cur[2], s)
                    if nxt and s == 7:
                        input_lo(nxt)
                    if nxt and s in (9, 13):
                        values_out(nxt, 0 if s == 9 else 2)
                    if s % 2 == 0 and cur and s // 2 + 1 < PAIRS:
                        pair_lo(cur[0], cur[2], s // 2 + 1)
                    if s == 14 and nxt:
                        pair_lo(nxt[0], nxt[2], 0)
                    if s == 6 and nxt:
                        input_apply(nxt)
                    beside_dve(s, "mid", *sides)
                    if cur:
                        inverse(cur[2], s)
                    at, h = (cur, s - 2) if s >= 2 else (prev, H + s - 2)
                    if at and h % 2 == 0:
                        probs_t_out(at[0], at[2], h)
                    if s == 1 and cur and cur[0] == 1 and not last_phase(cur):
                        carry(cur[1])
                    if s == 4 and cur[0] == 1 and not isinstance(cur[1], int):
                        dve.wait_ge(stored, 16 * cur[1])
                    if nxt and s == 5:
                        input_stats(nxt)
                    beside_dve(s, "end", *sides)
                if not cur:
                    carry(prev[1])
                    residual(prev)

            chain_link = [None]

            def chain(b, k, part=None):
                if part is None:
                    for part in range(CHAIN_PARTS.get(k, 1)):
                        chain(b, k, part)
                    return
                if k == "stats0":
                    chain_link[0] = Steps(dve, chain_step, CHAIN_STEPS * b)
                else:
                    chain_link[0].base = CHAIN_STEPS * b
                if isinstance(k, str):
                    n = int(k[-1])
                    if k.startswith("stats"):
                        norm_stats(dve, LN_CHAIN, 3 * b + n, (x_a, x_c, x_c)[n])
                    else:
                        norm_apply(dve, LN_CHAIN, 3 * b + n, (x_a, x_c, x_c)[n], cn).then_inc(chain_in, 1)
                    return
                link = chain_link[0]

                def here():
                    dve.wait_ge(chain_psum, 14 * b + k + 1)

                if k in (2, 5):
                    t = (k - 2) // 3
                    here()
                    dve.tensor_reduce(cneg[:, t:t + 1], m_ps[:, :], AX.X, ALU.max, negate=True)\
                        .then_inc(chain_in, 1)
                elif k in (4, 7):
                    t = (k - 4) // 3
                    here()
                    if t == 0:
                        wait(dve, carry_done, b)
                    link(dve.reciprocal(cinv[:, t:t + 1], csum[:, t:t + 1]))
                    dve.scalar_tensor_tensor(out=x_c[:, t, :], in0=m_ps[:, 0:D], scalar=cinv[:, t:t + 1],
                                             in1=x_a[:, t, :], op0=ALU.mult, op1=ALU.add)\
                        .then_inc(chain_dve, 1)
                    if k == 7:
                        dve.wait_ge(chain_dve, 7 * b + 2)
                elif k == 8:
                    here()
                    link(dve.tensor_copy(cn_t[:, :], m_ps[:, 0:T]))
                    dve.tensor_reduce(emb[:, :], cn_t[:, :].rearrange("p (t q) -> p t q", t=NT), AX.X,
                                      ALU.add).then_inc(chain_dve, 1)
                elif k == 9:
                    proj, size, bits, weak, cands, signed = (hsh[:, j, :, :] for j in range(6))
                    weighed, only = (hsh[:, j, :, :] for j in (6, 7))
                    code, least, flip, change = (hsv[:, j, :] for j in range(4))

                    def spread(v):
                        return v.rearrange("p (t o) -> p t o", o=1).to_broadcast([1, NT, BITS])

                    if part == 0:
                        here()
                        dve.tensor_scalar(proj, m_ps[0:1, 0:NT * BITS].rearrange("p (t j) -> p t j", t=NT),
                                          1.0 / P, None, ALU.mult).then_inc(chain_dve, 1)
                        dve.wait_ge(chain_dve, 7 * b + 4)
                        link(dve.tensor_scalar(bits, proj, 0.0, None, ALU.is_gt), wait=False)
                        link(dve.scalar_tensor_tensor(out=size, in0=proj, scalar=-1.0, in1=proj, op0=ALU.mult,
                                                      op1=ALU.max))
                    elif part == 1:
                        link(dve.tensor_scalar(signed, bits, -2.0, 1.0, ALU.mult, ALU.add), wait=False)
                        link(dve.tensor_tensor(weighed, bits, powers[:, :, :], ALU.mult), wait=False)
                        link(dve.tensor_reduce(least, size, AX.X, ALU.min))
                        link(dve.tensor_tensor(signed, signed, powers[:, :, :], ALU.mult), wait=False)
                        link(dve.tensor_reduce(code, weighed, AX.X, ALU.add), wait=False)
                        link(dve.tensor_tensor(weak, size, spread(least), ALU.is_equal))
                    elif part == 2:
                        link(dve.tensor_copy(chosen[:, 0, :], code), wait=False)
                        link(dve.scalar_tensor_tensor(out=cands, in0=weak, scalar=-float(E),
                                                      in1=powers_up[:, :, :], op0=ALU.mult, op1=ALU.add))
                        link(dve.tensor_reduce(flip, cands, AX.X, ALU.min))
                        link(dve.tensor_tensor(only, cands, spread(flip), ALU.is_equal))
                    elif part == 3:
                        link(dve.tensor_tensor(only, only, signed, ALU.mult))
                        link(dve.tensor_reduce(change, only, AX.X, ALU.add))
                    else:
                        link(dve.tensor_tensor(chosen[:, 1, :], change, code, ALU.add))
                        dve.tensor_copy(index[:, :, :], chosen[:, :, :]).then_inc(chain_in, 1)
                elif k == 10:
                    here()
                    dve.scalar_tensor_tensor(out=x_c[:, :, :], in0=m_ps[:, 0:NT * D].rearrange(
                        "p (t d) -> p t d", t=NT), scalar=0.5, in1=x_c[:, :, :], op0=ALU.mult, op1=ALU.add)\
                        .then_inc(chain_dve, 1)
                    dve.wait_ge(chain_dve, 7 * b + 5)
                elif k == 12:
                    if part == 0:
                        dve.wait_ge(chain_act, 9 * b + 9)
                        link(dve.tensor_scalar(cand[:, :], th[:, :], 0.5, 0.0, ALU.mult, ALU.min), wait=False)
                        link(dve.tensor_scalar(pos_part[:, :], m_ps[:, T:2 * T], bzh[:, 1:2], 0.0, ALU.add,
                                               ALU.max), wait=False)
                        link(dve.tensor_scalar(keep[:, :], tz[:, :], -0.5, 0.5, ALU.mult, ALU.add))
                    elif part == 1:
                        link(dve.scalar_tensor_tensor(out=cand[:, :], in0=cand[:, :], scalar=0.5,
                                                      in1=pos_part[:, :], op0=ALU.add, op1=ALU.add))
                    else:
                        link(dve.scalar_tensor_tensor(out=cand[:, :], in0=tz[:, :], scalar=1.0,
                                                      in1=cand[:, :], op0=ALU.add, op1=ALU.mult))
                        dve.tensor_tensor_scan(hid[:, :], keep[:, :], cand[:, :], 1.0, ALU.mult, ALU.add)\
                            .then_inc(chain_dve, 1)
                elif k == 13:
                    here()
                    dve.scalar_tensor_tensor(out=x_c[:, :, :], in0=m_ps[:, 0:NT * D].rearrange(
                        "p (t d) -> p t d", t=NT), scalar=0.5, in1=x_c[:, :, :], op0=ALU.mult, op1=ALU.add)\
                        .then_inc(chain_dve, 1)
                    dve.wait_ge(chain_dve, 7 * (b + 1))
                    link.end(CHAIN_STEPS)

            ffn_link = [None]

            def ffn(b, k, part=None):
                if part is None:
                    for part in range(FFN_PARTS.get(k, 1)):
                        ffn(b, k, part)
                    return
                if k == "stats":
                    norm_stats(dve, LN_FFN, b, x_f)
                    return
                if k == "apply" and part == 0:
                    ffn_link[0] = Steps(dve, ffn_step, FFN_STEPS * b)
                link = ffn_link[0]
                if k == "apply":
                    if part == 0:
                        link(norm_apply(dve, LN_FFN, b, x_f, fn))
                        link(dve.tensor_reduce(fmax[:, :], fn[:, :, :], AX.X, ALU.max,
                                               apply_absolute_value=True))
                    elif part == 1:
                        link(dve.tensor_scalar(fmax[:, :], fmax[:, :], 1e-5, None, ALU.max))
                        link(dve.reciprocal(fscale[:, :], fmax[:, :]))
                        link(dve.tensor_scalar(fscale[:, :], fscale[:, :], 127.0, None, ALU.mult))
                    elif part == 2:
                        link(dve.reciprocal(finv[:, :], fscale[:, :]), wait=False)
                        for t in range(NT):
                            link(dve.tensor_scalar(fn[:, t, :], fn[:, t, :], fscale[:, t:t + 1], ROUND,
                                                   ALU.mult, ALU.add), wait=t == NT - 1)
                    else:
                        for t in range(NT):
                            ins = dve.tensor_scalar(fn[:, t, :], fn[:, t, :], ROUND, finv[:, t:t + 1],
                                                    ALU.subtract, ALU.mult)
                        ins.then_inc(ffn_in, 1)
                elif k == 0:
                    dve.wait_ge(ffn_act, 4 * b + 1)
                    dve.tensor_tensor(f_lo[:, 1:T + 1], m_ps[:, 0:T], f32(f_hi[:, 1:T + 1]), ALU.subtract)\
                        .then_inc(ffn_dve, 1)
                elif k in (1, 2):
                    t = k - 1
                    if part == 0:
                        dve.wait_ge(ffn_act, 4 * b + k + 1)
                        dve.wait_ge(ffn_in, 3 * b + k)
                        dve.scalar_tensor_tensor(out=fy[:, :], in0=ftanh, scalar=1.0, in1=m_ps[:, :],
                                                 op0=ALU.add, op1=ALU.mult).then_inc(ffn_dve, 1)
                        dve.wait_ge(ffn_dve, 3 * b + k + 1)
                        link(dve.tensor_reduce(gmax[:, t:t + 1], fy[:, :], AX.X, ALU.max,
                                               apply_absolute_value=True))
                    elif part == 1:
                        link(dve.tensor_scalar(gmax[:, t:t + 1], gmax[:, t:t + 1], 0.5, 1e-5, ALU.mult,
                                               ALU.max))
                        link(dve.reciprocal(gscale[:, t:t + 1], gmax[:, t:t + 1]))
                        link(dve.tensor_scalar(gscale[:, t:t + 1], gscale[:, t:t + 1], 127.0, 0.5, ALU.mult,
                                               ALU.mult))
                    else:
                        link(dve.tensor_scalar(fy[:, :], fy[:, :], gscale[:, t:t + 1], ROUND, ALU.mult,
                                               ALU.add))
                        dve.tensor_scalar(fq[:, t, :], fy[:, :], ROUND, None, ALU.subtract)\
                            .then_inc(ffn_in, 1)
                elif k == 4 and part == 0:
                    link(dve.reciprocal(ginv[:, :], gscale[:, :]))
                    link(dve.tensor_scalar(ginv[:, :], ginv[:, :], 0.5, winv[:, 1:2], ALU.mult, ALU.mult))
                elif k == 4:
                    dve.wait_ge(ffn_psum, 5 * (b + 1))
                    if isinstance(b, int):
                        wait(dve, stored, 16 * b)
                    for t in range(NT):
                        last = dve.scalar_tensor_tensor(
                            out=y_out[:, t, :], in0=m_ps[:, D * t:D * t + D], scalar=ginv[:, t:t + 1],
                            in1=x_f[:, t, :], op0=ALU.mult, op1=ALU.add)
                    last.then_inc(y_ready, 1)
                    dve.wait_ge(y_ready, b + 1)
                    dve.memset(beat[:, 0:1], 0.0).then_inc(m_free, 1)
                    link.end(FFN_STEPS)

            prep_link = Steps(dve, prep_step, 0)

            def prepare(b, k):
                link = prep_link
                if k == 0:
                    dve.wait_ge(load_small, 16 * 14)
                    for j in range(2):
                        link(dve.tensor_reduce(wsum[:, j:j + 1], w12[:, j, :], AX.X, ALU.add,
                                               apply_absolute_value=True))
                    dve.memset(beat[:, 0:1], 0.0).then_inc(prep_in, 1)
                    dve.wait_ge(prep_psum, 1)
                    dve.tensor_copy(wzh_t[:, :, :], m_ps[:, 0:2 * P].rearrange("p (j h) -> p j h", j=2))\
                        .then_inc(prep_read, 1)
                elif k == 1:
                    dve.wait_ge(prep_psum, 2)
                    dve.tensor_scalar(wmean[:, :], m_ps[:, 0:2], 1.0 / (HID * D), 1e-5, ALU.mult, ALU.max)\
                        .then_inc(prep_read, 1)
                    dve.wait_ge(prep_read, 2)
                    link(dve.reciprocal(wscale[:, :], wmean[:, :]))
                    link(dve.reciprocal(winv[:, :], wscale[:, :]))
                    for j in range(2):
                        w = w12[:, j, :]
                        link(dve.tensor_scalar(w, w, wscale[:, j:j + 1], ROUND, ALU.mult, ALU.add))
                        link(dve.tensor_scalar(w, w, ROUND, 1.0, ALU.subtract, ALU.min))
                    link(dve.tensor_scalar(w12[:, 0, :], w12[:, 0, :], -1.0, winv[:, 0:1], ALU.max, ALU.mult))
                    link(dve.tensor_scalar(tern2, w12[:, 1, :], -1.0, None, ALU.max))
                    filters(0)
                elif k <= 4:
                    dve.wait_ge(prep_hi, k - 1)
                    dve.tensor_tensor(w1_lo[:, k - 2, :], m_ps[:, :], f32(w1_hi[:, k - 2, :]), ALU.subtract)\
                        .then_inc(prep_read, 1)
                    split_weights(1, k - 2)
                    if k < 4:
                        filters(k - 1)
                    else:
                        dve.memset(beat[:, 0:1], 0.0).then_inc(prep_in, 1)
                elif k == 5:
                    dve.wait_ge(prep_psum, 6)
                    dve.tensor_copy(w2t[:, :, :], m_bf[:, 0:HID].rearrange("p (c m) -> p c m", c=NH))\
                        .then_inc(prep_read, 1)
                    link(dve.tensor_copy(convb_r[0:1, :], convb[0:1, :]))
                    link(dve.tensor_copy(convb_r[32:33, :], convb[32:33, :]))
                    link(dve.tensor_tensor(convb_r[32:33, :], convb[32:33, :], f32(convb_r[32:33, :]),
                                           ALU.subtract))
                else:
                    dve.tensor_scalar(bq_scaled[:, :], bqkv[:, 0, :], SCALE1, None, ALU.mult)\
                        .then_inc(prep_read, 1)
                    dve.tensor_scalar(bzh_half[:, :], bzh[:, :], 0.5, None, ALU.mult).then_inc(prep_read, 1)
                    dve.wait_ge(prep_read, 8)
                    dve.memset(beat[:, 0:1], 0.0).then_inc(m_free, 1)

            def filters(j):
                for c in range(NH):
                    dve.tensor_scalar(filt[:, j, c, :], w12[:, 0, P * c:P * c + P], convw[:, c, j:j + 1],
                                      None, ALU.mult).then_inc(prep_step, 1)
                    prep_link.n += 1
                dve.wait_ge(prep_step, prep_link.n)
                dve.memset(beat[:, 0:1], 0.0).then_inc(prep_in, 1)

            dve.wait_ge(consts_ready, 29)
            for j in range(3):
                split_weights(0, j)
            program(dve, phase, chain, ffn, prepare, bridge)


_INS = ['x', 'ctx_1024', 'L0_attn_kernel', 'L0_attn_WO', 'L0_ffn_expert_weights', 'L0_ffn_hyperplanes',
        'L1_attn_Wz', 'L1_attn_bz', 'L1_attn_Wh', 'L1_attn_bh', 'L1_xattn_Wq', 'L1_xattn_bq', 'L1_xattn_Wk',
        'L1_xattn_bk', 'L1_xattn_Wv', 'L1_xattn_bv', 'L1_xattn_Wo', 'L1_xattn_bo', 'L1_ffn_w1',
        'L1_ffn_conv_w', 'L1_ffn_conv_b', 'L1_ffn_w2']
_OUTS = [((8, 256, 128), 'float32')]


def kernel(**inputs):
    import numpy as _np
    import concourse.bacc as _bacc
    from concourse import mybir as _mybir
    from concourse.bass_utils import run_bass_kernel_spmd as _run

    nc = _bacc.Bacc("TRN2", target_bir_lowering=False, num_devices=1)
    arrays, args = {}, []
    for name in _INS:
        a = _np.ascontiguousarray(inputs[name])
        arrays[f"in_{name}_dram"] = a
        args.append(nc.dram_tensor(f"in_{name}_dram", a.shape, _mybir.dt.from_np(a.dtype), kind="ExternalInput").ap())
    for i, (shape, dtype) in enumerate(_OUTS):
        dt = _mybir.dt.from_np(_np.dtype(dtype))
        args.append(nc.dram_tensor(f"out_{i}_dram", shape, dt, kind="ExternalOutput").ap())
    build(nc, *args)
    r = _run(nc, [arrays], core_ids=[0])
    return r.results[0]["out_0_dram"]
```

```python
from contextlib import ExitStack

import concourse.bass as bass
from concourse import mybir

P = 128
B, T, D = 8, 256, 128
NT = T // P
CTX = 512
NC = CTX // P
H, DH = 16, 64
HD = H * DH
PAIRS = H // 2
E = 64
BITS = 6
HID = 512
NH = HID // P
SCALE0 = 1.0 / (DH * DH * H)
SCALE1 = 1.0 / 8.0
EPS = 1e-5
ROUND = 12582912.0
MASKED = -1e36

CHAIN_AT = {
    4: (0,), 5: ("stats0",), 6: (1,), 7: (2,), 8: (3,), 9: (4,), 10: (5,), 11: (6,), 12: (7, "stats1"),
    13: (8,), 14: (9,)}
CHAIN_END_AT = {
    1: (10, "stats2"), 2: (11,), 3: (12,), 5: (13,)}
FFN_AT = {
    6: ("stats",), 9: (0,), 10: (1,), 12: (2,), 14: (3,), 15: (4,)}
PREP_AT = {4: (0,), 5: (1,), 7: (2,), 9: (3,), 11: (4,), 13: (5,), 14: (6,)}
FFN_ALL = ("stats", "apply", 0, 1, 2, 3, 4)
CHAIN_PARTS = {"weak": 2, "pick": 2, 12: 3}
CHAIN_DVE_AT = {
    (5, "end"): (("stats0", 0),), (6, "mid"): (("apply0", 0),), (7, "end"): ((2, 0),), (9, "end"): ((4, 0),),
    (10, "end"): ((5, 0),), (12, "end"): ((7, 0), ("stats1", 0)), (13, "mid"): (("apply1", 0),),
    (14, "end"): ((9, 0), ("weak", 0)), (15, "mid"): (("weak", 1),)}
CHAIN_END_DVE_AT = {
    (0, "mid"): (("pick", 0),), (0, "end"): (("pick", 1),), (1, "end"): ((10, 0), ("stats2", 0)),
    (2, "mid"): (("apply2", 0),), (3, "end"): ((12, 0),), (4, "mid"): ((12, 1), (12, 2)),
    (5, "end"): ((13, 0),)}
FFN_PARTS = {"apply": 4, 1: 3, 2: 3, 4: 2}
FFN_DVE_AT = {
    (6, "mid"): (("stats", 0),), (7, "mid"): (("apply", 0), ("apply", 1)),
    (8, "end"): (("apply", 2), ("apply", 3)), (9, "end"): ((0, 0),), (11, "mid"): ((1, 0),),
    (11, "end"): ((1, 1), (1, 2)), (12, "end"): ((2, 0),), (13, "end"): ((2, 1), (2, 2)),
    (14, "mid"): ((4, 0),), (15, "end"): ((4, 1),)}
TAIL = 1 + max(5, *CHAIN_END_AT, *(s for s, _ in CHAIN_END_DVE_AT))
INPUT_AT = ({"stats": 5, "apply": 6, "transpose": 8, "values": (9, 11, 14, 15)},
            {"stats": 2, "apply": 3, "transpose": 4, "values": (5, 6, 9, 11)})
DVE_HEADS = ((0, 2, 4, 6, 8, 10, 12, 13, 14), (0, 4, 6, 8, 10, 12, 14))
DVE_VALUES = ((0,), (0, 2))

F32 = mybir.dt.float32
F32R = mybir.dt.float32r
BF16 = mybir.dt.bfloat16
I32 = mybir.dt.int32
ALU = mybir.AluOpType
ACT = mybir.ActivationFunctionType
AX = mybir.AxisListType

LN_STEPS = 3
CHAIN_STEPS = 19
FFN_STEPS = 20


def build(nc, x, ctx_d, w0, wo0, experts, planes, wz, bz, wh, bh, wq1, bq1, wk1, bk1, wv1, bv1,
          wo1, bo1, w1, conv_w, conv_b, w2, out):
    with ExitStack() as st:
        def sb(name, shape, dt=F32):
            return st.enter_context(nc.sbuf_tensor(name, shape, dt))

        def pb(name):
            return st.enter_context(nc.psum_tensor(name, [P, 512], F32))

        def sem(name):
            return st.enter_context(nc.semaphore(name))

        ident = sb("ident", [P, P])
        identb = sb("identb", [P, P], BF16)
        mask = sb("mask", [P, P], BF16)
        ones = sb("ones", [P, P])
        onesr = sb("onesr", [P, P], F32R)
        powers = sb("powers", [1, NT, BITS])
        powers_down = sb("powers_down", [1, NT, BITS])
        stage = sb("stage", [P, 3, HD])
        whi = [sb(f"whi{l}", [P, 3, HD], F32R) for l in range(2)]
        wlo = [sb(f"wlo{l}", [P, 3, HD], F32R) for l in range(2)]
        wo = [sb(f"wo{l}", [P, PAIRS, D]) for l in range(2)]
        expert = sb("expert", [P, E * D])
        plane = sb("plane", [P, BITS])
        wzh = sb("wzh", [P, 2, D])
        wzh_t = sb("wzh_t", [P, 2, D])
        bzh = sb("bzh", [P, 2])
        bzh_half = sb("bzh_half", [P, 2])
        bqkv = sb("bqkv", [P, 3, PAIRS])
        bq_scaled = sb("bq_scaled", [P, PAIRS])
        bo_all = sb("bo_all", [P, D])
        w12 = sb("w12", [P, 2, HID])
        convw = sb("convw", [P, NH, 3])
        convb_r = sb("convb_r", [P, HID], F32R)
        w1_hi = sb("w1_hi", [P, 3, HID], F32R)
        w1_lo = sb("w1_lo", [P, 3, HID], F32R)
        w2t = sb("w2t", [P, NH, D], BF16)
        wsum = sb("wsum", [P, 2])
        wmean = sb("wmean", [P, 2])
        wscale = sb("wscale", [P, 2])
        winv = sb("winv", [P, 2])
        x_in = sb("x_in", [P, NT, D])
        x_a = sb("x_a", [P, NT, D])
        x_c = sb("x_c", [P, NT, D])
        x_f = sb("x_f", [P, NT, D])
        y_out = sb("y_out", [P, NT, D])
        stats = sb("stats", [P, 3, NT, 6])
        mv = sb("mv", [P, 3, NT, 2])
        rstd = sb("rstd", [P, 3, NT])
        eps_pow = sb("eps_pow", [P, 2, NT])
        beat = sb("beat", [P, 1])
        xn = sb("xn", [P, NT, D])
        xt_hi = [sb(f"xt_hi{j}", [P, T], F32R) for j in range(2)]
        xt_lo = [sb(f"xt_lo{j}", [P, T], F32R) for j in range(2)]
        ct_hi = sb("ct_hi", [P, T], F32R)
        ct_lo = sb("ct_lo", [P, T], F32R)
        q_hi = sb("q_hi", [P, 2, T], F32R)
        q_lo = sb("q_lo", [P, 2, T], F32R)
        k_hi = sb("k_hi", [P, 2, 2, T], F32R)
        k_lo = sb("k_lo", [P, 2, 2, T], F32R)
        v_sb = [sb(f"v_sb{j}", [P, NT, HD]) for j in range(2)]
        probs = sb("probs", [P, 4, NT, T])
        negmax = sb("negmax", [P, 4, NT])
        rsum = sb("rsum", [P, 4, NT])
        rinv = sb("rinv", [P, 4, NT])
        probs_t = sb("probs_t", [P, 4, NT, T])
        heads_t = sb("heads_t", [P, 2, T])
        ctx = sb("ctx", [P, NC, D])
        ctx_t = sb("ctx_t", [P, CTX])
        cn = sb("cn", [P, NT, D])
        cn_t = sb("cn_t", [P, T])
        cprobs = sb("cprobs", [P, CTX])
        cprobs_t = sb("cprobs_t", [P, NC, P])
        cneg = sb("cneg", [P, NT])
        csum = sb("csum", [P, NT])
        cinv = sb("cinv", [P, NT])
        emb = sb("emb", [P, NT])
        hsh = sb("hsh", [1, 6, NT, BITS])
        hsv = sb("hsv", [1, 4, NT])
        index = sb("index", [1, 2, NT], I32)
        tz = sb("tz", [P, T])
        th = sb("th", [P, T])
        keep = sb("keep", [P, T])
        cand = sb("cand", [P, T])
        pos_part = sb("pos_part", [P, T])
        hid = sb("hid", [P, T])
        fn = sb("fn", [P, NT, D])
        fmax = sb("fmax", [P, NT])
        fscale = sb("fscale", [P, NT])
        finv = sb("finv", [P, NT])
        f_hi = sb("f_hi", [P, T + 2], F32R)
        f_lo = sb("f_lo", [P, T + 2], F32R)
        ftanh = stage[:, 0, :].rearrange("p (t n) -> p t n", t=NT)
        fy = sb("fy", [P, HID])
        convb = fy
        gmax = sb("gmax", [P, NT])
        gscale = sb("gscale", [P, NT])
        ginv = sb("ginv", [P, NT])
        fq = sb("fq", [P, NT, HID], BF16)
        fq_t = stage[:, 1, 0:HID].bitcast(BF16).rearrange("p (c q) -> p c q", q=P)
        filt = expert[:, 0:3 * HID].rearrange("p (j c d) -> p j c d", j=3, c=NH)
        tern2 = fq[:, 0, :]

        s_ps = [pb("s_ps0"), pb("s_ps1")]
        t_ps = pb("t_ps")
        qk_ps = pb("qk_ps")
        v_ps = pb("v_ps")
        o_ps = pb("o_ps")
        out_ps = pb("out_ps")
        m_ps = pb("m_ps")
        m_bf = m_ps[:, :].bitcast(BF16)

        load_x = sem("load_x")
        x_kept = sem("x_kept")
        load_ctx = sem("load_ctx")
        load_w0 = [sem(f"load_w0_{j}") for j in range(3)]
        load_wo0 = sem("load_wo0")
        load_w1 = sem("load_w1")
        load_wo1 = sem("load_wo1")
        load_experts = sem("load_experts")
        load_small = sem("load_small")
        consts_ready = sem("consts_ready")
        w_hi_ready = sem("w_hi_ready")
        w_lo_ready = sem("w_lo_ready")
        prep_step = sem("prep_step")
        prep_psum = sem("prep_psum")
        prep_hi = sem("prep_hi")
        prep_in = sem("prep_in")
        prep_read = sem("prep_read")
        xn_ready = sem("xn_ready")
        xt_psum = sem("xt_psum")
        xt_hi_ready = sem("xt_hi_ready")
        xt_ready = sem("xt_ready")
        v_psum = sem("v_psum")
        v_even = sem("v_even")
        v_odd = sem("v_odd")
        qk_psum = sem("qk_psum")
        qk_hi = sem("qk_hi")
        qk_ready = sem("qk_ready")
        scores_ready = sem("scores_ready")
        max_ready = sem("max_ready")
        exp_done = sem("exp_done")
        rinv_ready = sem("rinv_ready")
        probs_ready = sem("probs_ready")
        pt_psum = sem("pt_psum")
        pt_even = sem("pt_even")
        pt_odd = sem("pt_odd")
        o_psum = sem("o_psum")
        o_ready = sem("o_ready")
        out_done = sem("out_done")
        resid_done = sem("resid_done")
        carry_done = sem("carry_done")
        ln_step = [sem(f"ln_step{j}") for j in range(3)]
        ln_stats = [sem(f"ln_stats{j}") for j in range(3)]
        ln_pool = [sem(f"ln_pool{j}") for j in range(3)]
        chain_step = sem("chain_step")
        ffn_step = sem("ffn_step")
        chain_psum = sem("chain_psum")
        chain_act = sem("chain_act")
        chain_dve = sem("chain_dve")
        chain_in = sem("chain_in")
        ctx_split = sem("ctx_split")
        ffn_in = sem("ffn_in")
        ffn_psum = sem("ffn_psum")
        ffn_act = sem("ffn_act")
        ffn_dve = sem("ffn_dve")
        m_free = sem("m_free")
        y_ready = sem("y_ready")
        stored = sem("stored")

        def wait(eng, s, value):
            if not isinstance(value, int) or value > 0:
                eng.wait_ge(s, value)

        def f32(ap):
            return ap.bitcast(F32)

        def rows(h):
            return slice(DH * (h % 2), DH * (h % 2) + DH)

        LN_PHASE, LN_CHAIN, LN_FFN = range(3)

        def source(at):
            return x_c if at[0] == 1 else x_in

        def norm_stats(dve, j, n, src):
            link = Steps(dve, ln_step[j], LN_STEPS * n)
            for t in range(NT):
                link(dve.bn_stats(stats[:, j, t, :], src[:, t, :]), wait=t == NT - 1)
            dve.memset(beat[:, 0:1], 0.0)
            link(dve.bn_aggr(mv[:, j, 0, :], stats[:, j, 0, :]), wait=False)
            dve.bn_aggr(mv[:, j, 1, :], stats[:, j, 1, :]).then_inc(ln_stats[j], 1)
            link.end(LN_STEPS)

        def norm_scale(pool, j, n):
            pool.wait_ge(ln_stats[j], n + 1)
            pool.tensor_tensor(rstd[:, j, :], mv[:, j, :, 1], eps_pow[:, 0, :], ALU.add)\
                .then_inc(ln_pool[j], 1)
            pool.wait_ge(ln_pool[j], 2 * n + 1)
            pool.tensor_tensor(rstd[:, j, :], rstd[:, j, :], eps_pow[:, 1, :], ALU.pow)\
                .then_inc(ln_pool[j], 1)

        def norm_apply(dve, j, n, src, dst):
            dve.wait_ge(ln_pool[j], 2 * n + 2)
            for t in range(NT):
                ins = dve.tensor_scalar(dst[:, t, :], src[:, t, :], mv[:, j, t, 0:1], rstd[:, j, t:t + 1],
                                        ALU.subtract, ALU.mult)
            return ins

        def hidden_ps(b, k):
            return s_ps[0] if k == 2 and isinstance(b, int) and b == B - 1 else m_ps

        class Steps:

            def __init__(self, eng, s, base):
                self.eng, self.s, self.base, self.n = eng, s, base, 0

            def __call__(self, ins, wait=True):
                self.n += 1
                ins.then_inc(self.s, 1)
                if wait:
                    self.eng.wait_ge(self.s, self.base + self.n)

            def end(self, total):
                assert self.n == total, (self.n, total)

        def phase_a(b):
            return (0, b, 0, 0) if isinstance(b, int) and b == 0 else (0, b, 2 * b - 1, 1)

        def phase_b(b):
            return (1, b, 2 * B - 1, 1) if isinstance(b, int) and b == B - 1 else (1, b, 2 * b + 2, 0)

        def program(eng, phase, chain, ffn, prepare, bridge):
            bridge(phase_a(0))
            phase(phase_a(0), None, phase_a(1), fresh=True, prep=True)
            phase(phase_a(1), phase_a(0), None, chain_of=0)
            phase(None, phase_a(1), None, end_of=0)
            bridge(phase_b(0))
            phase(phase_b(0), None, phase_a(2), fresh=True, chain_of=1)
            with eng.Fori(2, B - 1) as i:
                phase(phase_a(i), phase_b(i - 2), phase_b(i - 1), end_of=i - 1, ffn_of=i - 2)
                phase(phase_b(i - 1), phase_a(i), phase_a(i + 1), chain_of=i)
            phase(phase_a(B - 1), phase_b(B - 3), phase_b(B - 2), end_of=B - 2, ffn_of=B - 3)
            phase(phase_b(B - 2), phase_a(B - 1), None, chain_of=B - 1)
            phase(None, phase_b(B - 2), None, end_of=B - 1)
            bridge(phase_b(B - 1))
            phase(phase_b(B - 1), None, None, fresh=True, ffn_of=B - 2)
            phase(None, phase_b(B - 1), None)
            for k in FFN_ALL:
                ffn(B - 1, k)

        def beside(s, chain, ffn, prepare, prep, chain_of, end_of, ffn_of):
            for steps, at, b in ((prepare, PREP_AT, 0 if prep else None), (chain, CHAIN_END_AT, end_of),
                                 (chain, CHAIN_AT, chain_of), (ffn, FFN_AT, ffn_of)):
                for k in at.get(s, ()) if b is not None else ():
                    steps(b, k)

        def load_projection(eng, j):
            eng.dma_start(stage[:, j, :].rearrange("p (h d) -> p h d", h=H),
                          w0[j, :, :, :].rearrange("h m d -> m h d")).then_inc(load_w0[j], 16)

        block = st.enter_context(nc.Block())

        @block.sync
        def _(sp):
            def load_batch_x(b):
                sp.dma_start(x_in[:, :, :], x[b, :, :].rearrange("(t p) d -> p t d", p=P))\
                    .then_inc(load_x, 16)

            def load_batch_ctx(b):
                sp.dma_start(ctx[:, :, :], ctx_d[b, :, :].rearrange("(t p) d -> p t d", p=P))\
                    .then_inc(load_ctx, 16)

            def store(b):
                sp.wait_ge(y_ready, b + 1)
                sp.dma_start(out[b, :, :].rearrange("(t p) d -> p t d", p=P), y_out[:, :, :])\
                    .then_inc(stored, 16)

            load_batch_x(0)
            for j in (0, 2):
                load_projection(sp, j)
            for dst, src in (
                    (w12[:, 0, :].rearrange("p (c d) -> p c d", c=NH), w1.rearrange("(c p) d -> p c d", p=P)),
                    (w12[:, 1, :], w2),
                    (plane[:, :], planes),
                    (wzh[:, 0, :], wz),
                    (wzh[:, 1, :], wh),
                    (bzh[:, 0:1], bz.rearrange("(p o) -> p o", o=1)),
                    (bzh[:, 1:2], bh.rearrange("(p o) -> p o", o=1)),
                    (bqkv[:, 0, :], bq1.rearrange("(c p) -> p c", p=P)),
                    (bqkv[:, 1, :], bk1.rearrange("(c p) -> p c", p=P)),
                    (bqkv[:, 2, :], bv1.rearrange("(c p) -> p c", p=P)),
                    (bo_all[:, :], bo1.rearrange("(o m) -> o m", o=1).to_broadcast([P, D])),
                    (convw[:, :, :], conv_w.rearrange("(c p) o j -> p c (o j)", p=P)),
                    (convb[0:1, :], conv_b.rearrange("(o m) -> o m", o=1)),
                    (convb[32:33, :], conv_b.rearrange("(o m) -> o m", o=1))):
                sp.dma_start(dst, src, allow_slow_non_contiguous=True).then_inc(load_small, 16)

            load_batch_ctx(0)
            sp.dma_start(wo[1][:, :, :], wo1.rearrange("(c p) m -> p c m", p=P)).then_inc(load_wo1, 16)
            sp.wait_ge(w_lo_ready, 3)
            for j, w in enumerate((wq1, wk1, wv1)):
                sp.dma_start(stage[:, j, :], w).then_inc(load_w1, 16)
            sp.wait_ge(x_kept, 1)
            load_batch_x(1)
            sp.wait_ge(prep_read, 5)
            sp.dma_start(expert[:, :].rearrange("p (e n) -> p e n", e=E),
                         experts.rearrange("e d n -> d e n")).then_inc(load_experts, 16)
            sp.wait_ge(x_kept, 2)
            load_batch_x(2)
            sp.wait_ge(chain_dve, 2)
            load_batch_ctx(1)
            sp.wait_ge(chain_dve, 8)
            load_batch_ctx(2)
            with sp.Fori(2, B - 1) as i:
                sp.wait_ge(x_kept, i + 1)
                load_batch_x(i + 1)
                store(i - 2)
                sp.wait_ge(chain_dve, 6 * i + 2)
                load_batch_ctx(i + 1)
            for b in range(B - 3, B):
                store(b)
            sp.wait_ge(stored, 16 * B)

        @block.gpsimd
        def _(pool):
            pool.memset(ident[:, :], 0.0).then_inc(consts_ready, 1)
            pool.memset(mask[:, :], 0.0).then_inc(consts_ready, 1)
            pool.memset(identb[:, :], 0.0).then_inc(consts_ready, 1)
            pool.wait_ge(consts_ready, 3)
            pool.affine_select(out=ident[:, :], in_=ident[:, :], compare_op=ALU.not_equal, fill=1.0,
                               base=0, pattern=[[-1, P]], channel_multiplier=1).then_inc(consts_ready, 1)
            pool.affine_select(out=identb[:, :], in_=identb[:, :], compare_op=ALU.not_equal, fill=1.0,
                               base=0, pattern=[[-1, P]], channel_multiplier=1).then_inc(consts_ready, 1)
            pool.affine_select(out=mask[:, :], in_=mask[:, :], compare_op=ALU.is_ge, fill=MASKED,
                               base=0, pattern=[[-1, P]], channel_multiplier=1).then_inc(consts_ready, 1)
            for k in (k_hi, k_lo):
                pool.memset(f32(k[:, :, :, :]), 0.0).then_inc(consts_ready, 1)
            pool.memset(ones[:, :], 1.0).then_inc(consts_ready, 1)
            pool.memset(f32(onesr[:, :]), 1.0).then_inc(consts_ready, 1)
            pool.memset(f32(convb_r[:, :]), 0.0).then_inc(consts_ready, 1)
            for f in (f_hi, f_lo):
                pool.memset(f32(f[:, 0:1]), 0.0).then_inc(consts_ready, 1)
                pool.memset(f32(f[:, T + 1:T + 2]), 0.0).then_inc(consts_ready, 1)
            for j in range(BITS):
                pool.memset(powers[:, :, j], float(2 ** j)).then_inc(consts_ready, 1)
                pool.memset(powers_down[:, :, j], float(2 ** j - E)).then_inc(consts_ready, 1)

            for t in range(2):
                pool.memset(eps_pow[:, t, :], (EPS, -0.5)[t]).then_inc(consts_ready, 1)
            pool.wait_ge(consts_ready, 29)

            def normalise(layer, pos, h):
                b4 = h % 4
                pool.wait_ge(rinv_ready, 16 * pos + h + 1)
                if layer == 0:
                    last = pool.tensor_tensor(
                        probs[:, b4, :, :], probs[:, b4, :, :],
                        rinv[:, b4, :].rearrange("p (t o) -> p t o", o=1).to_broadcast([P, NT, T]),
                        ALU.mult)
                else:
                    for t in range(NT):
                        n = P * (t + 1)
                        last = pool.tensor_tensor(
                            probs[:, b4, t, 0:n], probs[:, b4, t, 0:n],
                            rinv[:, b4, t:t + 1].to_broadcast([P, n]), ALU.mult)
                last.then_inc(probs_ready, 1)

            def split_context(b, pos):
                pool.wait_ge(chain_act, 10 * b + 1)
                pool.wait_ge(qk_psum, 8 * pos + 8)
                pool.tensor_tensor(ct_hi[:, :], ctx_t[:, 0:T], ones[:, 0:1].to_broadcast([P, T]), ALU.mult)\
                    .then_inc(ctx_split, 1)
                pool.wait_ge(ctx_split, 2 * b + 1)
                pool.tensor_tensor(ct_lo[:, :], ctx_t[:, 0:T], f32(ct_hi[:, :]), ALU.subtract)\
                    .then_inc(ctx_split, 1)

            def chain(b, k):
                if str(k).startswith("stats"):
                    norm_scale(pool, LN_CHAIN, 3 * b + int(k[-1]))

            def ffn(b, k):
                if k == "stats":
                    norm_scale(pool, LN_FFN, b)

            def prepare(b, k):
                pass

            def bridge(nxt):
                norm_scale(pool, LN_PHASE, nxt[2])

            def phase(cur, prev, nxt, fresh=False, prep=False, chain_of=None, end_of=None, ffn_of=None):
                at_slot = INPUT_AT[cur[0] if cur else 0]
                for s in range(H if cur else TAIL):
                    at, h = (cur, s - 1) if s >= 1 else (prev, H - 1)
                    if at:
                        normalise(at[0], at[2], h)
                    beside(s, chain, ffn, prepare, prep, chain_of, end_of, ffn_of)
                    if nxt and s == at_slot["stats"]:
                        norm_scale(pool, LN_PHASE, nxt[2])
                    if chain_of is not None and s == 14:
                        split_context(chain_of, cur[2])

            program(pool, phase, chain, ffn, prepare, bridge)

        @block.scalar
        def _(act):
            load_projection(act, 1)
            act.dma_start(wo[0][0:DH, :, :],
                          wo0[0, :, :].rearrange("(d c h) m -> h d c m", c=PAIRS, h=2)[0, :, :, :])\
                .then_inc(load_wo0, 16)
            act.dma_start(wo[0][DH:P, :, :],
                          wo0[0, :, :].rearrange("(d c h) m -> h d c m", c=PAIRS, h=2)[1, :, :, :])\
                .then_inc(load_wo0, 16)
            def split_weights(layer, j):
                if layer == 0:
                    act.wait_ge(load_w0[j], 16)
                else:
                    act.wait_ge(load_w1, 48)
                act.activation(whi[layer][:, j, :], stage[:, j, :], ACT.Copy,
                               scale=(SCALE0, SCALE1)[layer] if j == 0 else 1.0).then_inc(w_hi_ready, 1)

            def pair_hi(layer, pos, p):
                act.wait_ge(qk_psum, 8 * pos + p + 1)
                wait(act, scores_ready, 16 * pos + 2 * (p - 1))
                wait(act, qk_ready, 8 * pos + p - 1)
                j = p % 2
                if layer == 0:
                    act.activation(q_hi[:, j, :], qk_ps[:, 0:T], ACT.Copy)
                else:
                    act.activation(q_hi[:, j, :], qk_ps[:, 0:T], ACT.Identity, bias=bq_scaled[:, p:p + 1])
                for h in range(2):
                    if layer == 0:
                        last = act.activation(k_hi[rows(h), j, h, :], qk_ps[rows(h), T:2 * T], ACT.Copy)
                    else:
                        last = act.activation(k_hi[rows(h), j, h, :], qk_ps[rows(h), T:2 * T],
                                              ACT.Identity, bias=bqkv[rows(h), 1, p:p + 1])
                last.then_inc(qk_hi, 1)

            def keep_input(b):
                act.wait_ge(load_x, 16 * (b + 1))
                wait(act, chain_dve, 6 * (b - 1) + 2)
                act.activation(x_a[:, :, :], x_in[:, :, :], ACT.Copy).then_inc(x_kept, 1)

            def input_hi(nxt):
                _, _, pos, j = nxt
                act.wait_ge(xt_psum, pos + 1)
                act.activation(xt_hi[j][:, :], v_ps[:, 0:T], ACT.Copy).then_inc(xt_hi_ready, 1)

            def values_out(nxt, g):
                _, _, pos, j = nxt
                act.wait_ge(v_psum, 4 * pos + g + 1)
                c = 512 * (g % 2)
                act.activation(v_sb[j][:, g // 2, c:c + 512], v_ps[:, :], ACT.Copy)\
                    .then_inc((v_even, v_odd)[g % 2], 1)

            def exponentials(layer, pos, h):
                act.wait_ge(max_ready, 16 * pos + h + 1)
                wait(act, pt_psum, 16 * pos + h - 3)
                for t in range(NT):
                    n = T if layer == 0 else P * (t + 1)
                    last = act.activation(probs[:, h % 4, t, 0:n], s_ps[h % 2][:, t * T:t * T + n],
                                          ACT.Exp, bias=negmax[:, h % 4, t:t + 1],
                                          accum_out=rsum[:, h % 4, t:t + 1])
                last.then_inc(exp_done, 1)

            def probs_t_out(layer, pos, h):
                act.wait_ge(pt_psum, 16 * pos + h + 1)
                wait(act, o_psum, 8 * pos + h // 2 - 1)
                if layer == 0:
                    act.activation(probs_t[:, h % 4, :, :], t_ps[:, :].rearrange(
                        "p (c q) -> p c q", c=NT), ACT.Copy).then_inc((pt_even, pt_odd)[h % 2], 1)
                else:
                    act.activation(probs_t[:, h % 4, 0, :], t_ps[:, 0:T], ACT.Copy)
                    act.activation(probs_t[:, h % 4, 1, P:T], t_ps[:, T + P:2 * T], ACT.Copy)\
                        .then_inc((pt_even, pt_odd)[h % 2], 1)

            def heads_out(layer, pos, p):
                act.wait_ge(o_psum, 8 * pos + p + 1)
                wait(act, out_done, 8 * pos + p - 1)
                if layer == 0:
                    act.activation(heads_t[:, p % 2, :], o_ps[:, 0:T], ACT.Copy).then_inc(o_ready, 1)
                else:
                    act.activation(heads_t[:, p % 2, :], o_ps[:, 0:T], ACT.Identity,
                                   bias=bqkv[:, 2, p:p + 1]).then_inc(o_ready, 1)

            def bridge(nxt):
                input_hi(nxt)
                for j in range(3 if nxt[2] == 0 else 0):
                    split_weights(0, j)
                pair_hi(nxt[0], nxt[2], 0)

            def phase(cur, prev, nxt, fresh=False, prep=False, chain_of=None, end_of=None, ffn_of=None):
                at_slot = INPUT_AT[cur[0] if cur else 0]
                for s in range(H if cur else TAIL):
                    if s % 2 == 0 and cur and s // 2 + 1 < PAIRS:
                        pair_hi(cur[0], cur[2], s // 2 + 1)
                    if s == 14 and nxt:
                        pair_hi(nxt[0], nxt[2], 0)
                    if cur:
                        exponentials(cur[0], cur[2], s)
                    if fresh and s in (1, 3):
                        values_out(cur, s)
                    if nxt and s == at_slot["transpose"]:
                        input_hi(nxt)
                    if nxt and s in at_slot["values"] and at_slot["values"].index(s) not in DVE_VALUES[nxt[0]]:
                        values_out(nxt, at_slot["values"].index(s))
                    if cur and cur[0] == 0 and s == (15 if isinstance(cur[1], int) and cur[1] == 1 else 1):
                        keep_input(cur[1])
                    at, h = (cur, s - 3) if s >= 3 else (prev, H + s - 3)
                    if at and h not in DVE_HEADS[at[0]]:
                        probs_t_out(at[0], at[2], h)
                    at, p = (cur, (s - 5) // 2) if s >= 5 else (prev, PAIRS + (s - 5) // 2)
                    if at and s % 2 == 1:
                        heads_out(at[0], at[2], p)
                    beside(s, chain, ffn, prepare, prep, chain_of, end_of, ffn_of)

            def chain(b, k):
                def here():
                    act.wait_ge(chain_psum, 14 * b + k + 1)

                if k == 0:
                    here()
                    wait(act, ctx_split, 2 * b)
                    act.activation(ctx_t[:, :], m_ps[:, :], ACT.Copy).then_inc(chain_act, 1)
                elif k in (1, 11):
                    here()
                    act.activation(cn_t[:, :], m_ps[:, 0:T], ACT.Copy).then_inc(chain_act, 1)
                elif k == 8:
                    here()
                    for t in range(NT):
                        last = act.activation(cn_t[:, P * t:P * t + P], m_ps[:, P * t:P * t + P], ACT.Copy,
                                              accum_out=emb[:, t:t + 1])
                    last.then_inc(chain_act, 1)
                elif k in (2, 5):
                    t = (k - 2) // 3
                    act.wait_ge(chain_in, 6 * b + 2 + t)
                    act.activation(cprobs[:, :], m_ps[:, :], ACT.Exp, bias=cneg[:, t:t + 1],
                                   accum_out=csum[:, t:t + 1]).then_inc(chain_act, 1)
                elif k in (3, 6):
                    here()
                    act.activation(cprobs_t[:, :, :], m_ps[:, :].rearrange("p (c q) -> p c q", c=NC),
                                   ACT.Copy).then_inc(chain_act, 1)
                elif k == 12:
                    here()
                    act.activation(tz[:, :], m_ps[:, 0:T], ACT.Tanh, bias=bzh_half[:, 0:1], scale=0.5)\
                        .then_inc(chain_act, 1)
                    act.activation(th[:, :], m_ps[:, T:2 * T], ACT.Tanh, bias=bzh_half[:, 1:2], scale=0.5)\
                        .then_inc(chain_act, 1)

            def ffn(b, k):
                if k not in (0, 1, 2, 3):
                    return
                act.wait_ge(ffn_psum, 5 * b + k + 1)
                if k == 0:
                    act.activation(f_hi[:, 1:T + 1], m_ps[:, 0:T], ACT.Copy).then_inc(ffn_act, 1)
                elif k in (1, 2):
                    act.activation(ftanh[:, k - 1, :], hidden_ps(b, k)[:, :], ACT.Tanh, scale=0.5).then_inc(ffn_act, 1)
                elif k == 3:
                    act.activation(fq_t, m_bf.rearrange("p (c q) -> p c q", q=P), ACT.Copy)\
                        .then_inc(ffn_act, 1)

            def prepare(b, k):
                if 2 <= k <= 4:
                    act.wait_ge(prep_psum, 1 + k)
                    act.activation(w1_hi[:, k - 2, :], m_ps[:, :], ACT.Copy).then_inc(prep_hi, 1)
                    split_weights(1, k - 2)
                if k == 6:
                    act.wait_ge(prep_read, 8)

            program(act, phase, chain, ffn, prepare, bridge)

        @block.tensor
        def _(pe):
            def product3(dst, l_hi, l_lo, r_hi, r_lo, start=True, stop=True):
                pe.matmul(dst, l_hi, r_hi, start=start, stop=False)
                pe.matmul(dst, l_hi, r_lo, start=False, stop=False)
                return pe.matmul(dst, l_lo, r_hi, start=False, stop=stop)

            def project_pair(at, p):
                layer, _, pos, j = at
                cols = slice(P * p, P * p + P)
                c_hi, c_lo = (xt_hi[j], xt_lo[j]) if layer == 0 else (ct_hi, ct_lo)
                product3(qk_ps[:, 0:T], whi[layer][:, 0, cols], wlo[layer][:, 0, cols],
                         xt_hi[j][:, :], xt_lo[j][:, :])
                product3(qk_ps[:, T:2 * T], whi[layer][:, 1, cols], wlo[layer][:, 1, cols],
                         c_hi[:, :], c_lo[:, :]).then_inc(qk_psum, 1)

            def transpose_input(nxt):
                pe.wait_ge(xn_ready, nxt[2] + 1)
                for t in range(NT):
                    last = pe.transpose(v_ps[:, P * t:P * t + P], xn[:, t, :], ident[:, :])
                last.then_inc(xt_psum, 1)

            def project_values(nxt, g):
                layer, _, _, j = nxt
                c_hi, c_lo = (xt_hi[j], xt_lo[j]) if layer == 0 else (ct_hi, ct_lo)
                tile, cols = slice(P * (g // 2), P * (g // 2) + P), slice(512 * (g % 2), 512 * (g % 2) + 512)
                product3(v_ps[:, :], c_hi[:, tile], c_lo[:, tile], whi[layer][:, 2, cols],
                         wlo[layer][:, 2, cols]).then_inc(v_psum, 1)

            def scores(layer, pos, h):
                j = (h // 2) % 2
                pe.wait_ge(qk_ready, 8 * pos + h // 2 + 1)
                wait(pe, exp_done, 16 * pos + h - 1)
                for t in range(NT):
                    q = slice(P * t, P * t + P)
                    dst = s_ps[h % 2][:, T * t:T * t + T]
                    last = product3(dst, q_hi[:, j, q], q_lo[:, j, q], k_hi[:, j, h % 2, :],
                                    k_lo[:, j, h % 2, :], stop=layer == 0)
                    if layer == 1:
                        last = pe.matmul(s_ps[h % 2][:, T * t + P * t:T * t + P * t + P], identb[:, :],
                                         mask[:, :], start=False, stop=True)
                last.then_inc(scores_ready, 1)

            def transposes(layer, pos, h):
                pe.wait_ge(probs_ready, 16 * pos + h + 1)
                wait(pe, (pt_odd, pt_even)[h % 2], 8 * pos + (h + 1) // 2)
                for c in range(NT):
                    for t in range(NT):
                        if layer == 1 and t < c:
                            continue
                        last = pe.transpose(t_ps[:, T * c + P * t:T * c + P * t + P],
                                            probs[:, h % 4, t, P * c:P * c + P], ident[:, :])
                last.then_inc(pt_psum, 1)

            def values(layer, pos, j, p):
                if p == 0:
                    pe.wait_ge(v_odd, 2 * pos + 2)
                    pe.wait_ge(v_even, 2 * pos + 2)
                pe.wait_ge(pt_even, 8 * pos + p + 1)
                pe.wait_ge(pt_odd, 8 * pos + p + 1)
                wait(pe, o_ready, 8 * pos + p)
                for c in range(NT):
                    q0 = P * c if layer == 1 else 0
                    for h in (2 * p, 2 * p + 1):
                        last = pe.matmul(o_ps[rows(h), q0:T], v_sb[j][:, c, DH * h:DH * h + DH],
                                         probs_t[:, h % 4, c, q0:T], start=(c == 0), stop=(c == NT - 1),
                                         skip_group_check=True)
                last.then_inc(o_psum, 1)

            def output(layer, pos, p):
                pe.wait_ge(o_ready, 8 * pos + p + 1)
                if p == 0:
                    wait(pe, resid_done, pos)
                    if isinstance(pos, int) and pos == 0:
                        pe.wait_ge(load_wo0, 32)
                for t in range(NT):
                    last = pe.matmul(out_ps[:, D * t:D * t + D], heads_t[:, p % 2, P * t:P * t + P],
                                     wo[layer][:, p, :], start=(p == 0 and t == 0),
                                     stop=(p == PAIRS - 1 and t == NT - 1), skip_group_check=True)
                last.then_inc(out_done, 1)

            def bridge(nxt):
                _, b, pos, _ = nxt
                if pos == 0:
                    pe.wait_ge(consts_ready, 29)
                transpose_input(nxt)
                pe.wait_ge(xt_ready, pos + 1)
                if nxt[0] == 1:
                    pe.wait_ge(ctx_split, 2 * (b + 1))
                pe.wait_ge(w_lo_ready, 3 * nxt[0] + 2)
                wait(pe, qk_ready, 8 * pos)
                project_pair(nxt, 0)

            def phase(cur, prev, nxt, fresh=False, prep=False, chain_of=None, end_of=None, ffn_of=None):
                at_slot = INPUT_AT[cur[0] if cur else 0]
                for s in range(H if cur else TAIL):
                    if s % 2 == 0 and cur and s // 2 + 1 < PAIRS:
                        p, pos = s // 2 + 1, cur[2]
                        pe.wait_ge(qk_ready, 8 * pos + p)
                        project_pair(cur, p)
                    if s == 14 and nxt:
                        pe.wait_ge(qk_ready, 8 * nxt[2])
                        project_pair(nxt, 0)
                    if cur:
                        scores(cur[0], cur[2], s)
                    if fresh and s < 4:
                        if s == 0:
                            pe.wait_ge(w_lo_ready, 3 * cur[0] + 3)
                        else:
                            pe.wait_ge((v_even, v_odd)[(s - 1) % 2], 2 * cur[2] + (s + 1) // 2)
                        project_values(cur, s)
                    if nxt and s == at_slot["transpose"]:
                        if fresh:
                            pe.wait_ge(v_odd, 2 * cur[2] + 2)
                        transpose_input(nxt)
                    if nxt and s in at_slot["values"]:
                        g = at_slot["values"].index(s)
                        if g == 0:
                            pe.wait_ge(xt_ready, nxt[2] + 1)
                        else:
                            pe.wait_ge((v_even, v_odd)[(g - 1) % 2], 2 * nxt[2] + (g + 1) // 2)
                        if nxt[0] == 1 and g == 0:
                            pe.wait_ge(ctx_split, 2 * (nxt[1] + 1))
                        project_values(nxt, g)
                    at, h = (cur, s - 3) if s >= 3 else (prev, H + s - 3)
                    if at:
                        transposes(at[0], at[2], h)
                    if s % 2 == 1:
                        at, p = (cur, (s - 5) // 2) if s >= 5 else (prev, PAIRS + (s - 5) // 2)
                        if at:
                            values(at[0], at[2], at[3], p)
                    else:
                        at, p = (cur, (s - 6) // 2) if s >= 6 else (prev, PAIRS + (s - 6) // 2)
                        if at and p < PAIRS:
                            output(at[0], at[2], p)
                    beside(s, chain, ffn, prepare, prep, chain_of, end_of, ffn_of)

            def chain(b, k):
                if not isinstance(k, int):
                    return
                if k == 0:
                    pe.wait_ge(m_free, max(1, b) if isinstance(b, int) else b)
                    pe.wait_ge(load_ctx, 16 * (b + 1))
                    for c in range(NC):
                        last = pe.transpose(m_ps[:, P * c:P * c + P], ctx[:, c, :], ident[:, :])
                elif k in (1, 8, 11):
                    pe.wait_ge(chain_in, 6 * b + {1: 1, 8: 4, 11: 6}[k])
                    if k == 1:
                        pe.wait_ge(chain_act, 10 * b + 1)
                    for t in range(NT):
                        last = pe.transpose(m_ps[:, P * t:P * t + P], cn[:, t, :], ident[:, :])
                elif k in (2, 5):
                    t = (k - 2) // 3
                    if k == 2:
                        pe.wait_ge(chain_act, 10 * b + 2)
                    else:
                        pe.wait_ge(chain_dve, 6 * b + 1)
                    last = pe.matmul(m_ps[:, :], cn_t[:, P * t:P * t + P], ctx_t[:, :], start=True, stop=True)
                elif k in (3, 6):
                    pe.wait_ge(chain_act, 10 * b + k - (k == 6))
                    for c in range(NC):
                        last = pe.transpose(m_ps[:, P * c:P * c + P], cprobs[:, P * c:P * c + P], ident[:, :])
                elif k in (4, 7):
                    pe.wait_ge(chain_act, 10 * b + k - (k == 7))
                    for c in range(NC):
                        last = pe.matmul(m_ps[:, 0:D], cprobs_t[:, c, :], ctx[:, c, :], start=(c == 0),
                                         stop=(c == NC - 1))
                elif k == 9:
                    pe.wait_ge(chain_act, 10 * b + 7)
                    for t in range(NT):
                        last = pe.matmul(m_ps[0:1, BITS * t:BITS * t + BITS], emb[:, t:t + 1], plane[:, :],
                                         start=(t == 0), stop=(t == NT - 1), skip_group_check=True)
                elif k == 10:
                    pe.wait_ge(chain_in, 6 * b + 5)
                    pe.matmul(m_ps[:, 0:1], identb[:, :], identb[:, 0:1], start=True, stop=True)
                    if isinstance(b, int) and b == 0:
                        pe.wait_ge(load_experts, 16)
                    _, picked = nc.values_load_multi_w_load_instructions(
                        index[0:1, :, :].rearrange("o e t -> o (e t)"), engines=(mybir.EngineType.PE,),
                        min_val=0, max_val=E - 1)
                    for t in range(NT):
                        for e in range(2):
                            last = pe.matmul(m_ps[:, D * t:D * t + D], cn_t[:, P * t:P * t + P],
                                             expert[:, bass.ds(picked[NT * e + t] * D, D)], start=(t == 0 and e == 0),
                                             stop=(t == NT - 1 and e == 1), skip_group_check=True)
                elif k == 12:
                    pe.wait_ge(chain_act, 10 * b + 8)
                    for j in range(2):
                        last = pe.matmul(m_ps[:, T * j:T * j + T], wzh_t[:, j, :], cn_t[:, :],
                                         start=True, stop=True)
                elif k == 13:
                    pe.wait_ge(chain_dve, 6 * b + 5)
                    for t in range(NT):
                        last = pe.transpose(m_ps[:, P * t:P * t + P], hid[:, P * t:P * t + P], ident[:, :])
                last.then_inc(chain_psum, 1)

            def ffn(b, k):
                if not isinstance(k, int):
                    return
                if k == 0:
                    pe.wait_ge(ffn_in, 3 * b + 1)
                    for t in range(NT):
                        last = pe.transpose(m_ps[:, P * t:P * t + P], fn[:, t, :], ident[:, :])
                elif k in (1, 2):
                    t = k - 1
                    acc = hidden_ps(b, k)
                    pe.wait_ge(ffn_dve, 3 * b + (k if acc is m_ps else 1))
                    pe.matmul(acc[:, :], onesr[:, :], convb_r[:, :], start=True, stop=False)
                    for j in range(3):
                        q = slice(P * t + j, P * t + j + P)
                        last = product3(acc[:, :], f_hi[:, q], f_lo[:, q], w1_hi[:, j, :], w1_lo[:, j, :],
                                        start=False, stop=(j == 2))
                elif k == 3:
                    pe.wait_ge(ffn_in, 3 * b + 3)
                    for t in range(NT):
                        for c in range(NH):
                            n = NH * t + c
                            last = pe.transpose(m_bf[:, P * n:P * n + P], fq[:, t, P * c:P * c + P],
                                                identb[:, :])
                elif k == 4:
                    pe.wait_ge(ffn_act, 4 * b + 4)
                    for t in range(NT):
                        for c in range(NH):
                            last = pe.matmul(m_ps[:, D * t:D * t + D], fq_t[:, NH * t + c, :], w2t[:, c, :],
                                             start=(t == 0 and c == 0), stop=(t == NT - 1 and c == NH - 1),
                                             skip_group_check=True)
                last.then_inc(ffn_psum, 1)

            def prepare(b, k):
                if k == 0:
                    pe.wait_ge(load_small, 16 * 14)
                    for j in range(2):
                        last = pe.transpose(m_ps[:, P * j:P * j + P], wzh[:, j, :], ident[:, :])
                    last.then_inc(prep_psum, 1)
                elif k == 1:
                    pe.wait_ge(prep_in, 1)
                    pe.wait_ge(prep_read, 1)
                    pe.matmul(m_ps[:, 0:2], ones[:, :], wsum[:, :], start=True, stop=True)\
                        .then_inc(prep_psum, 1)
                elif k <= 4:
                    pe.wait_ge(prep_in, k)
                    pe.wait_ge(prep_read, k)
                    for c in range(NH):
                        last = pe.transpose(m_ps[:, P * c:P * c + P], filt[:, k - 2, c, :], ident[:, :])
                    last.then_inc(prep_psum, 1)
                elif k == 5:
                    pe.wait_ge(prep_in, 5)
                    pe.wait_ge(prep_read, 5)
                    for c in range(NH):
                        last = pe.transpose(m_bf[:, P * c:P * c + P], tern2[:, P * c:P * c + P], identb[:, :])
                    last.then_inc(prep_psum, 1)
                elif k == 6:
                    pe.wait_ge(load_wo1, 16)

            program(pe, phase, chain, ffn, prepare, bridge)

        @block.vector
        def _(dve):
            def split_weights(layer, j):
                dve.wait_ge(w_hi_ready, 3 * layer + j + 1)
                dve.scalar_tensor_tensor(
                    out=wlo[layer][:, j, :], in0=stage[:, j, :],
                    scalar=(SCALE0, SCALE1)[layer] if j == 0 else 1.0,
                    in1=f32(whi[layer][:, j, :]), op0=ALU.mult, op1=ALU.subtract).then_inc(w_lo_ready, 1)

            def pair_lo(layer, pos, p):
                dve.wait_ge(qk_hi, 8 * pos + p + 1)
                j = p % 2
                if layer == 0:
                    dve.tensor_tensor(q_lo[:, j, :], qk_ps[:, 0:T], f32(q_hi[:, j, :]), ALU.subtract)
                else:
                    dve.scalar_tensor_tensor(out=q_lo[:, j, :], in0=qk_ps[:, 0:T], scalar=bq_scaled[:, p:p + 1],
                                             in1=f32(q_hi[:, j, :]), op0=ALU.add, op1=ALU.subtract)
                for h in range(2):
                    r = rows(h)
                    if layer == 0:
                        last = dve.tensor_tensor(k_lo[r, j, h, :], qk_ps[r, T:2 * T], f32(k_hi[r, j, h, :]),
                                                 ALU.subtract)
                    else:
                        last = dve.scalar_tensor_tensor(
                            out=k_lo[r, j, h, :], in0=qk_ps[r, T:2 * T], scalar=bqkv[r, 1, p:p + 1],
                            in1=f32(k_hi[r, j, h, :]), op0=ALU.add, op1=ALU.subtract)
                last.then_inc(qk_ready, 1)

            def inverse(pos, h):
                dve.wait_ge(exp_done, 16 * pos + h + 1)
                wait(dve, probs_ready, 16 * pos + h - 3)
                dve.reciprocal(rinv[:, h % 4, :], rsum[:, h % 4, :]).then_inc(rinv_ready, 1)

            def input_stats(nxt):
                layer, b, pos, _ = nxt
                if layer == 0:
                    dve.wait_ge(load_x, 16 * (b + 1))
                norm_stats(dve, LN_PHASE, pos, source(nxt))

            def input_apply(nxt):
                wait(dve, xt_psum, nxt[2])
                norm_apply(dve, LN_PHASE, nxt[2], source(nxt), xn).then_inc(xn_ready, 1)

            def input_lo(nxt):
                _, _, pos, j = nxt
                dve.wait_ge(xt_hi_ready, pos + 1)
                dve.tensor_tensor(xt_lo[j][:, :], v_ps[:, 0:T], f32(xt_hi[j][:, :]), ALU.subtract)\
                    .then_inc(xt_ready, 1)

            def values_out(nxt, g):
                _, _, pos, j = nxt
                dve.wait_ge(v_psum, 4 * pos + g + 1)
                c = 512 * (g % 2)
                dve.tensor_copy(v_sb[j][:, g // 2, c:c + 512], v_ps[:, :])\
                    .then_inc((v_even, v_odd)[g % 2], 1)

            def maxima(layer, pos, h):
                dve.wait_ge(scores_ready, 16 * pos + h + 1)
                wait(dve, exp_done, 16 * pos + h - 3)
                if layer == 0:
                    dve.tensor_reduce(negmax[:, h % 4, :], s_ps[h % 2][:, :].rearrange(
                        "p (t k) -> p t k", t=NT), AX.X, ALU.max, negate=True).then_inc(max_ready, 1)
                else:
                    dve.tensor_reduce(negmax[:, h % 4, 0:1], s_ps[h % 2][:, 0:P], AX.X, ALU.max,
                                      negate=True)
                    dve.tensor_reduce(negmax[:, h % 4, 1:2], s_ps[h % 2][:, T:2 * T], AX.X, ALU.max,
                                      negate=True).then_inc(max_ready, 1)

            def probs_t_out(layer, pos, h):
                dve.wait_ge(pt_psum, 16 * pos + h + 1)
                wait(dve, o_psum, 8 * pos + h // 2 - 1)
                if layer == 0:
                    dve.tensor_copy(probs_t[:, h % 4, :, :], t_ps[:, :].rearrange(
                        "p (c q) -> p c q", c=NT)).then_inc((pt_even, pt_odd)[h % 2], 1)
                else:
                    dve.tensor_copy(probs_t[:, h % 4, 0, :], t_ps[:, 0:T])
                    dve.tensor_copy(probs_t[:, h % 4, 1, P:T], t_ps[:, T + P:2 * T])\
                        .then_inc((pt_even, pt_odd)[h % 2], 1)

            def last_phase(at):
                return at[0] == 1 and isinstance(at[1], int) and at[1] == B - 1

            def carry(b):
                dve.tensor_tensor(x_f[:, :, :], x_c[:, :, :], bo_all[:, :].rearrange(
                    "p (o d) -> p o d", o=1).to_broadcast([P, NT, D]), ALU.add).then_inc(carry_done, 1)

            def residual(at):
                layer, b, pos, _ = at
                dve.wait_ge(out_done, 8 * (pos + 1))
                o = out_ps[:, 0:NT * D].rearrange("p (t d) -> p t d", t=NT)
                if layer == 0:
                    dve.wait_ge(x_kept, b + 1)
                    dve.tensor_tensor(x_a[:, :, :], o, x_a[:, :, :], ALU.add).then_inc(resid_done, 1)
                else:
                    dve.wait_ge(carry_done, b + 1)
                    dve.tensor_tensor(x_f[:, :, :], o, x_f[:, :, :], ALU.add).then_inc(resid_done, 1)
                dve.wait_ge(resid_done, pos + 1)

            def bridge(nxt):
                input_stats(nxt)
                input_apply(nxt)
                input_lo(nxt)
                for j in range(3 if nxt[2] == 0 else 0):
                    split_weights(0, j)
                pair_lo(nxt[0], nxt[2], 0)

            def beside_dve(s, place, prep, chain_of, end_of, ffn_of):
                for steps, at, b in ((chain, CHAIN_END_DVE_AT, end_of), (chain, CHAIN_DVE_AT, chain_of),
                                     (ffn, FFN_DVE_AT, ffn_of)):
                    for k, part in at.get((s, place), ()) if b is not None else ():
                        steps(b, k, part)
                if prep and place == "end":
                    for k in PREP_AT.get(s, ()):
                        prepare(0, k)

            def phase(cur, prev, nxt, fresh=False, prep=False, chain_of=None, end_of=None, ffn_of=None):
                sides = (prep, chain_of, end_of, ffn_of)
                at_slot = INPUT_AT[cur[0] if cur else 0]
                for s in range(H if cur else TAIL):
                    if s == 5 and prev:
                        if last_phase(prev):
                            carry(prev[1])
                        residual(prev)
                    at, h = (cur, s - 1) if s >= 1 else (prev, H - 1)
                    if at:
                        inverse(at[2], h)
                    if cur:
                        maxima(cur[0], cur[2], s)
                    if fresh and s in (0, 2):
                        values_out(cur, s)
                    if nxt and s == at_slot["transpose"]:
                        input_lo(nxt)
                    if nxt and s in at_slot["values"] and at_slot["values"].index(s) in DVE_VALUES[nxt[0]]:
                        values_out(nxt, at_slot["values"].index(s))
                    if nxt and s == at_slot["apply"]:
                        input_apply(nxt)
                    beside_dve(s, "mid", *sides)
                    at, h = (cur, s - 3) if s >= 3 else (prev, H + s - 3)
                    if at and h in DVE_HEADS[at[0]]:
                        probs_t_out(at[0], at[2], h)
                    if s % 2 == 0 and cur and s // 2 + 1 < PAIRS:
                        pair_lo(cur[0], cur[2], s // 2 + 1)
                    if s == 14 and nxt:
                        pair_lo(nxt[0], nxt[2], 0)
                    if s == 1 and cur and cur[0] == 1 and not last_phase(cur):
                        carry(cur[1])
                    if s == 4 and cur and cur[0] == 1 and not isinstance(cur[1], int):
                        dve.wait_ge(stored, 16 * cur[1])
                    beside_dve(s, "end", *sides)
                    if nxt and s == at_slot["stats"]:
                        input_stats(nxt)

            chain_link = [None]

            def chain(b, k, part=None):
                if part is None:
                    for part in range(CHAIN_PARTS.get(k, 1)):
                        chain(b, k, part)
                    return
                if k == "stats0":
                    chain_link[0] = Steps(dve, chain_step, CHAIN_STEPS * b)
                else:
                    chain_link[0].base = CHAIN_STEPS * b
                if isinstance(k, str) and k[-1].isdigit():
                    n = int(k[-1])
                    if k.startswith("stats"):
                        norm_stats(dve, LN_CHAIN, 3 * b + n, (x_a, x_c, x_c)[n])
                    else:
                        norm_apply(dve, LN_CHAIN, 3 * b + n, (x_a, x_c, x_c)[n], cn).then_inc(chain_in, 1)
                    return
                link = chain_link[0]

                def here():
                    dve.wait_ge(chain_psum, 14 * b + k + 1)

                if k in (2, 5):
                    t = (k - 2) // 3
                    here()
                    dve.tensor_reduce(cneg[:, t:t + 1], m_ps[:, :], AX.X, ALU.max, negate=True)\
                        .then_inc(chain_in, 1)
                elif k in (4, 7):
                    t = (k - 4) // 3
                    here()
                    if t == 0:
                        wait(dve, carry_done, b)
                    link(dve.reciprocal(cinv[:, t:t + 1], csum[:, t:t + 1]))
                    dve.scalar_tensor_tensor(out=x_c[:, t, :], in0=m_ps[:, 0:D], scalar=cinv[:, t:t + 1],
                                             in1=x_a[:, t, :], op0=ALU.mult, op1=ALU.add)\
                        .then_inc(chain_dve, 1)
                    if k == 7:
                        dve.wait_ge(chain_dve, 6 * b + 2)
                elif k in (9, "weak", "pick"):
                    proj, size, weighed, signed, cands, only = (hsh[:, j, :, :] for j in range(6))
                    code, least, flip, change = (hsv[:, j, :] for j in range(4))
                    if k == 9:
                        here()
                        dve.tensor_scalar(proj, m_ps[0:1, 0:NT * BITS].rearrange("p (t j) -> p t j", t=NT),
                                          1.0 / P, None, ALU.mult).then_inc(chain_dve, 1)
                        dve.wait_ge(chain_dve, 6 * b + 3)
                        link(dve.scalar_tensor_tensor(out=weighed, in0=proj, scalar=0.0, in1=powers[:, :, :],
                                                      op0=ALU.is_gt, op1=ALU.mult), wait=False)
                        link(dve.scalar_tensor_tensor(out=size, in0=proj, scalar=-1.0, in1=proj, op0=ALU.mult,
                                                      op1=ALU.max))
                    elif (k, part) == ("weak", 0):
                        link(dve.scalar_tensor_tensor(out=signed, in0=weighed, scalar=-2.0,
                                                      in1=powers[:, :, :], op0=ALU.mult, op1=ALU.add),
                             wait=False)
                        link(dve.tensor_reduce(code, weighed, AX.X, ALU.add), wait=False)
                        link(dve.tensor_reduce(least, size, AX.X, ALU.min))
                    elif k == "weak":
                        for t in range(NT):
                            link(dve.scalar_tensor_tensor(out=cands[:, t, :], in0=size[:, t, :],
                                                          scalar=least[:, t:t + 1], in1=powers_down[:, t, :],
                                                          op0=ALU.is_equal, op1=ALU.mult), wait=False)
                        link(dve.tensor_copy(index[:, 0, :], code))
                        link(dve.tensor_reduce(flip, cands, AX.X, ALU.min))
                    elif part == 0:
                        for t in range(NT):
                            link(dve.scalar_tensor_tensor(out=only[:, t, :], in0=cands[:, t, :],
                                                          scalar=flip[:, t:t + 1], in1=signed[:, t, :],
                                                          op0=ALU.is_equal, op1=ALU.mult), wait=t == NT - 1)
                        link(dve.tensor_reduce(change, only, AX.X, ALU.add))
                    else:
                        dve.tensor_tensor(index[:, 1, :], change, code, ALU.add).then_inc(chain_in, 1)
                elif k == 10:
                    here()
                    dve.scalar_tensor_tensor(out=x_c[:, :, :], in0=m_ps[:, 0:NT * D].rearrange(
                        "p (t d) -> p t d", t=NT), scalar=0.5, in1=x_c[:, :, :], op0=ALU.mult, op1=ALU.add)\
                        .then_inc(chain_dve, 1)
                    dve.wait_ge(chain_dve, 6 * b + 4)
                elif k == 12:
                    if part == 0:
                        dve.wait_ge(chain_act, 10 * b + 10)
                        link(dve.tensor_scalar(cand[:, :], th[:, :], 0.5, 0.0, ALU.mult, ALU.min), wait=False)
                        link(dve.tensor_scalar(pos_part[:, :], m_ps[:, T:2 * T], bzh[:, 1:2], 0.0, ALU.add,
                                               ALU.max), wait=False)
                        link(dve.tensor_scalar(keep[:, :], tz[:, :], -0.5, 0.5, ALU.mult, ALU.add))
                    elif part == 1:
                        link(dve.scalar_tensor_tensor(out=cand[:, :], in0=cand[:, :], scalar=0.5,
                                                      in1=pos_part[:, :], op0=ALU.add, op1=ALU.add))
                    else:
                        link(dve.scalar_tensor_tensor(out=cand[:, :], in0=tz[:, :], scalar=1.0,
                                                      in1=cand[:, :], op0=ALU.add, op1=ALU.mult))
                        dve.tensor_tensor_scan(hid[:, :], keep[:, :], cand[:, :], 1.0, ALU.mult, ALU.add)\
                            .then_inc(chain_dve, 1)
                elif k == 13:
                    here()
                    dve.scalar_tensor_tensor(out=x_c[:, :, :], in0=m_ps[:, 0:NT * D].rearrange(
                        "p (t d) -> p t d", t=NT), scalar=0.5, in1=x_c[:, :, :], op0=ALU.mult, op1=ALU.add)\
                        .then_inc(chain_dve, 1)
                    dve.wait_ge(chain_dve, 6 * (b + 1))
                    link.end(CHAIN_STEPS)

            ffn_link = [None]

            def ffn(b, k, part=None):
                if part is None:
                    for part in range(FFN_PARTS.get(k, 1)):
                        ffn(b, k, part)
                    return
                if k == "stats":
                    norm_stats(dve, LN_FFN, b, x_f)
                    return
                if k == "apply" and part == 0:
                    ffn_link[0] = Steps(dve, ffn_step, FFN_STEPS * b)
                link = ffn_link[0]
                if k == "apply":
                    if part == 0:
                        link(norm_apply(dve, LN_FFN, b, x_f, fn))
                        link(dve.tensor_reduce(fmax[:, :], fn[:, :, :], AX.X, ALU.max,
                                               apply_absolute_value=True))
                    elif part == 1:
                        link(dve.tensor_scalar(fmax[:, :], fmax[:, :], 1e-5, None, ALU.max))
                        link(dve.reciprocal(fscale[:, :], fmax[:, :]))
                        link(dve.tensor_scalar(fscale[:, :], fscale[:, :], 127.0, None, ALU.mult))
                    elif part == 2:
                        link(dve.reciprocal(finv[:, :], fscale[:, :]), wait=False)
                        for t in range(NT):
                            link(dve.tensor_scalar(fn[:, t, :], fn[:, t, :], fscale[:, t:t + 1], ROUND,
                                                   ALU.mult, ALU.add), wait=t == NT - 1)
                    else:
                        for t in range(NT):
                            ins = dve.tensor_scalar(fn[:, t, :], fn[:, t, :], ROUND, finv[:, t:t + 1],
                                                    ALU.subtract, ALU.mult)
                        ins.then_inc(ffn_in, 1)
                elif k == 0:
                    dve.wait_ge(ffn_act, 4 * b + 1)
                    dve.tensor_tensor(f_lo[:, 1:T + 1], m_ps[:, 0:T], f32(f_hi[:, 1:T + 1]), ALU.subtract)\
                        .then_inc(ffn_dve, 1)
                elif k in (1, 2):
                    t = k - 1
                    if part == 0:
                        dve.wait_ge(ffn_act, 4 * b + k + 1)
                        dve.wait_ge(ffn_in, 3 * b + k)
                        dve.scalar_tensor_tensor(out=fy[:, :], in0=ftanh[:, t, :], scalar=1.0,
                                                 in1=hidden_ps(b, k)[:, :],
                                                 op0=ALU.add, op1=ALU.mult).then_inc(ffn_dve, 1)
                        dve.wait_ge(ffn_dve, 3 * b + k + 1)
                        link(dve.tensor_reduce(gmax[:, t:t + 1], fy[:, :], AX.X, ALU.max,
                                               apply_absolute_value=True))
                    elif part == 1:
                        link(dve.tensor_scalar(gmax[:, t:t + 1], gmax[:, t:t + 1], 0.5, 1e-5, ALU.mult,
                                               ALU.max))
                        link(dve.reciprocal(gscale[:, t:t + 1], gmax[:, t:t + 1]))
                        link(dve.tensor_scalar(gscale[:, t:t + 1], gscale[:, t:t + 1], 127.0, 0.5, ALU.mult,
                                               ALU.mult))
                    else:
                        link(dve.tensor_scalar(fy[:, :], fy[:, :], gscale[:, t:t + 1], ROUND, ALU.mult,
                                               ALU.add))
                        dve.tensor_scalar(fq[:, t, :], fy[:, :], ROUND, None, ALU.subtract)\
                            .then_inc(ffn_in, 1)
                elif k == 4 and part == 0:
                    link(dve.reciprocal(ginv[:, :], gscale[:, :]))
                    link(dve.tensor_scalar(ginv[:, :], ginv[:, :], 0.5, winv[:, 1:2], ALU.mult, ALU.mult))
                elif k == 4:
                    dve.wait_ge(ffn_psum, 5 * (b + 1))
                    if isinstance(b, int):
                        wait(dve, stored, 16 * b)
                    for t in range(NT):
                        last = dve.scalar_tensor_tensor(
                            out=y_out[:, t, :], in0=m_ps[:, D * t:D * t + D], scalar=ginv[:, t:t + 1],
                            in1=x_f[:, t, :], op0=ALU.mult, op1=ALU.add)
                    last.then_inc(y_ready, 1)
                    dve.wait_ge(y_ready, b + 1)
                    dve.memset(beat[:, 0:1], 0.0).then_inc(m_free, 1)
                    link.end(FFN_STEPS)

            prep_link = Steps(dve, prep_step, 0)

            def prepare(b, k):
                link = prep_link
                if k == 0:
                    dve.wait_ge(load_small, 16 * 14)
                    for j in range(2):
                        link(dve.tensor_reduce(wsum[:, j:j + 1], w12[:, j, :], AX.X, ALU.add,
                                               apply_absolute_value=True))
                    dve.memset(beat[:, 0:1], 0.0).then_inc(prep_in, 1)
                    dve.wait_ge(prep_psum, 1)
                    dve.tensor_copy(wzh_t[:, :, :], m_ps[:, 0:2 * P].rearrange("p (j h) -> p j h", j=2))\
                        .then_inc(prep_read, 1)
                elif k == 1:
                    dve.wait_ge(prep_psum, 2)
                    dve.tensor_scalar(wmean[:, :], m_ps[:, 0:2], 1.0 / (HID * D), 1e-5, ALU.mult, ALU.max)\
                        .then_inc(prep_read, 1)
                    dve.wait_ge(prep_read, 2)
                    link(dve.reciprocal(wscale[:, :], wmean[:, :]))
                    link(dve.reciprocal(winv[:, :], wscale[:, :]))
                    for j in range(2):
                        w = w12[:, j, :]
                        link(dve.tensor_scalar(w, w, wscale[:, j:j + 1], ROUND, ALU.mult, ALU.add))
                        link(dve.tensor_scalar(w, w, ROUND, 1.0, ALU.subtract, ALU.min))
                    link(dve.tensor_scalar(w12[:, 0, :], w12[:, 0, :], -1.0, winv[:, 0:1], ALU.max, ALU.mult))
                    link(dve.tensor_scalar(tern2, w12[:, 1, :], -1.0, None, ALU.max))
                    filters(0)
                elif k <= 4:
                    dve.wait_ge(prep_hi, k - 1)
                    dve.tensor_tensor(w1_lo[:, k - 2, :], m_ps[:, :], f32(w1_hi[:, k - 2, :]), ALU.subtract)\
                        .then_inc(prep_read, 1)
                    split_weights(1, k - 2)
                    if k < 4:
                        filters(k - 1)
                    else:
                        dve.memset(beat[:, 0:1], 0.0).then_inc(prep_in, 1)
                elif k == 5:
                    dve.wait_ge(prep_psum, 6)
                    dve.tensor_copy(w2t[:, :, :], m_bf[:, 0:HID].rearrange("p (c m) -> p c m", c=NH))\
                        .then_inc(prep_read, 1)
                    link(dve.tensor_copy(convb_r[0:1, :], convb[0:1, :]))
                    link(dve.tensor_copy(convb_r[32:33, :], convb[32:33, :]))
                    link(dve.tensor_tensor(convb_r[32:33, :], convb[32:33, :], f32(convb_r[32:33, :]),
                                           ALU.subtract))
                else:
                    dve.tensor_scalar(bq_scaled[:, :], bqkv[:, 0, :], SCALE1, None, ALU.mult)\
                        .then_inc(prep_read, 1)
                    dve.tensor_scalar(bzh_half[:, :], bzh[:, :], 0.5, None, ALU.mult).then_inc(prep_read, 1)
                    dve.wait_ge(prep_read, 8)
                    dve.memset(beat[:, 0:1], 0.0).then_inc(m_free, 1)

            def filters(j):
                for c in range(NH):
                    dve.tensor_scalar(filt[:, j, c, :], w12[:, 0, P * c:P * c + P], convw[:, c, j:j + 1],
                                      None, ALU.mult).then_inc(prep_step, 1)
                    prep_link.n += 1
                dve.wait_ge(prep_step, prep_link.n)
                dve.memset(beat[:, 0:1], 0.0).then_inc(prep_in, 1)

            dve.wait_ge(consts_ready, 29)
            program(dve, phase, chain, ffn, prepare, bridge)


_INS = ['x', 'ctx_1024', 'L0_attn_kernel', 'L0_attn_WO', 'L0_ffn_expert_weights', 'L0_ffn_hyperplanes',
        'L1_attn_Wz', 'L1_attn_bz', 'L1_attn_Wh', 'L1_attn_bh', 'L1_xattn_Wq', 'L1_xattn_bq', 'L1_xattn_Wk',
        'L1_xattn_bk', 'L1_xattn_Wv', 'L1_xattn_bv', 'L1_xattn_Wo', 'L1_xattn_bo', 'L1_ffn_w1',
        'L1_ffn_conv_w', 'L1_ffn_conv_b', 'L1_ffn_w2']
_OUTS = [((8, 256, 128), 'float32')]


def kernel(**inputs):
    import numpy as _np
    import concourse.bacc as _bacc
    from concourse import mybir as _mybir
    from concourse.bass_utils import run_bass_kernel_spmd as _run

    nc = _bacc.Bacc("TRN2", target_bir_lowering=False, num_devices=1)
    arrays, args = {}, []
    for name in _INS:
        a = _np.ascontiguousarray(inputs[name])
        arrays[f"in_{name}_dram"] = a
        args.append(nc.dram_tensor(f"in_{name}_dram", a.shape, _mybir.dt.from_np(a.dtype), kind="ExternalInput").ap())
    for i, (shape, dtype) in enumerate(_OUTS):
        dt = _mybir.dt.from_np(_np.dtype(dtype))
        args.append(nc.dram_tensor(f"out_{i}_dram", shape, dt, kind="ExternalOutput").ap())
    build(nc, *args)
    r = _run(nc, [arrays], core_ids=[0])
    return r.results[0]["out_0_dram"]
```
